# Optimizing a Trainium2 kernel written in Bass

```python
import numpy as np
import jax
import jax.numpy as jnp

def _softmax(x, axis=-1):
    return jax.nn.softmax(x, axis=axis)
def _gelu(x):
    return jax.nn.gelu(x, approximate=True)
def _silu(x):
    return jax.nn.silu(x)
def _sigmoid(x):
    return jax.nn.sigmoid(x)
def _layernorm(x, axis=-1, eps=1e-5):
    m = jnp.mean(x, axis=axis, keepdims=True)
    v = jnp.var(x, axis=axis, keepdims=True)
    return (x - m) / jnp.sqrt(v + eps)
def _scatter_add(tgt, idx, src, axis=0):
    return tgt.at[idx].add(src)
def _segment_sum(src, seg, n):
    return jax.ops.segment_sum(src, seg, n)

kernel_name = 'mk_conv_seq_d2_conv_nchw256_321816'

def setup_inputs(seed: int = 0):
    np.random.seed(seed)
    _w = jnp.asarray
    def _rec_inputs():
        import jax
        import jax.numpy as jnp
        _gk = jax.random.key(seed)
        x = -0.0002928 + 1 * jax.random.normal(jax.random.fold_in(_gk, 1), (4, 256, 64, 64), jnp.float32)
        return x
    x = _rec_inputs()
    def _L0_conv_setup():
        import jax, jax.numpy as jnp
        from jax import lax
        import numpy as np
        import math
        B, CH, H, W = (4, 256, 64, 64)
        TOK = 8
        GCN = math.ceil(CH / TOK)
        PAD = TOK * GCN
        DIN = 2 * GCN
        DSTATE = 16
        DTR = math.ceil(GCN / 16)
        GROUPS = 4
        EPS = 1e-05

        def _forward(x, W_in, W_x, W_dt, b_dt, A_logs, Ds, W_out, gn_w, gn_b):
            b, c, h, w = x.shape
            M = b * h * w
            xf = jnp.transpose(x, (0, 2, 3, 1)).reshape(M, TOK, GCN)
            xz = xf @ W_in
            xp, z = (xz[..., :DIN], xz[..., DIN:])
            xs = jnp.concatenate([xp, xp[:, ::-1]], axis=0)
            x_dbl = xs @ W_x
            dts = x_dbl[..., :DTR]
            Bs = x_dbl[..., DTR:DTR + DSTATE]
            Cs = x_dbl[..., DTR + DSTATE:]
            dts = dts @ W_dt + b_dt
            A = -jnp.exp(A_logs)
            delta = jax.nn.softplus(dts + b_dt)

            def step(hst, inp):
                d_t, u_t, B_t, C_t = inp
                dA = jnp.exp(d_t[:, :, None] * A)
                hst = dA * hst + (d_t * u_t)[:, :, None] * B_t[:, None, :]
                y_t = jnp.einsum('bdn,bn->bd', hst, C_t)
                return (hst, y_t)
            h0 = jnp.zeros((2 * M, DIN, DSTATE), dtype=x.dtype)
            scan_in = (jnp.swapaxes(delta, 0, 1), jnp.swapaxes(xs, 0, 1), jnp.swapaxes(Bs, 0, 1), jnp.swapaxes(Cs, 0, 1))
            _, ys = lax.scan(step, h0, scan_in)
            ys = jnp.swapaxes(ys, 0, 1) + xs * Ds
            y1, y2 = (ys[:M], ys[M:])
            y = y1 + y2[:, ::-1]
            y = y * jax.nn.gelu(z, approximate=False)
            y = y @ W_out
            y = y.reshape(b, h, w, PAD).transpose(0, 3, 1, 2)
            yg = y.reshape(b, GROUPS, -1)
            mu = yg.mean(-1, keepdims=True)
            var = yg.var(-1, keepdims=True)
            yg = (yg - mu) * lax.rsqrt(var + EPS)
            y = yg.reshape(b, PAD, h, w) * gn_w[None, :, None, None] + gn_b[None, :, None, None]
            return x + y[:, :c]
        key = jax.random.key(seed)
        ks = jax.random.split(key, 8)
        x = jax.random.normal(ks[0], (B, CH, H, W), dtype=jnp.float32)
        W_in = jax.random.normal(ks[1], (GCN, 2 * DIN), dtype=jnp.float32) * 0.05
        W_x = jax.random.normal(ks[2], (DIN, DTR + 2 * DSTATE), dtype=jnp.float32) * 0.05
        dt_init_std = DTR ** (-0.5)
        W_dt = jax.random.uniform(ks[3], (DTR, DIN), dtype=jnp.float32, minval=-dt_init_std, maxval=dt_init_std)
        dt = jnp.exp(jax.random.uniform(ks[4], (DIN,), dtype=jnp.float32) * (math.log(0.1) - math.log(0.001)) + math.log(0.001))
        dt = jnp.clip(dt, 0.0001)
        b_dt = dt + jnp.log(-jnp.expm1(-dt))
        A_logs = jnp.log(jnp.broadcast_to(jnp.arange(1, DSTATE + 1, dtype=jnp.float32), (DIN, DSTATE)))
        Ds = jnp.ones((DIN,), dtype=jnp.float32)
        W_out = jax.random.normal(ks[5], (DIN, GCN), dtype=jnp.float32) * 0.05
        gn_w = jnp.ones((PAD,), dtype=jnp.float32)
        gn_b = jnp.zeros((PAD,), dtype=jnp.float32)
        return {'x': x, 'W_in': W_in, 'W_x': W_x, 'W_dt': W_dt, 'b_dt': b_dt, 'A_logs': A_logs, 'Ds': Ds, 'W_out': W_out, 'gn_w': gn_w, 'gn_b': gn_b}
    _L0_conv_all = _L0_conv_setup()
    _L0_conv_in = {k: v for k, v in _L0_conv_all.items() if k in ('W_in', 'W_x', 'W_dt', 'b_dt', 'A_logs', 'Ds', 'W_out', 'gn_w', 'gn_b', )}
    del _L0_conv_all

    def _L1_conv_setup():
        import jax, jax.numpy as jnp
        import numpy as np
        key = jax.random.key(seed)
        ks = jax.random.split(key, 7)
        B, C, H, W = (8, 256, 64, 64)
        Cp = C // 8
        sc = 1.0 / np.sqrt(C)
        return {'x': jax.random.normal(ks[0], (B, C, H, W), dtype=jnp.float32), 'Wq': jax.random.normal(ks[1], (Cp, C), dtype=jnp.float32) * sc, 'bq': jnp.zeros((Cp,), dtype=jnp.float32), 'Wk': jax.random.normal(ks[2], (Cp, C), dtype=jnp.float32) * sc, 'bk': jnp.zeros((Cp,), dtype=jnp.float32), 'Wv': jax.random.normal(ks[3], (C, C), dtype=jnp.float32) * sc, 'bv': jnp.zeros((C,), dtype=jnp.float32), 'gamma': jnp.float32(0.5)}
    _L1_conv_all = _L1_conv_setup()
    _L1_conv_in = {k: v for k, v in _L1_conv_all.items() if k in ('Wq', 'bq', 'Wk', 'bk', 'Wv', 'bv', 'gamma', )}
    del _L1_conv_all

    return {
        "x": x,
        "L0_conv_W_in": _L0_conv_in["W_in"],
        "L0_conv_W_x": _L0_conv_in["W_x"],
        "L0_conv_W_dt": _L0_conv_in["W_dt"],
        "L0_conv_b_dt": _L0_conv_in["b_dt"],
        "L0_conv_A_logs": _L0_conv_in["A_logs"],
        "L0_conv_Ds": _L0_conv_in["Ds"],
        "L0_conv_W_out": _L0_conv_in["W_out"],
        "L0_conv_gn_w": _L0_conv_in["gn_w"],
        "L0_conv_gn_b": _L0_conv_in["gn_b"],
        "L1_conv_Wq": _L1_conv_in["Wq"],
        "L1_conv_bq": _L1_conv_in["bq"],
        "L1_conv_Wk": _L1_conv_in["Wk"],
        "L1_conv_bk": _L1_conv_in["bk"],
        "L1_conv_Wv": _L1_conv_in["Wv"],
        "L1_conv_bv": _L1_conv_in["bv"],
        "L1_conv_gamma": _L1_conv_in["gamma"],
    }

def reference(x, L0_conv_W_in, L0_conv_W_x, L0_conv_W_dt, L0_conv_b_dt, L0_conv_A_logs, L0_conv_Ds, L0_conv_W_out, L0_conv_gn_w, L0_conv_gn_b, L1_conv_Wq, L1_conv_bq, L1_conv_Wk, L1_conv_bk, L1_conv_Wv, L1_conv_bv, L1_conv_gamma):
    import jax
    import jax.numpy as jnp
    def _L0_conv_ref(x, W_in, W_x, W_dt, b_dt, A_logs, Ds, W_out, gn_w, gn_b):
        import jax, jax.numpy as jnp
        from jax import lax
        import numpy as np
        import math
        B, CH, H, W = (4, 256, 64, 64)
        TOK = 8
        GCN = math.ceil(CH / TOK)
        PAD = TOK * GCN
        DIN = 2 * GCN
        DSTATE = 16
        DTR = math.ceil(GCN / 16)
        GROUPS = 4
        EPS = 1e-05

        def _forward(x, W_in, W_x, W_dt, b_dt, A_logs, Ds, W_out, gn_w, gn_b):
            b, c, h, w = x.shape
            M = b * h * w
            xf = jnp.transpose(x, (0, 2, 3, 1)).reshape(M, TOK, GCN)
            xz = xf @ W_in
            xp, z = (xz[..., :DIN], xz[..., DIN:])
            xs = jnp.concatenate([xp, xp[:, ::-1]], axis=0)
            x_dbl = xs @ W_x
            dts = x_dbl[..., :DTR]
            Bs = x_dbl[..., DTR:DTR + DSTATE]
            Cs = x_dbl[..., DTR + DSTATE:]
            dts = dts @ W_dt + b_dt
            A = -jnp.exp(A_logs)
            delta = jax.nn.softplus(dts + b_dt)

            def step(hst, inp):
                d_t, u_t, B_t, C_t = inp
                dA = jnp.exp(d_t[:, :, None] * A)
                hst = dA * hst + (d_t * u_t)[:, :, None] * B_t[:, None, :]
                y_t = jnp.einsum('bdn,bn->bd', hst, C_t)
                return (hst, y_t)
            h0 = jnp.zeros((2 * M, DIN, DSTATE), dtype=x.dtype)
            scan_in = (jnp.swapaxes(delta, 0, 1), jnp.swapaxes(xs, 0, 1), jnp.swapaxes(Bs, 0, 1), jnp.swapaxes(Cs, 0, 1))
            _, ys = lax.scan(step, h0, scan_in)
            ys = jnp.swapaxes(ys, 0, 1) + xs * Ds
            y1, y2 = (ys[:M], ys[M:])
            y = y1 + y2[:, ::-1]
            y = y * jax.nn.gelu(z, approximate=False)
            y = y @ W_out
            y = y.reshape(b, h, w, PAD).transpose(0, 3, 1, 2)
            yg = y.reshape(b, GROUPS, -1)
            mu = yg.mean(-1, keepdims=True)
            var = yg.var(-1, keepdims=True)
            yg = (yg - mu) * lax.rsqrt(var + EPS)
            y = yg.reshape(b, PAD, h, w) * gn_w[None, :, None, None] + gn_b[None, :, None, None]
            return x + y[:, :c]
        return _forward(x, W_in, W_x, W_dt, b_dt, A_logs, Ds, W_out, gn_w, gn_b)

    def _L1_conv_ref(x, Wq, bq, Wk, bk, Wv, bv, gamma):
        import jax, jax.numpy as jnp
        import numpy as np
        B, C, H, W = x.shape
        xf = x.reshape(B, C, H * W)
        q = jnp.einsum('dc,bcn->bnd', Wq, xf) + bq
        k = jnp.einsum('dc,bcn->bdn', Wk, xf) + bk[:, None]
        v = jnp.einsum('dc,bcn->bdn', Wv, xf) + bv[:, None]
        scores = jnp.einsum('bnd,bdm->bnm', q, k)
        attn = jax.nn.softmax(scores, axis=-1)
        o = jnp.einsum('bcm,bnm->bcn', v, attn)
        o = o.reshape(B, C, H, W)
        return gamma * o + x

    def _gn(v, G=32, eps=1e-5):
        B_, C_, H_, W_ = v.shape
        g = v.reshape(B_, G, C_ // G, H_, W_)
        m = jnp.mean(g, axis=(2, 3, 4), keepdims=True)
        s = jnp.var(g, axis=(2, 3, 4), keepdims=True)
        return ((g - m) / jnp.sqrt(s + eps)).reshape(v.shape)

    def _ln_c(v, eps=1e-6):
        m = jnp.mean(v, axis=1, keepdims=True)
        s = jnp.var(v, axis=1, keepdims=True)
        return (v - m) / jnp.sqrt(s + eps)

    def _ln_t(v, eps=1e-5):
        m = jnp.mean(v, axis=-1, keepdims=True)
        s = jnp.var(v, axis=-1, keepdims=True)
        return (v - m) / jnp.sqrt(s + eps)

    def _to_tokens(v):
        B_, C_, H_, W_ = v.shape
        return v.reshape(B_, C_, H_ * W_).transpose(0, 2, 1)
    def _from_tokens(t, like):
        B_, C_, H_, W_ = like.shape
        return t.transpose(0, 2, 1).reshape(B_, C_, H_, W_)

    x = _L0_conv_ref(x, L0_conv_W_in, L0_conv_W_x, L0_conv_W_dt, L0_conv_b_dt, L0_conv_A_logs, L0_conv_Ds, L0_conv_W_out, L0_conv_gn_w, L0_conv_gn_b)
    x = _L1_conv_ref(x, L1_conv_Wq, L1_conv_bq, L1_conv_Wk, L1_conv_bk, L1_conv_Wv, L1_conv_bv, L1_conv_gamma)
    return x


_drawn_inputs = setup_inputs


def setup_inputs(seed=0):
    import zlib

    import numpy as np

    out = dict(_drawn_inputs(seed))
    spreads = {'L0_conv_Ds': (1.0, 0.6),
     'L0_conv_gn_w': (1.0, 0.2),
     'L0_conv_gn_b': (0.0, 0.1),
     'L1_conv_bq': (0.0, 0.1),
     'L1_conv_bk': (0.0, 2.0),
     'L1_conv_bv': (0.0, 0.719)}
    factors = {'L0_conv_W_x': 64.0, 'L0_conv_W_dt': 64.0, 'L0_conv_b_dt': 64.0, 'L0_conv_A_logs': 8.0}
    for name, (base, spread) in spreads.items():
        noise = np.random.default_rng([zlib.crc32(name.encode()), seed]).standard_normal(out[name].shape)
        drawn = base * np.exp(spread * noise) if base else spread * noise
        out[name] = jnp.asarray(drawn.astype(out[name].dtype))
    for name, factor in factors.items():
        out[name] = (out[name] * factor).astype(out[name].dtype)
    return out
```

```python
import numpy as np
from contextlib import ExitStack

import concourse.bass as bass
from concourse import mybir

F32 = mybir.dt.float32
BF16 = mybir.dt.bfloat16
ALU = mybir.AluOpType
ACT = mybir.ActivationFunctionType
AX = mybir.AxisListType

P = 128
IMAGES, CH, PIX = 4, 256, 64 * 64
TOK, GCN, DIN, NST = 8, 32, 64, 16
PB = 128
BLOCKS = PIX // PB
ALL = IMAGES * BLOCKS
TILES = 4
HT = TOK // 2
BANK = 512
KG = PIX // BANK
CHUNK = 512
CHUNKS = PIX // CHUNK
VC = CH + 1
GN_EPS = 1e-5
POOL_SUMS = (1, 2, 3)
FWD, BWD = 15, 15 + len(POOL_SUMS)
SC = TOK + (TOK - 2 - len(POOL_SUMS))
DMA = 16


def wait(eng, sem, value):
    if isinstance(value, int) and value <= 0:
        return
    assert isinstance(value, int) or value.min_val > 0
    eng.wait_ge(sem, value)


def build(nc, x, W_in, W_x, W_dt, b_dt, A_logs, Ds, W_out, gn_w, gn_b, Wq, bq, Wk, bk, Wv, bv, gamma,
          ident_in, spread_in, sum_in, group_in, out):
    ctx = ExitStack()
    with ctx:
        def sb(name, shape, dt=F32):
            return ctx.enter_context(nc.sbuf_tensor(name, shape, dt))

        def ps(name, shape, dt=F32):
            return ctx.enter_context(nc.psum_tensor(name, shape, dt))

        def sem(name):
            return ctx.enter_context(nc.semaphore(name))

        x_v = x.rearrange("b (h p) y z -> b p h (y z)", p=P)
        x_tok = x.rearrange("b (t g) y z -> b g t (y z)", g=GCN)
        out_v = out.rearrange("b (h p) y z -> b p h (y z)", p=P)
        y_dram = nc.dram_tensor("y_scratch", (P, 2, PIX), F32, kind="Internal").ap()
        x1_dram = nc.dram_tensor("x1_scratch", (P, 2, PIX), F32, kind="Internal").ap()
        qa_dram = nc.dram_tensor("qa_scratch", (96, PIX), BF16, kind="Internal").ap()
        qb_dram = nc.dram_tensor("qb_scratch", (96, PIX), BF16, kind="Internal").ap()

        ident = sb("ident", [P, P])
        identb = sb("identb", [P, P], BF16)
        spread = sb("spread", [96, TILES, P], BF16)
        statesum = sb("statesum", [P, 2 * TILES, DIN])
        groupmean = sb("groupmean", [P, P])
        w_in = sb("w_in", [GCN, 2 * DIN])
        w_u = sb("w_u", [GCN, P])
        w_skip = sb("w_skip", [GCN, DIN])
        w_dbc = sb("w_dbc", [GCN, 3, P])
        w_out = sb("w_out", [P, 2, GCN])
        a_col = sb("a_col", [P, 2 * TILES])
        b2_col = sb("b2_col", [P, 1])
        gnw = sb("gnw", [P, 2])
        gnb = sb("gnb", [P, 2])
        wq_t = sb("wq_t", [P, 2, 96])
        wk_t = sb("wk_t", [P, 2, 96])
        wv_t = sb("wv_t", [P, 2, CH])
        bq_col = sb("bq_col", [96, 1])
        bk_col = sb("bk_col", [96, 1])
        bv_row = sb("bv_row", [1, CH])
        ones_row = sb("ones_row", [1, P])
        gamma_col = sb("gamma_col", [P, 1])

        xa = sb("xa", [GCN, TOK, PB])
        xb = sb("xb", [GCN, TOK, PB])
        t_e = sb("t_e", [P, TOK * PB])
        t_r = sb("t_r", [P, TOK * PB])
        t_l = sb("t_l", [P, TOK * PB])
        t_c = sb("t_c", [P, TOK * PB])
        top = sb("top", [P, TOK * PB], BF16)
        mid = sb("mid", [P, TOK * PB], BF16)
        low = sb("low", [P, TOK * PB], BF16)
        parts_delta = [sb(f"parts_delta{h}", [96, TOK * PB], BF16) for h in range(2)]
        parts_du = [sb(f"parts_du{h}", [96, TOK * PB], BF16) for h in range(2)]
        b_rep = sb("b_rep", [P, TOK, PB])
        c_rep = sb("c_rep", [P, TOK, PB])
        decay = [sb(f"decay{h}", [P, TOK, TILES, PB]) for h in range(2)]
        inject = sb("inject", [P, TOK, TILES, PB])
        fwd = [sb(f"fwd{h}", [P, TOK, TILES, PB]) for h in range(2)]
        bwd = sb("bwd", [P, TOK, TILES, PB])
        gz = sb("gz", [P, HT * PB])
        yz = sb("yz", [P, HT * PB])
        yo = sb("yo", [P, 2, PB])
        stats = sb("stats", [P, 2, BLOCKS, 6])
        mv = sb("mv", [P, 2, 2])
        gst = sb("gst", [P, 2, 2])
        gsum = sb("gsum", [P, 2, 2])
        gvar = sb("gvar", [P, 2])
        gsd = sb("gsd", [P, 2])
        gscale = sb("gscale", [P, 2])
        gbias = sb("gbias", [P, 2])
        ka = sb("ka", [99, PIX], BF16)
        kb = sb("kb", [96, PIX], BF16)
        v_t = sb("v_t", [P, PIX // P, VC])
        qa = sb("qa", [99, PB], BF16)
        qb = sb("qb", [96, PB], BF16)
        x1b = sb("x1b", [P, 2, PB])
        prob = [sb(f"prob{i}", [P, BANK]) for i in range(2)]
        mx8 = sb("mx8", [P, KG])
        nmax = sb("nmax", [P, 1])
        nres = sb("nres", [P, 1])
        nparts = sb("nparts", [P, 3], BF16)
        rden = sb("rden", [P, 2])
        o_n = sb("o_n", [P, CH])
        o_c = sb("o_c", [P, 2, PB])

        d0 = inject[:, :, :, :].rearrange("p t j x -> p (t j x)")
        d1 = decay[1][:, :, :, :].rearrange("p t j x -> p (t j x)")
        f0 = fwd[0][:, :, :, :].rearrange("p t j x -> p (t j x)")

        def halves(ap):
            return ap.rearrange("p (h x) -> p h x", h=2)

        yc = [halves(d0[:, i * 1024:(i + 1) * 1024]) for i in range(2)]
        xc = [halves(d0[:, (2 + i) * 1024:(3 + i) * 1024]) for i in range(2)]
        xm = [halves(d1[:, i * 1024:(i + 1) * 1024]) for i in range(2)]
        x1c = [halves(d1[:, (2 + i) * 1024:(3 + i) * 1024]) for i in range(2)]
        kf = f0[0:96, 0:CHUNK]
        qf = f0[0:96, CHUNK:2 * CHUNK]
        kres = f0[0:96, 2 * CHUNK:3 * CHUNK]
        qres = f0[0:96, 3 * CHUNK:4 * CHUNK]
        qac = fwd[1][0:96, 0, 0:2, :].rearrange("p j x -> p (j x)").bitcast(BF16)
        qbc = fwd[1][0:96, 0, 2:4, :].rearrange("p j x -> p (j x)").bitcast(BF16)

        p_delta = [ps(f"p_delta{i}", [P, BANK]) for i in range(2)]
        p_du = [ps(f"p_du{i}", [P, BANK]) for i in range(2)]
        p_c = ps("p_c", [P, BANK])
        p_y = ps("p_y", [P, BANK])
        p_s = ps("p_s", [P, BANK])
        p_o = ps("p_o", [P, BANK])

        consts_in = sem("consts_in")
        setup_pe, setup_dve, setup_act, setup_ready = sem("setup_pe"), sem("setup_dve"), sem("setup_act"), sem("setup_ready")
        xa_in, xb_in = sem("xa_in"), sem("xb_in")
        dts_ready, u_ready, b_ready, c_ready, z_ready, yo_ready = map(
            sem, ("dts_ready", "u_ready", "b_ready", "c_ready", "z_ready", "yo_ready"))
        abs_relu, e_ready, ln_ready, square_ready, top_ready, mid_ready = map(
            sem, ("abs_relu", "e_ready", "ln_ready", "square_ready", "top_ready", "mid_ready"))
        sp_step, du_ready, res_ready, low_ready = map(sem, ("sp_step", "du_ready", "res_ready", "low_ready"))
        delta_in = [sem(f"delta_in{h}") for h in range(2)]
        du_in = [sem(f"du_in{h}") for h in range(2)]
        b_copied, c_copied, gz_ready, yo_copied = map(sem, ("b_copied", "c_copied", "gz_ready", "yo_copied"))
        delta_spread, du_spread, decay_ready, inject_ready = map(
            sem, ("delta_spread", "du_spread", "decay_ready", "inject_ready"))
        fwd_step, bwd_step, c_step, y_summed, skip_done, gated, stat_done, y_stored = map(
            sem, ("fwd_step", "bwd_step", "c_step", "y_summed", "skip_done", "gated", "stat_done", "y_stored"))
        gn_step, gn_pe, gn_act = sem("gn_step"), sem("gn_pe"), sem("gn_act")
        chunk_in = [sem(f"chunk_in{i}") for i in range(2)]
        xm_ready, x1_ready, kq_ready, v_ready, kq_copied, v_copied = map(
            sem, ("xm_ready", "x1_ready", "kq_ready", "v_ready", "kq_copied", "v_copied"))
        a_done, kq_res, b_done, kq_parts, x1_stored, q_stored = map(
            sem, ("a_done", "kq_res", "b_done", "kq_parts", "x1_stored", "q_stored"))
        q_in, x1_in = sem("q_in"), sem("x1_in")
        rows_ready, max_step, nmax_step, nmax_t, nmax_in = map(
            sem, ("rows_ready", "max_step", "nmax_step", "nmax_t", "nmax_in"))
        cols_ready, prob_ready, pv_done, den_step, o_norm, o_turned, o_added, out_stored = map(
            sem, ("cols_ready", "prob_ready", "pv_done", "den_step", "o_norm", "o_turned", "o_added", "out_stored"))

        passed = {e.engine: sem(f"passed_{n}") for n, e in (("sp", nc.sync), ("pe", nc.tensor), ("act", nc.scalar), ("dve", nc.vector))}
        CONSTS = [0]

        def peeled(b):
            return 2 if isinstance(b, int) and b == 0 else 1

        def chunk_pairs(eng, b):
            if isinstance(b, int) and b == 0:
                yield 0
                with eng.Fori(1, CHUNKS // 2) as pair:
                    yield pair
            else:
                with eng.Fori(0, CHUNKS // 2) as pair:
                    yield pair

        def c_count(tokens):
            return sum(1 + (t not in POOL_SUMS and 0 < t < TOK - 1) for t in range(TOK - tokens, TOK))

        def wait_alone(eng, sem, value):
            wait(eng, sem, value)
            if not isinstance(value, int):
                eng.sem_inc(passed[eng.engine], 1)

        block = ctx.enter_context(nc.Block())

        @block.sync
        def _(sp):
            n = 0
            src_dst = [(ident[:, :], ident_in), (groupmean[:, :], group_in),
                       (t_r[0:96, 2 * CH:4 * CH].rearrange("p (j x) -> p j x", j=TILES), spread_in), (statesum[:, :, :], sum_in)]
            src_dst.append((w_in[:, :], W_in))
            for r in range(2):
                src_dst.append((t_c[DIN * r:DIN * r + DIN, 0:GCN], W_out))
                src_dst.append((b2_col[DIN * r:DIN * r + DIN, :], b_dt.rearrange("(d o) -> d o", o=1)))
            for r in range(3):
                src_dst.append((bq_col[32 * r:32 * r + 32, :], bq.rearrange("(d o) -> d o", o=1)))
                src_dst.append((bk_col[32 * r:32 * r + 32, :], bk.rearrange("(d o) -> d o", o=1)))
            src_dst += [
                (t_e[0:DIN, 0:34], W_x), (t_e[0:2, 64:128], W_dt),
                (t_e[0:GCN, 128:192], Ds.rearrange("(o d) -> o d", o=1).to_broadcast([GCN, DIN])),
                (t_r[0:32, 0:CH], Wq), (t_r[0:32, CH:2 * CH], Wk),
                (t_l[:, 0:CH], Wv[0:P, :]), (t_l[:, CH:2 * CH], Wv[P:2 * P, :]),
                (bv_row[:, :], bv.rearrange("(o d) -> o d", o=1)),
                (gamma_col[:, :], gamma.rearrange("(o d) -> o d", o=1).to_broadcast([P, 1])),
            ]
            for dst, src in src_dst:
                sp.dma_start(dst, src).then_inc(consts_in, DMA)
                n += 1
            with nc.allow_non_contiguous_dma(reason="small parameters, once"):
                sp.dma_start(a_col[:, :], A_logs.rearrange("(j d) n -> (d n) j", d=8)).then_inc(consts_in, DMA)
                sp.dma_start(gnw[:, :], gn_w.rearrange("(h p) -> p h", p=P)).then_inc(consts_in, DMA)
                sp.dma_start(gnb[:, :], gn_b.rearrange("(h p) -> p h", p=P)).then_inc(consts_in, DMA)
            CONSTS[0] = (n + 3) * DMA

            def load_xa(b, i):
                sp.dma_start(xa[:, :, :], x_tok[b, :, :, bass.ds(i * PB, PB)]).then_inc(xa_in, DMA)

            def load_q(a, i, b_done_count):
                wait_alone(sp, q_stored, b_done_count * CHUNKS * 2 * DMA)
                wait_alone(sp, x1_stored, b_done_count * CHUNKS * DMA)
                wait_alone(sp, cols_ready, KG * a)
                sp.dma_start(qa[0:96, :], qa_dram[:, bass.ds(i * PB, PB)]).then_inc(q_in, DMA)
                sp.dma_start(qb[:, :], qb_dram[:, bass.ds(i * PB, PB)]).then_inc(q_in, DMA)
                wait_alone(sp, o_added, a)
                sp.dma_start(x1b[:, :, :], x1_dram[:, :, bass.ds(i * PB, PB)]).then_inc(x1_in, DMA)

            def spread_parts(k):
                wait_alone(sp, top_ready, k + 1)
                for h, (bufs, sems, base, used) in enumerate(
                        [(parts_delta, delta_in, 0, delta_spread), (parts_du, du_in, DIN, du_spread)] * 2):
                    q, h = h % 2, h // 2
                    wait_alone(sp, used, 16 * k - 8 * (1 - h))
                    sp.dma_start(bufs[h][0:32, :], top[base + 32 * h:base + 32 * h + 32, :]).then_inc(sems[h], DMA)
                wait_alone(sp, mid_ready, k + 1)
                wait_alone(sp, low_ready, k + 1)
                for h in range(2):
                    for bufs, sems, base in ((parts_delta, delta_in, 0), (parts_du, du_in, DIN)):
                        for n_part, part in ((1, mid), (2, low)):
                            sp.dma_start(bufs[h][32 * n_part:32 * n_part + 32, :],
                                         part[base + 32 * h:base + 32 * h + 32, :]).then_inc(sems[h], DMA)

            def store_y(k, i):
                wait_alone(sp, yo_copied, k + 1)
                sp.dma_start(y_dram[:, :, bass.ds(i * PB, PB)], yo[:, :, :]).then_inc(y_stored, DMA)

            def store_out(a, b, i):
                wait_alone(sp, o_added, a + 1)
                sp.dma_start(out_v[b, :, :, bass.ds(i * PB, PB)], o_c[:, :, :]).then_inc(out_stored, DMA)

            def load_xb(k, b, i):
                wait_alone(sp, skip_done, k)
                wait_alone(sp, z_ready, k)
                sp.dma_start(xb[:, :, :], x_tok[b, :, :, bass.ds(i * PB, PB)]).then_inc(xb_in, DMA)

            def next_xa(k, b, i):
                wait_alone(sp, b_ready, 2 * k + 2)
                load_xa(b, i)

            def iteration(k, b, i, head, att, last=False):
                if att:
                    load_q(att[0], att[2], b)
                spread_parts(k + 1)
                if not head:
                    store_y(k - 1, i - 1)
                if att:
                    store_out(*att)
                if not last:
                    load_xb(k + 1, b, i + 1)

            def phase(b, att):
                k0 = b * BLOCKS
                a0 = k0 - BLOCKS
                for i in range(peeled(b)):
                    iteration(k0 + i, b, i, i == 0, (a0 + i, b - 1, i) if att else None)
                    next_xa_at(b, i)
                with sp.Fori(peeled(b), BLOCKS - 2) as i:
                    iteration(k0 + i, b, i, False, (a0 + i, b - 1, i) if att else None)
                    next_xa_at(b, i)
                for i in (BLOCKS - 2, BLOCKS - 1):
                    iteration(k0 + i, b, i, False, (a0 + i, b - 1, i) if att else None, last=i == BLOCKS - 1)
                    if i == BLOCKS - 2:
                        next_image_xa(b, 0, k0 + i)
                    else:
                        load_next_xb(b, k0 + i)
                        next_image_xa(b, 1, k0 + i)
                store_y(k0 + BLOCKS - 1, BLOCKS - 1)

            def next_xa_at(b, i):
                next_xa(b * BLOCKS + i + 1, b, i + 2)

            def clamp(b):
                return min(b + 1, IMAGES - 1) if isinstance(b, int) else b + 1

            def next_image_xa(b, place, k):
                next_xa(k + 1, clamp(b), place)

            def load_next_xb(b, k):
                load_xb(k + 1, clamp(b), 0)

            def prep(b):
                k_end = BLOCKS * (b + 1)
                wait_alone(sp, y_stored, DMA * k_end)
                for pair in chunk_pairs(sp, b):
                    c0 = pair * 2
                    for par in range(2):
                        c = c0 + par
                        n_c = b * CHUNKS + c0
                        wait_alone(sp, xm_ready, 2 * n_c) if par == 0 else None
                        cols = bass.ds(c * CHUNK, CHUNK)
                        sp.dma_start(yc[par], y_dram[:, :, cols]).then_inc(chunk_in[par], DMA)
                        sp.dma_start(xc[par], x_v[b, :, :, cols]).then_inc(chunk_in[par], DMA)
                    for par in range(2):
                        c = c0 + par
                        n_c = b * CHUNKS + c
                        cols = bass.ds(c * CHUNK, CHUNK)
                        wait_alone(sp, x1_ready, 2 * n_c + 2)
                        sp.dma_start(x1_dram[:, :, cols], x1c[par]).then_inc(x1_stored, DMA)
                        wait_alone(sp, kq_parts, 6 * n_c + 6)
                        sp.dma_start(qa_dram[:, cols], qac).then_inc(q_stored, DMA)
                        sp.dma_start(qb_dram[:, cols], qbc).then_inc(q_stored, DMA)

            load_xa(0, 0)
            sp.dma_start(xb[:, :, :], x_tok[0, :, :, 0:PB]).then_inc(xb_in, DMA)
            wait_alone(sp, setup_ready, 1)
            spread_parts(0)
            wait_alone(sp, b_ready, 2)
            load_xa(0, 1)
            phase(0, False)
            prep(0)
            phase(1, True)
            with sp.Fori(2, IMAGES - 1) as b:
                prep(b - 1)
                phase(b, True)
            prep(IMAGES - 2)
            phase(IMAGES - 1, True)
            prep(IMAGES - 1)
            with sp.Fori(0, BLOCKS) as i:
                load_q(ALL - BLOCKS + i, i, IMAGES)
                store_out(ALL - BLOCKS + i, IMAGES - 1, i)
            sp.wait_ge(out_stored, DMA * ALL)
            sp.wait_ge(y_stored, DMA * ALL)
            sp.wait_ge(x1_stored, DMA * IMAGES * CHUNKS)
            sp.wait_ge(q_stored, 2 * DMA * IMAGES * CHUNKS)
            sp.wait_ge(xa_in, DMA * (ALL + 2))
            sp.wait_ge(xb_in, DMA * (ALL + 1))
            for h in range(2):
                sp.wait_ge(delta_in[h], 3 * DMA * (ALL + 1))
                sp.wait_ge(du_in[h], 3 * DMA * (ALL + 1))

        @block.tensor
        def _(pe):
            mm = pe.matmul

            def project(dst, weights, xt, tokens, done):
                for n, t in enumerate(tokens):
                    last = mm(dst[:, n * PB:(n + 1) * PB], weights, xt[:, t, :], start=True, stop=True)
                last.then_inc(done, 1)

            def dts(k, th):
                if th == 0:
                    wait(pe, xa_in, DMA * (k + 1))
                wait(pe, abs_relu, 4 * k + 2 * th)
                project(p_c, w_dbc[:, 0, :], xa, range(HT * th, HT * th + HT), dts_ready)

            def u(k, th):
                wait(pe, abs_relu, 4 * k + 4)
                wait(pe, du_ready, 2 * k + th)
                project(p_c, w_u[:, :], xa, range(HT * th, HT * th + HT), u_ready)

            def b_states(k, th):
                wait(pe, b_copied, 2 * k + th)
                project(p_c, w_dbc[:, 1, :], xa, range(HT * th, HT * th + HT), b_ready)

            def c_states(k, th):
                wait(pe, xb_in, DMA * (k + 1))
                wait(pe, du_ready, 2 * (k + 1) + 2)
                wait(pe, c_copied, 2 * k + th)
                project(p_c, w_dbc[:, 2, :], xb, range(HT * th, HT * th + HT), c_ready)

            def z_gate(k):
                wait(pe, b_copied, 2 * (k + 1) + 2)
                for t in range(TOK):
                    h = t // HT
                    last = mm(p_c[DIN * h:DIN * h + DIN, (t % HT) * PB:(t % HT + 1) * PB],
                              w_in[:, DIN:2 * DIN], xb[:, t, :], start=True, stop=True)
                last.then_inc(z_ready, 1)

            def y_out(k):
                wait_alone(pe, gated, k + 1)
                for t in range(TOK):
                    r, h = 32 * (t % HT), t // HT
                    last = mm(p_c[r:r + 32, h * PB:(h + 1) * PB], w_out[:, h, :],
                              yz[:, (t % HT) * PB:(t % HT + 1) * PB], start=True, stop=True)
                last.then_inc(yo_ready, 1)

            def spread_delta(k, h, i):
                n = 16 * k + 8 * h + i
                th, j = 1 - i // TILES, i % TILES
                if i == 0:
                    wait(pe, delta_in[h], 3 * DMA * (k + 1))
                wait(pe, decay_ready, n - 1)
                mm(p_delta[i % 2][:, :], spread[:, j, :], parts_delta[h][:, th * BANK:(th + 1) * BANK],
                   start=True, stop=True).then_inc(delta_spread, 1)

            def spread_du(k, h, i):
                n = 16 * k + 8 * h + i
                th, j = 1 - i // TILES, i % TILES
                if i == 0:
                    wait(pe, du_in[h], 3 * DMA * (k + 1))
                wait(pe, inject_ready, n - 1)
                mm(p_du[i % 2][:, :], spread[:, j, :], parts_du[h][:, th * BANK:(th + 1) * BANK],
                   start=True, stop=True).then_inc(du_spread, 1)

            def sum_states(k, h, th):
                unit = 2 * k + h
                if h == 0:
                    wait(pe, gated, k)
                wait(pe, c_step, SC * unit + (SC if th == 0 else c_count(HT)))
                region = p_y[DIN * th:DIN * th + DIN, :]
                for j in range(TILES):
                    last = mm(region, statesum[:, TILES * h + j, :], fwd[h][:, HT * th:HT * th + HT, j, :],
                              start=(h == 0 and j == 0), stop=(h == 1 and j == TILES - 1))
                last.then_inc(y_summed, 1)

            def skip_term(k):
                for t in range(TOK):
                    h = t // HT
                    last = mm(p_y[DIN * h:DIN * h + DIN, (t % HT) * PB:(t % HT + 1) * PB],
                              w_skip[:, :], xb[:, t, :], start=False, stop=False, skip_group_check=True)
                last.then_inc(skip_done, 1)

            def key_rows(a, g):
                if g == 0:
                    wait(pe, q_in, 2 * DMA * (a + 1))
                    wait(pe, o_added, a)
                wait(pe, max_step, KG * a + g)
                cols = slice(g * BANK, (g + 1) * BANK)
                mm(p_s[:, :], qa[0:96, :], ka[0:96, cols], start=True, stop=False)
                mm(p_s[:, :], qb[:, :], kb[:, cols], start=False, stop=True).then_inc(rows_ready, 1)

            def turn_max(a):
                wait(pe, nmax_step, 5 * a + 5)
                wait(pe, max_step, KG * a + KG)
                pe.transpose(p_s[0:3, 0:PB // 2].bitcast(BF16), nparts[:, :], identb[:, :]).then_inc(nmax_t, 1)

            def key_cols(a, g):
                wait(pe, nmax_in, a + 1)
                wait(pe, prob_ready, KG * a + g)
                for m in range(4):
                    keys = slice(g * BANK + m * P, g * BANK + (m + 1) * P)
                    region = p_s[:, m * PB:(m + 1) * PB]
                    mm(region, ka[:, keys], qa[:, :], start=True, stop=False)
                    last = mm(region, kb[:, keys], qb[:, :], start=False, stop=True)
                last.then_inc(cols_ready, 1)

            def values(a, g):
                if g == 0:
                    wait(pe, o_norm, a)
                wait(pe, prob_ready, KG * a + g + 1)
                for m in range(4):
                    last = mm(p_o[:, 0:VC], prob[g % 2][:, m * PB:(m + 1) * PB], v_t[:, 4 * g + m, :],
                              start=(g == 0 and m == 0), stop=(g == KG - 1 and m == 3))
                last.then_inc(pv_done, 1)

            def turn_out(a):
                wait(pe, o_norm, a + 1)
                for h in range(2):
                    last = pe.transpose(p_s[:, h * PB:(h + 1) * PB], o_n[:, h * P:(h + 1) * P], ident[:, :])
                last.then_inc(o_turned, 1)

            def iteration(k, head, att):
                if head:
                    wait(pe, yo_copied, k)
                wait(pe, gz_ready, k)
                wait(pe, b_copied, 2 * k + 2)
                for i in range(8):
                    spread_du(k, 0, i)
                    spread_delta(k, 1, i)
                    if i == 0:
                        dts(k + 1, 0)
                    if i == 2:
                        dts(k + 1, 1)
                    if att is not None:
                        key_rows(att, i)
                if att is not None:
                    turn_max(att)
                u(k + 1, 0)
                if not head:
                    sum_states(k - 1, 1, 1)
                u(k + 1, 1)
                if not head:
                    sum_states(k - 1, 1, 0)
                c_states(k, 0)
                c_states(k, 1)
                for i in range(8):
                    spread_du(k, 1, i)
                    if i == 1 and not head:
                        wait(pe, c_copied, 2 * k + 2)
                        y_out(k - 1)
                    if att is not None and i < 4:
                        key_cols(att, i)
                        if i >= 1:
                            values(att, i - 1)
                if head:
                    wait(pe, c_copied, 2 * k + 2)
                else:
                    wait(pe, yo_copied, k)
                b_states(k + 1, 0)
                b_states(k + 1, 1)
                z_gate(k)
                for i in range(4):
                    spread_delta(k + 1, 0, 2 * i)
                    spread_delta(k + 1, 0, 2 * i + 1)
                    if att is not None:
                        key_cols(att, 4 + i)
                        values(att, 3 + i)
                    if i == 1:
                        sum_states(k, 0, 1)
                sum_states(k, 0, 0)
                skip_term(k)
                if att is not None:
                    values(att, KG - 1)
                    turn_out(att)

            def tail(k):
                sum_states(k, 1, 1)
                sum_states(k, 1, 0)
                wait(pe, gz_ready, k + 1)
                y_out(k)

            def prep(b):
                wait(pe, gn_step, 12 * b + 4)
                wait(pe, yo_copied, BLOCKS * (b + 1))
                mm(p_c[:, 0:4], groupmean[:, :], gst[:, :, :].rearrange("p a c -> p (a c)"),
                   start=True, stop=True).then_inc(gn_pe, 1)
                for pair in chunk_pairs(pe, b):
                    c0 = pair * 2
                    for par in range(2):
                        n_c = b * CHUNKS + c0 + par
                        wait(pe, x1_ready, 2 * n_c + 2)
                        wait(pe, kq_copied, 2 * n_c)
                        wait(pe, decay_ready, 16 * BLOCKS * (b + 1) + 8)
                        for bank, w in ((p_delta[0], wk_t), (p_delta[1], wq_t)):
                            for h in range(2):
                                last = mm(bank[0:96, :], w[:, h, :], x1c[par][:, h, :], start=(h == 0), stop=(h == 1))
                            last.then_inc(kq_ready, 1)
                        wait(pe, v_copied, 2 * n_c)
                        for m in range(4):
                            region = p_du[m // 2][:, (m % 2) * CH:(m % 2 + 1) * CH]
                            for h in range(2):
                                mm(region, x1c[par][:, h, m * P:(m + 1) * P], wv_t[:, h, :], start=(h == 0), stop=False)
                            last = mm(region, ones_row[:, :], bv_row[:, :], start=False, stop=True)
                            if m % 2:
                                last.then_inc(v_ready, 1)
                wait_alone(pe, kq_copied, 2 * CHUNKS * (b + 1))
                wait_alone(pe, v_copied, 2 * CHUNKS * (b + 1))

            pe.wait_ge(consts_in, CONSTS[0])
            pe.transpose(p_c[0:DIN, 0:GCN], w_in[:, 0:DIN], ident[0:GCN, 0:GCN]).then_inc(setup_pe, 1)
            pe.transpose(p_y[0:2, 0:DIN], t_e[0:DIN, 0:2], ident[0:DIN, 0:DIN]).then_inc(setup_pe, 1)
            for n, bank in ((0, p_s), (1, p_o)):
                for h in range(2):
                    last = pe.transpose(bank[:, h * 32:(h + 1) * 32], t_r[0:32, n * CH + h * P:n * CH + (h + 1) * P],
                                        ident[0:32, 0:32])
            last.then_inc(setup_pe, 1)
            for h in range(2):
                for c in range(2):
                    last = pe.transpose(p_du[h][:, c * P:(c + 1) * P], t_l[:, c * CH + h * P:c * CH + (h + 1) * P],
                                        ident[:, :])
            last.then_inc(setup_pe, 1)
            pe.wait_ge(setup_dve, 2)
            mm(p_delta[0][0:DIN, 0:DIN], t_c[0:2, 64:128], t_e[0:2, 64:128], start=True, stop=True).then_inc(setup_pe, 1)
            pe.wait_ge(setup_dve, 4)
            mm(p_delta[1][0:GCN, 0:3 * P], t_c[0:DIN, 128:128 + GCN], t_c[0:DIN, 256:640], start=True, stop=True).then_inc(setup_pe, 1)
            pe.wait_ge(setup_ready, 1)
            dts(0, 0)
            dts(0, 1)
            u(0, 0)
            u(0, 1)
            pe.wait_ge(du_ready, 2)
            b_states(0, 0)
            b_states(0, 1)
            for i in range(8):
                spread_delta(0, 0, i)

            def phase(b, att):
                k0 = b * BLOCKS
                for i in range(peeled(b)):
                    iteration(k0 + i, i == 0, k0 - BLOCKS + i if att else None)
                with pe.Fori(peeled(b), BLOCKS) as i:
                    iteration(k0 + i, False, k0 - BLOCKS + i if att else None)
                tail(k0 + BLOCKS - 1)

            phase(0, False)
            prep(0)
            phase(1, True)
            with pe.Fori(2, IMAGES) as b:
                prep(b - 1)
                phase(b, True)
            prep(IMAGES - 1)
            with pe.Fori(ALL - BLOCKS, ALL) as a:
                for g in range(KG):
                    key_rows(a, g)
                turn_max(a)
                for g in range(KG):
                    key_cols(a, g)
                    if g:
                        values(a, g - 1)
                values(a, KG - 1)
                turn_out(a)

        @block.scalar
        def _(act):
            f = nc.scalar.activation

            def abs_relu_half(k, th):
                cols = slice(th * BANK, (th + 1) * BANK)
                wait(act, dts_ready, 2 * k + th + 1)
                if th == 0:
                    wait(act, res_ready, k)
                    wait(act, low_ready, k)
                f(t_e[:, cols], p_c[:, :], ACT.Abs, bias=b2_col[:, :]).then_inc(abs_relu, 1)
                f(t_r[:, cols], p_c[:, :], ACT.Relu, bias=b2_col[:, :]).then_inc(abs_relu, 1)

            def exp_abs(k):
                wait(act, abs_relu, 4 * k + 4)
                f(t_e[:, :], t_e[:, :], ACT.Exp, scale=-1.0).then_inc(e_ready, 1)

            def log_part(k):
                wait(act, e_ready, k + 1)
                f(t_l[:, :], t_e[:, :], ACT.Ln, bias=1.0).then_inc(ln_ready, 1)

            def square(k):
                wait(act, sp_step, 5 * k + 2)
                f(t_l[:, :], t_e[:, :], ACT.Square, scale=0.5 ** 0.5).then_inc(square_ready, 1)

            def top_part(k):
                wait(act, du_ready, 2 * k + 2)
                for s in (delta_in, du_in):
                    for h in range(2):
                        wait(act, s[h], 3 * DMA * k)
                f(top[:, :], t_l[:, :], ACT.Copy).then_inc(top_ready, 1)

            def mid_part(k):
                wait(act, res_ready, k + 1)
                f(mid[:, :], t_r[:, :], ACT.Copy).then_inc(mid_ready, 1)

            def decays(k, h, i):
                n = 16 * k + 8 * h + i
                th, j = 1 - i // TILES, i % TILES
                wait(act, delta_spread, n + 1)
                if i == 0:
                    wait(act, fwd_step, FWD * (2 * k + h - 1))
                    wait(act, bwd_step, BWD * (2 * k + h - 1))
                f(decay[h][:, HT * th:HT * th + HT, j, :],
                  p_delta[i % 2][:, :].rearrange("p (t x) -> p t x", t=HT), ACT.Exp,
                  scale=a_col[:, TILES * h + j:TILES * h + j + 1]).then_inc(decay_ready, 1)

            def copy_b(k, th):
                wait(act, b_ready, 2 * k + th + 1)
                if th == 0:
                    wait(act, inject_ready, 16 * k)
                f(b_rep[:, HT * th:HT * th + HT, :], p_c[:, :].rearrange("p (t x) -> p t x", t=HT),
                  ACT.Copy).then_inc(b_copied, 1)

            def copy_c(k, th):
                wait(act, c_ready, 2 * k + th + 1)
                if th == 0:
                    wait(act, c_step, 2 * SC * k)
                f(c_rep[:, HT * th:HT * th + HT, :], p_c[:, :].rearrange("p (t x) -> p t x", t=HT),
                  ACT.Copy).then_inc(c_copied, 1)

            def gelu_z(k):
                wait(act, z_ready, k + 1)
                wait(act, gated, k)
                f(gz[:, :], p_c[:, :], ACT.Gelu).then_inc(gz_ready, 1)
                act.preload_act_table_set("natural_log_exp_and_others")

            def copy_yo(k):
                wait(act, yo_ready, k + 1)
                wait(act, y_stored, DMA * k)
                wait(act, stat_done, 2 * k)
                f(yo[:, :, :], p_c[:, 0:2 * PB].rearrange("p (h x) -> p h x", h=2), ACT.Copy).then_inc(yo_copied, 1)

            def put_max(a):
                wait(act, nmax_t, a + 1)
                f(qa[96:99, :], p_s[0:3, 0:PB // 2].bitcast(BF16), ACT.Copy).then_inc(nmax_in, 1)

            def probs(a, g):
                wait(act, cols_ready, KG * a + g + 1)
                wait(act, pv_done, KG * a + max(g - 1, 0))
                f(prob[g % 2][:, :], p_s[:, :], ACT.Exp).then_inc(prob_ready, 1)

            def norm_o(a):
                wait(act, den_step, 2 * a + 2)
                wait(act, o_turned, a)
                f(o_n[:, :], p_o[:, 0:CH], ACT.Copy, scale=rden[:, 1:2]).then_inc(o_norm, 1)

            def iteration(k, head, att):
                abs_relu_half(k + 1, 0)
                decays(k, 1, 0)
                decays(k, 1, 1)
                abs_relu_half(k + 1, 1)
                exp_abs(k + 1)
                decays(k, 1, 2)
                log_part(k + 1)
                for i in range(3, 8):
                    decays(k, 1, i)
                square(k + 1)
                if att is not None:
                    put_max(att)
                top_part(k + 1)
                copy_c(k, 0)
                copy_c(k, 1)
                mid_part(k + 1)
                if att is not None:
                    probs(att, 0)
                if not head:
                    copy_yo(k - 1)
                if att is not None:
                    for g in range(1, 4):
                        probs(att, g)
                copy_b(k + 1, 0)
                copy_b(k + 1, 1)
                gelu_z(k)
                for i in range(4):
                    decays(k + 1, 0, 2 * i)
                    decays(k + 1, 0, 2 * i + 1)
                    if att is not None:
                        probs(att, 4 + i)
                if att is not None:
                    norm_o(att)

            def prep(b):
                wait(act, gn_step, 12 * b + 8)
                f(gsd[:, :], gvar[:, :], ACT.Sqrt).then_inc(gn_act, 1)
                act.preload_act_table_set("natural_log_exp_and_others")
                wait(act, gn_step, 12 * b + 12)
                for pair in chunk_pairs(act, b):
                    c0 = pair * 2
                    for par in range(2):
                        n_c = b * CHUNKS + c0 + par
                        wait(act, x1_stored, DMA * (b * CHUNKS + c0))
                        wait(act, v_ready, 2 * (b * CHUNKS + c0))
                        for h in range(2):
                            wait(act, xm_ready, 2 * n_c + h + 1)
                            f(x1c[par][:, h, :], xm[par][:, h, :], ACT.Identity, bias=gbias[:, h:h + 1]).then_inc(x1_ready, 1)
                        wait(act, kq_ready, 2 * n_c + 1)
                        wait(act, kq_res, 2 * n_c)
                        f(kf, p_delta[0][0:96, :], ACT.Identity, bias=bk_col[:, :]).then_inc(kq_copied, 1)
                        wait(act, kq_ready, 2 * n_c + 2)
                        f(qf, p_delta[1][0:96, :], ACT.Identity, bias=bq_col[:, :]).then_inc(kq_copied, 1)
                        cols = bass.ds((c0 + par) * CHUNK, CHUNK)
                        wait(act, kq_copied, 2 * n_c + 2)
                        wait(act, kq_parts, 6 * n_c)
                        wait(act, q_stored, 2 * DMA * n_c)
                        f(ka[0:96, cols], kf, ACT.Copy).then_inc(a_done, 1)
                        f(qac, qf, ACT.Copy).then_inc(a_done, 1)
                        wait(act, kq_res, 2 * n_c + 1)
                        f(kb[:, cols], kres, ACT.Copy).then_inc(b_done, 1)
                        wait(act, kq_res, 2 * n_c + 2)
                        f(qbc, qres, ACT.Copy).then_inc(b_done, 1)
                        for m in range(2):
                            wait(act, v_ready, 2 * n_c + m + 1)
                            f(v_t[:, bass.ds((c0 + par) * 4 + 2 * m, 2), 0:CH],
                              p_du[m][:, :].rearrange("p (m c) -> p m c", m=2), ACT.Copy).then_inc(v_copied, 1)
                wait_alone(act, v_ready, 2 * CHUNKS * (b + 1))
                wait_alone(act, x1_stored, DMA * CHUNKS * (b + 1))

            act.wait_ge(consts_in, CONSTS[0])
            act.preload_act_table_set("natural_log_exp_and_others")
            f(a_col[:, :], a_col[:, :], ACT.Exp).then_inc(setup_act, 1)
            act.wait_ge(setup_ready, 1)
            abs_relu_half(0, 0)
            abs_relu_half(0, 1)
            exp_abs(0)
            log_part(0)
            square(0)
            top_part(0)
            mid_part(0)
            copy_b(0, 0)
            copy_b(0, 1)
            for i in range(8):
                decays(0, 0, i)

            def phase(b, att):
                k0 = b * BLOCKS
                for i in range(peeled(b)):
                    iteration(k0 + i, i == 0, k0 - BLOCKS + i if att else None)
                with act.Fori(peeled(b), BLOCKS) as i:
                    iteration(k0 + i, False, k0 - BLOCKS + i if att else None)
                copy_yo(k0 + BLOCKS - 1)

            phase(0, False)
            prep(0)
            phase(1, True)
            with act.Fori(2, IMAGES) as b:
                prep(b - 1)
                phase(b, True)
            prep(IMAGES - 1)
            with act.Fori(ALL - BLOCKS, ALL) as a:
                put_max(a)
                for g in range(KG):
                    probs(a, g)
                norm_o(a)

        @block.vector
        def _(dve):
            tt = nc.vector.tensor_tensor

            def softplus_steps(k):
                def back():
                    wait(dve, e_ready, k + 1)
                    nc.vector.tensor_scalar(t_c[:, :], t_e[:, :], 1.0, -1.0, ALU.add, ALU.add).then_inc(sp_step, 1)

                def less_log():
                    wait(dve, sp_step, 5 * k + 1)
                    wait(dve, ln_ready, k + 1)
                    tt(t_c[:, :], t_c[:, :], t_l[:, :], ALU.subtract).then_inc(sp_step, 1)

                def hold():
                    wait(dve, sp_step, 5 * k + 2)
                    wait(dve, square_ready, k + 1)
                    nc.vector.scalar_tensor_tensor(t_c[:, :], t_c[:, :], 0.0, t_l[:, :], ALU.max, ALU.min).then_inc(sp_step, 1)

                def less_g():
                    wait(dve, sp_step, 5 * k + 3)
                    tt(t_l[:, :], t_e[:, :], t_c[:, :], ALU.subtract).then_inc(sp_step, 1)

                def plus_relu():
                    wait(dve, sp_step, 5 * k + 4)
                    tt(t_l[:, :], t_l[:, :], t_r[:, :], ALU.add).then_inc(sp_step, 1)

                def times_u(th):
                    cols = slice(th * BANK, (th + 1) * BANK)
                    wait(dve, sp_step, 5 * k + 5)
                    wait(dve, u_ready, 2 * k + th + 1)
                    tt(t_l[DIN:P, cols], t_l[DIN:P, cols], p_c[DIN:P, :], ALU.mult).then_inc(du_ready, 1)

                def rest():
                    wait(dve, top_ready, k + 1)
                    tt(t_r[:, :], t_l[:, :], top[:, :], ALU.subtract).then_inc(res_ready, 1)

                def last_part():
                    wait(dve, mid_ready, k + 1)
                    tt(low[:, :], t_r[:, :], mid[:, :], ALU.subtract).then_inc(low_ready, 1)

                return [back, less_log, hold, less_g, plus_relu, lambda: times_u(0), lambda: times_u(1), rest, last_part]

            def inject_item(k, h, i):
                n = 16 * k + 8 * h + i
                th, j = 1 - i // TILES, i % TILES
                if i == 0:
                    wait(dve, fwd_step, FWD * (2 * k + h))
                    wait(dve, bwd_step, BWD * (2 * k + h - 1) + 2 * (HT - 1))
                    wait(dve, b_copied, 2 * k + 2)
                if i == TILES:
                    wait(dve, bwd_step, BWD * (2 * k + h - 1) + FWD)
                wait(dve, du_spread, n + 1)
                ts = slice(HT * th, HT * th + HT)
                tt(inject[:, ts, j, :], p_du[i % 2][:, :].rearrange("p (t x) -> p t x", t=HT),
                   b_rep[:, ts, :], ALU.mult).then_inc(inject_ready, 1)

            def forward(k, h):
                unit = 2 * k + h
                steps = []

                def scale(t):
                    if t == 1:
                        wait(dve, decay_ready, 8 * unit + 8)
                        wait(dve, inject_ready, 8 * unit + 8)
                        wait(dve, y_summed, 2 * (unit - 1))
                        prev = inject[:, 0, :, :]
                    else:
                        wait(dve, fwd_step, FWD * unit + 2 * (t - 1))
                        prev = fwd[h][:, t - 1, :, :]
                    tt(fwd[h][:, t, :, :], decay[h][:, t, :, :], prev, ALU.mult).then_inc(fwd_step, 1)

                def add(t):
                    wait(dve, fwd_step, FWD * unit + 2 * (t - 1) + 1)
                    tt(fwd[h][:, t, :, :], fwd[h][:, t, :, :], inject[:, t, :, :], ALU.add).then_inc(fwd_step, 1)

                def both_at_end():
                    wait(dve, fwd_step, FWD * unit + 14)
                    tt(fwd[h][:, TOK - 1, :, :], fwd[h][:, TOK - 1, :, :], inject[:, TOK - 1, :, :],
                       ALU.add).then_inc(fwd_step, 1)

                for t in range(1, TOK):
                    steps += [lambda t=t: scale(t), lambda t=t: add(t)]
                return steps + [both_at_end]

            def sum_and_c(k, h):
                unit = 2 * k + h
                steps = []
                count = 0
                for t in reversed(range(TOK)):
                    mine = 0 < t < TOK - 1 and t not in POOL_SUMS
                    if mine:
                        count += 1

                        def both(t=t):
                            wait(dve, bwd_step, BWD * unit + 2 * (TOK - 1 - t))
                            wait(dve, fwd_step, FWD * unit + FWD)
                            tt(fwd[h][:, t, :, :], fwd[h][:, t, :, :], bwd[:, t, :, :], ALU.add).then_inc(c_step, 1)
                        steps.append(both)

                    def times_c(t=t, mine=mine, count=count):
                        if mine:
                            wait(dve, c_step, SC * unit + count)
                        elif t in POOL_SUMS or t == 0:
                            wait(dve, bwd_step, BWD * unit + 15 + (len(POOL_SUMS) - sorted(POOL_SUMS).index(t) if t else 0))
                        else:
                            wait(dve, fwd_step, FWD * unit + FWD)
                            wait(dve, c_copied, 2 * k + 2)
                        tt(fwd[h][:, t, :, :], fwd[h][:, t, :, :],
                           c_rep[:, t, :].unsqueeze(1).to_broadcast([P, TILES, PB]), ALU.mult).then_inc(c_step, 1)
                    steps.append(times_c)
                    count += 1
                assert count == SC
                return steps

            def gate(k):
                wait(dve, y_summed, 4 * k + 4)
                wait(dve, gz_ready, k + 1)
                wait(dve, yo_ready, k)
                tt(yz[:, :], p_y[:, :], gz[:, :], ALU.mult).then_inc(gated, 1)

            def channel_stats(k, i):
                wait(dve, yo_copied, k + 1)
                for h in range(2):
                    nc.vector.bn_stats(stats[:, h, i, :], yo[:, h, :]).then_inc(stat_done, 1)

            def max_item(a, g):
                wait(dve, rows_ready, KG * a + g + 1)
                nc.vector.tensor_reduce(mx8[:, g:g + 1], p_s[:, :], AX.X, ALU.max).then_inc(max_step, 1)

            def max_steps(a):
                def whole():
                    wait(dve, max_step, KG * a + KG)
                    nc.vector.tensor_reduce(nmax[:, :], mx8[:, :], AX.X, ALU.max, negate=True).then_inc(nmax_step, 1)

                def first():
                    wait(dve, nmax_step, 5 * a + 1)
                    nc.vector.tensor_copy(nparts[:, 0:1], nmax[:, :]).then_inc(nmax_step, 1)

                def rest():
                    wait(dve, nmax_step, 5 * a + 2)
                    tt(nres[:, :], nmax[:, :], nparts[:, 0:1], ALU.subtract).then_inc(nmax_step, 1)

                def second():
                    wait(dve, nmax_step, 5 * a + 3)
                    nc.vector.tensor_copy(nparts[:, 1:2], nres[:, :]).then_inc(nmax_step, 1)

                def third():
                    wait(dve, nmax_step, 5 * a + 4)
                    tt(nparts[:, 2:3], nres[:, :], nparts[:, 1:2], ALU.subtract).then_inc(nmax_step, 1)

                return [whole, first, rest, second, third]

            def denominators(a):
                wait(dve, pv_done, KG * a + KG)
                nc.vector.reciprocal(rden[:, 0:1], p_o[:, CH:CH + 1]).then_inc(den_step, 1)
                wait(dve, den_step, 2 * a + 1)
                tt(rden[:, 1:2], rden[:, 0:1], gamma_col[:, :], ALU.mult).then_inc(den_step, 1)

            def add_residual(a):
                wait(dve, o_turned, a + 1)
                wait(dve, x1_in, DMA * (a + 1))
                wait(dve, out_stored, DMA * a)
                tt(o_c[:, :, :], p_s[:, 0:2 * PB].rearrange("p (h x) -> p h x", h=2), x1b[:, :, :],
                   ALU.add).then_inc(o_added, 1)

            def interleave(main, fill, after):
                fill = list(zip(after, fill))
                for n, step in enumerate(main):
                    step()
                    while fill and fill[0][0] <= n + 1:
                        fill.pop(0)[1]()
                for _, step in fill:
                    step()

            def alternate(first, second):
                both = []
                while first or second:
                    both += first[:1] + second[:1]
                    first, second = first[1:], second[1:]
                return both

            def iteration(k, i, head, att):
                items = [lambda n=n: inject_item(k, 0, n) for n in range(8)]
                interleave(items, [lambda g=g: max_item(att, g) for g in range(KG)] if att is not None else [],
                           range(1, KG + 1))
                main = alternate(forward(k, 0), [] if head else sum_and_c(k - 1, 1))
                fill = list(zip((2, 4, 7, 10, 13, 16, 21, 24, 28), softplus_steps(k + 1)))
                if att is not None:
                    fill += list(zip((1, 3, 6, 9, 11), max_steps(att)))
                fill.sort(key=lambda at_step: at_step[0])
                interleave(main, [step for _, step in fill], [at for at, _ in fill])
                if not head:
                    gate(k - 1)
                for n in range(8):
                    inject_item(k, 1, n)
                main = alternate(forward(k, 1), sum_and_c(k, 0))
                interleave(main, [lambda: channel_stats(k - 1, i - 1)] if not head else [], [8])
                if att is not None:
                    denominators(att)
                    add_residual(att)

            def tail(k):
                for step in sum_and_c(k, 1):
                    step()
                gate(k)
                channel_stats(k, BLOCKS - 1)

            def prep(b):
                g0 = 12 * b
                step = [0]

                def chain(ins):
                    ins.then_inc(gn_step, 1)
                    step[0] += 1
                    wait_alone(dve, gn_step, g0 + step[0])

                wait_alone(dve, stat_done, 2 * BLOCKS * (b + 1))
                for h in range(2):
                    chain(nc.vector.bn_aggr(mv[:, h, :], stats[:, h, :, :].rearrange("p n s -> p (n s)")))
                chain(tt(gst[:, :, 1], mv[:, :, 0], mv[:, :, 0], ALU.mult))
                nc.vector.tensor_copy(gst[:, :, 0], mv[:, :, 0])
                chain(tt(gst[:, :, 1], gst[:, :, 1], mv[:, :, 1], ALU.add))
                dve.wait_ge(gn_pe, b + 1)
                chain(nc.vector.tensor_copy(gsum[:, :, :], p_c[:, 0:4].rearrange("p (h s) -> p h s", h=2)))
                chain(tt(gvar[:, :], gsum[:, :, 0], gsum[:, :, 0], ALU.mult))
                chain(tt(gvar[:, :], gsum[:, :, 1], gvar[:, :], ALU.subtract))
                chain(nc.vector.tensor_scalar(gvar[:, :], gvar[:, :], GN_EPS, None, ALU.add))
                dve.wait_ge(gn_act, b + 1)
                chain(nc.vector.reciprocal(gsd[:, :], gsd[:, :]))
                chain(tt(gscale[:, :], gsd[:, :], gnw[:, :], ALU.mult))
                chain(tt(gbias[:, :], gsum[:, :, 0], gscale[:, :], ALU.mult))
                chain(tt(gbias[:, :], gnb[:, :], gbias[:, :], ALU.subtract))
                for pair in chunk_pairs(dve, b):
                    c0 = pair * 2
                    for par in range(2):
                        n_c = b * CHUNKS + c0 + par
                        cols = bass.ds((c0 + par) * CHUNK, CHUNK)
                        dve.wait_ge(chunk_in[par], DMA * (b * CHUNKS + c0) + 2 * DMA)
                        wait(dve, x1_ready, 2 * (b * CHUNKS + c0))
                        for h in range(2):
                            nc.vector.scalar_tensor_tensor(xm[par][:, h, :], yc[par][:, h, :], gscale[:, h:h + 1],
                                                           xc[par][:, h, :], ALU.mult, ALU.add).then_inc(xm_ready, 1)
                        wait(dve, a_done, 2 * n_c + 1)
                        wait(dve, b_done, 2 * n_c)
                        tt(kres, kf, ka[0:96, cols], ALU.subtract).then_inc(kq_res, 1)
                        wait(dve, a_done, 2 * n_c + 2)
                        tt(qres, qf, qac, ALU.subtract).then_inc(kq_res, 1)
                        wait(dve, b_done, 2 * n_c + 1)
                        wait(dve, kq_res, 2 * n_c + 2)
                        nc.vector.tensor_copy(kb[32:64, cols], ka[32:64, cols]).then_inc(kq_parts, 1)
                        nc.vector.tensor_copy(ka[64:96, cols], kb[64:96, cols]).then_inc(kq_parts, 1)
                        wait(dve, kq_parts, 6 * n_c + 2)
                        tt(kb[64:96, cols], kres[64:96, :], kb[64:96, cols], ALU.subtract).then_inc(kq_parts, 1)
                        wait(dve, b_done, 2 * n_c + 2)
                        nc.vector.tensor_copy(qbc[64:96, :], qac[64:96, :]).then_inc(kq_parts, 1)
                        nc.vector.tensor_copy(qac[32:64, :], qbc[32:64, :]).then_inc(kq_parts, 1)
                        wait(dve, kq_parts, 6 * n_c + 5)
                        tt(qbc[32:64, :], qres[32:64, :], qbc[32:64, :], ALU.subtract).then_inc(kq_parts, 1)
                wait_alone(dve, b_done, 2 * CHUNKS * (b + 1))
                wait_alone(dve, q_stored, 2 * DMA * CHUNKS * (b + 1))

            cp = nc.vector.tensor_copy
            dve.wait_ge(consts_in, CONSTS[0])
            dve.wait_ge(setup_pe, 1)
            cp(t_c[0:DIN, 128:128 + GCN], p_c[0:DIN, 0:GCN]).then_inc(setup_dve, 1)
            dve.wait_ge(setup_pe, 2)
            cp(t_c[0:2, 64:128], p_y[0:2, 0:DIN]).then_inc(setup_dve, 1)
            for n in range(2):
                cp(t_c[0:DIN, 384 + n * P:384 + (n + 1) * P].rearrange("p (d n) -> p d n", d=8),
                   t_e[0:DIN, 2 + n * NST:2 + (n + 1) * NST].unsqueeze(1).to_broadcast([DIN, 8, NST]))
            dve.wait_ge(setup_pe, 5)
            last = cp(t_c[0:DIN, 256:256 + DIN], p_delta[0][0:DIN, 0:DIN]).then_inc(setup_dve, 1)
            last = cp(t_c[0:DIN, 256 + DIN:256 + P], p_delta[0][0:DIN, 0:DIN]).then_inc(setup_dve, 1)
            dve.wait_ge(setup_pe, 6)
            cp(w_dbc[:, :, :], p_delta[1][0:GCN, 0:3 * P].rearrange("p (n c) -> p n c", n=3)).then_inc(setup_dve, 1)
            for n in range(2):
                cp(w_u[:, n * DIN:(n + 1) * DIN], w_in[:, 0:DIN]).then_inc(setup_dve, 1)
            nc.vector.tensor_scalar(t_e[0:GCN, 128:192], t_e[0:GCN, 128:192], 2.0, None, ALU.mult).then_inc(setup_dve, 1)
            dve.wait_ge(setup_dve, 8)
            tt(w_skip[:, :], w_in[:, 0:DIN], t_e[0:GCN, 128:192], ALU.mult).then_inc(setup_dve, 1)
            nc.vector.tensor_scalar(b2_col[:, :], b2_col[:, :], 2.0, None, ALU.mult).then_inc(setup_dve, 1)
            dve.wait_ge(setup_act, 1)
            nc.vector.tensor_scalar(a_col[:, :], a_col[:, :], -1.0, None, ALU.mult).then_inc(setup_dve, 1)
            for bank, w in ((p_s, wq_t), (p_o, wk_t)):
                for r in range(3):
                    cp(w[:, :, 32 * r:32 * r + 32], bank[:, 0:64].rearrange("p (h d) -> p h d", h=2)).then_inc(setup_dve, 1)
            for h in range(2):
                cp(wv_t[:, h, :], p_du[h][:, 0:CH]).then_inc(setup_dve, 1)
            cp(identb[:, :], ident[:, :]).then_inc(setup_dve, 1)
            cp(spread[:, :, :], t_r[0:96, 2 * CH:4 * CH].rearrange("p (j x) -> p j x", j=TILES)).then_inc(setup_dve, 1)
            nc.vector.memset(ones_row[:, :], 1.0).then_inc(setup_dve, 1)
            for h in range(2):
                d = slice(DIN * h, DIN * h + DIN)
                other = slice(DIN * (1 - h), DIN * (1 - h) + DIN)
                cp(w_out[d, h, :], t_c[d, 0:GCN]).then_inc(setup_dve, 1)
                nc.vector.memset(w_out[other, h, :], 0.0).then_inc(setup_dve, 1)
            nc.vector.memset(ka[96:99, :], 1.0).then_inc(setup_dve, 1)
            nc.vector.memset(v_t[:, :, CH:CH + 1], 1.0).then_inc(setup_dve, 1)
            dve.wait_ge(setup_dve, 28)
            nc.vector.memset(nres[:, :], 0.0).then_inc(setup_ready, 1)
            for step in softplus_steps(0):
                step()

            def phase(b, att):
                k0 = b * BLOCKS
                for i in range(peeled(b)):
                    iteration(k0 + i, i, i == 0, k0 - BLOCKS + i if att else None)
                with dve.Fori(peeled(b), BLOCKS) as i:
                    iteration(k0 + i, i, False, k0 - BLOCKS + i if att else None)
                tail(k0 + BLOCKS - 1)

            phase(0, False)
            prep(0)
            phase(1, True)
            with dve.Fori(2, IMAGES) as b:
                prep(b - 1)
                phase(b, True)
            prep(IMAGES - 1)
            with dve.Fori(ALL - BLOCKS, ALL) as a:
                for g in range(KG):
                    max_item(a, g)
                for step in max_steps(a):
                    step()
                denominators(a)
                add_residual(a)

        @block.gpsimd
        def _(pool):
            tt = nc.gpsimd.tensor_tensor

            def backward(k, h):
                unit = 2 * k + h
                for t in reversed(range(TOK - 1)):
                    n = BWD * unit + 2 * (TOK - 2 - t)
                    if t == TOK - 2:
                        wait(pool, decay_ready, 8 * unit + 4)
                        wait(pool, inject_ready, 8 * unit + 4)
                    if t == HT - 1:
                        wait(pool, decay_ready, 8 * unit + 8)
                        wait(pool, inject_ready, 8 * unit + 8)
                    later = inject[:, TOK - 1, :, :] if t == TOK - 2 else bwd[:, t + 1, :, :]
                    if 0 < t and t not in POOL_SUMS:
                        wait(pool, c_step, SC * (unit - 1) + c_count(TOK - t) - 1)
                    wait(pool, bwd_step, n)
                    tt(bwd[:, t, :, :], decay[h][:, t, :, :], later, ALU.mult).then_inc(bwd_step, 1)
                    pool.wait_ge(bwd_step, n + 1)
                    tt(bwd[:, t, :, :], bwd[:, t, :, :], inject[:, t, :, :], ALU.add).then_inc(bwd_step, 1)
                pool.wait_ge(bwd_step, BWD * unit + 14)
                wait(pool, y_summed, 2 * (unit - 1))
                tt(fwd[h][:, 0, :, :], bwd[:, 0, :, :], inject[:, 0, :, :], ALU.add).then_inc(bwd_step, 1)
                pool.wait_ge(fwd_step, FWD * unit + FWD)
                for t in sorted(POOL_SUMS, reverse=True):
                    tt(fwd[h][:, t, :, :], fwd[h][:, t, :, :], bwd[:, t, :, :], ALU.add).then_inc(bwd_step, 1)

            pool.wait_ge(setup_ready, 1)
            for h in range(2):
                backward(0, h)
            with pool.Fori(1, ALL) as k:
                for h in range(2):
                    backward(k, h)


def constants():
    spread = np.zeros((96, TILES, P), np.float32)
    for part in range(3):
        for j in range(TILES):
            for d in range(8):
                spread[32 * part + 8 * j + d, j, NST * d:NST * d + NST] = 1
    total = np.zeros((P, 2 * TILES, DIN), np.float32)
    for j in range(2 * TILES):
        for d in range(8):
            total[NST * d:NST * d + NST, j, 8 * j + d] = 1
    group = np.zeros((P, P), np.float32)
    for g in range(2):
        group[64 * g:64 * g + 64, 64 * g:64 * g + 64] = 1 / 64
    return {"ident": np.eye(P, dtype=np.float32), "spread": spread, "sum": total, "group": group}


_INS = ["x", "L0_conv_W_in", "L0_conv_W_x", "L0_conv_W_dt", "L0_conv_b_dt", "L0_conv_A_logs", "L0_conv_Ds",
        "L0_conv_W_out", "L0_conv_gn_w", "L0_conv_gn_b", "L1_conv_Wq", "L1_conv_bq", "L1_conv_Wk", "L1_conv_bk",
        "L1_conv_Wv", "L1_conv_bv", "L1_conv_gamma"]


def kernel(**inputs):
    import concourse.bacc as bacc
    from concourse.bass_utils import run_bass_kernel_spmd

    nc = bacc.Bacc("TRN2", target_bir_lowering=False, num_devices=1, dynamic_dma_scratch_size=1024)
    arrays, args = {}, []
    data = [(name, np.ascontiguousarray(np.atleast_1d(inputs[name]))) for name in _INS]
    for name, a in data + list(constants().items()):
        arrays[f"in_{name}"] = a
        args.append(nc.dram_tensor(f"in_{name}", a.shape, mybir.dt.from_np(a.dtype), kind="ExternalInput").ap())
    out = nc.dram_tensor("out", (IMAGES, CH, 64, 64), F32, kind="ExternalOutput").ap()
    build(nc, *args, out)
    r = run_bass_kernel_spmd(nc, [arrays], core_ids=[0])
    return r.results[0]["out"]
```

```python
import numpy as np
from contextlib import ExitStack

import concourse.bass as bass
from concourse import mybir

F32 = mybir.dt.float32
BF16 = mybir.dt.bfloat16
ALU = mybir.AluOpType
ACT = mybir.ActivationFunctionType
AX = mybir.AxisListType

P = 128
IMAGES, CH, PIX = 4, 256, 64 * 64
TOK, GCN, DIN, NST = 8, 32, 64, 16
PB = 128
BLOCKS = PIX // PB
ALL = IMAGES * BLOCKS
TILES = 4
HT = TOK // 2
BANK = 512
KG = PIX // BANK
CHUNK = 512
CHUNKS = PIX // CHUNK
VC = CH + 1
GN_EPS = 1e-5
POOL_SUMS = (1, 2, 3, 4, 5)
FWD, BWD = 15, 15 + len(POOL_SUMS)
SC = TOK + (TOK - 2 - len(POOL_SUMS))
DMA = 16


def wait(eng, sem, value):
    if isinstance(value, int) and value <= 0:
        return
    assert isinstance(value, int) or value.min_val > 0
    eng.wait_ge(sem, value)


def build(nc, x, W_in, W_x, W_dt, b_dt, A_logs, Ds, W_out, gn_w, gn_b, Wq, bq, Wk, bk, Wv, bv, gamma,
          ident_in, spread_in, sum_in, group_in, out):
    ctx = ExitStack()
    with ctx:
        def sb(name, shape, dt=F32):
            return ctx.enter_context(nc.sbuf_tensor(name, shape, dt))

        def ps(name, shape, dt=F32):
            return ctx.enter_context(nc.psum_tensor(name, shape, dt))

        def sem(name):
            return ctx.enter_context(nc.semaphore(name))

        x_v = x.rearrange("b (h p) y z -> b p h (y z)", p=P)
        x_tok = x.rearrange("b (t g) y z -> b g t (y z)", g=GCN)
        out_v = out.rearrange("b (h p) y z -> b p h (y z)", p=P)
        y_dram = nc.dram_tensor("y_scratch", (P, 2, PIX), F32, kind="Internal").ap()
        x1_dram = nc.dram_tensor("x1_scratch", (P, 2, PIX), F32, kind="Internal").ap()
        qa_dram = nc.dram_tensor("qa_scratch", (96, PIX), BF16, kind="Internal").ap()
        qb_dram = nc.dram_tensor("qb_scratch", (96, PIX), BF16, kind="Internal").ap()

        ident = sb("ident", [P, P])
        identb = sb("identb", [P, P], BF16)
        spread = sb("spread", [96, TILES, P], BF16)
        statesum = sb("statesum", [P, 2 * TILES, DIN])
        groupmean = sb("groupmean", [P, P])
        w_in = sb("w_in", [GCN, 2 * DIN])
        w_out_raw = sb("w_out_raw", [P, GCN])
        w_skip = sb("w_skip", [GCN, DIN])
        w_dbc = sb("w_dbc", [GCN, 3, P])
        w_out = sb("w_out", [P, 2, GCN])
        a_col = sb("a_col", [P, 2 * TILES])
        b2_col = sb("b2_col", [P, 1])
        gnw = sb("gnw", [P, 2])
        gnb = sb("gnb", [P, 2])
        wq_t = sb("wq_t", [P, 2, 96])
        wk_t = sb("wk_t", [P, 2, 96])
        wv_t = sb("wv_t", [P, 2, CH])
        bq_col = sb("bq_col", [96, 1])
        bk_col = sb("bk_col", [96, 1])
        bv_row = sb("bv_row", [1, CH])
        ones_row = sb("ones_row", [1, P])
        gamma_col = sb("gamma_col", [P, 1])

        xa = sb("xa", [GCN, TOK, PB])
        xb = sb("xb", [GCN, TOK, PB])
        t_e = sb("t_e", [P, HT * PB])
        t_r = sb("t_r", [P, HT * PB])
        t_l = sb("t_l", [P, HT * PB])
        t_c = sb("t_c", [P, HT * PB])
        t_d = sb("t_d", [P, 2, HT * PB])
        t_rest = sb("t_rest", [P, 2, HT * PB])
        top = sb("top", [P, 2, HT * PB], BF16)
        mid = sb("mid", [P, 2, HT * PB], BF16)
        low = sb("low", [P, 2, HT * PB], BF16)
        parts = [sb(f"parts{h}", [96, 2, TOK * PB], BF16) for h in range(2)]
        b_rep = sb("b_rep", [P, TOK, PB])
        c_rep = sb("c_rep", [P, TOK, PB])
        decay = [sb(f"decay{h}", [P, TOK, TILES, PB]) for h in range(2)]
        inject = sb("inject", [P, TOK, TILES, PB])
        fwd = [sb(f"fwd{h}", [P, TOK, TILES, PB]) for h in range(2)]
        bwd = sb("bwd", [P, TOK, TILES, PB])
        gz = sb("gz", [P, HT * PB])
        yz = sb("yz", [P, HT * PB])
        yo = sb("yo", [P, 2, PB])
        stats = sb("stats", [P, 2, BLOCKS, 6])
        mv = sb("mv", [P, 2, 2])
        gst = sb("gst", [P, 2, 2])
        gsum = sb("gsum", [P, 2, 2])
        gvar = sb("gvar", [P, 2])
        gsd = sb("gsd", [P, 2])
        gscale = sb("gscale", [P, 2])
        gbias = sb("gbias", [P, 2])
        ka = sb("ka", [99, PIX], BF16)
        kb = sb("kb", [96, PIX], BF16)
        v_t = sb("v_t", [P, PIX // P, VC])
        qa = [sb(f"qa{i}", [99, PB], BF16) for i in range(2)]
        qb = [sb(f"qb{i}", [96, PB], BF16) for i in range(2)]
        x1b = sb("x1b", [P, 2, PB])
        prob = [sb(f"prob{i}", [P, BANK]) for i in range(2)]
        mx8 = sb("mx8", [P, KG])
        nmax = sb("nmax", [P, 1])
        nres = sb("nres", [P, 1])
        nparts = sb("nparts", [P, 3], BF16)
        rden = sb("rden", [P, 2])
        o_n = sb("o_n", [P, CH])
        o_c = sb("o_c", [P, 2, PB])

        d0 = inject[:, :, :, :].rearrange("p t j x -> p (t j x)")
        d1 = decay[1][:, :, :, :].rearrange("p t j x -> p (t j x)")
        f0 = fwd[0][:, :, :, :].rearrange("p t j x -> p (t j x)")
        s_small, s_qk, s_v, s_mid = (f0[:, i * 1024:(i + 1) * 1024] for i in range(4))

        def halves(ap):
            return ap.rearrange("p (h x) -> p h x", h=2)

        yc = [halves(d0[:, i * 1024:(i + 1) * 1024]) for i in range(2)]
        xc = [halves(d0[:, (2 + i) * 1024:(3 + i) * 1024]) for i in range(2)]
        xm = [halves(d1[:, i * 1024:(i + 1) * 1024]) for i in range(2)]
        x1c = [halves(d1[:, (2 + i) * 1024:(3 + i) * 1024]) for i in range(2)]
        kf = f0[0:96, 0:CHUNK]
        qf = f0[0:96, CHUNK:2 * CHUNK]
        kres = f0[0:96, 2 * CHUNK:3 * CHUNK]
        qres = f0[0:96, 3 * CHUNK:4 * CHUNK]
        qac = fwd[1][0:96, 0, 0:2, :].rearrange("p j x -> p (j x)").bitcast(BF16)
        qbc = fwd[1][0:96, 0, 2:4, :].rearrange("p j x -> p (j x)").bitcast(BF16)

        p_delta = [ps(f"p_delta{i}", [P, BANK]) for i in range(2)]
        p_du = [ps(f"p_du{i}", [P, BANK]) for i in range(2)]
        p_c = ps("p_c", [P, BANK])
        p_y = ps("p_y", [P, BANK])
        p_s = ps("p_s", [P, BANK])
        p_o = ps("p_o", [P, BANK])

        consts_in = sem("consts_in")
        setup_pe, setup_dve, setup_act, setup_ready = sem("setup_pe"), sem("setup_dve"), sem("setup_act"), sem("setup_ready")
        xa_in, xb_in = sem("xa_in"), sem("xb_in")
        dts_ready, u_ready, b_ready, c_ready, z_ready, yo_ready = map(
            sem, ("dts_ready", "u_ready", "b_ready", "c_ready", "z_ready", "yo_ready"))
        abs_relu, e_ready, ln_ready, square_ready, top_ready, mid_ready = map(
            sem, ("abs_relu", "e_ready", "ln_ready", "square_ready", "top_ready", "mid_ready"))
        sp_step, du_ready, res_ready, low_ready = map(sem, ("sp_step", "du_ready", "res_ready", "low_ready"))
        parts_in = [sem(f"parts_in{h}") for h in range(2)]
        b_copied, c_copied, gz_ready, yo_copied = map(sem, ("b_copied", "c_copied", "gz_ready", "yo_copied"))
        delta_spread, du_spread, decay_ready, inject_ready = map(
            sem, ("delta_spread", "du_spread", "decay_ready", "inject_ready"))
        fwd_step, bwd_step, c_step, y_summed, skip_done, gated, stat_done, y_stored = map(
            sem, ("fwd_step", "bwd_step", "c_step", "y_summed", "skip_done", "gated", "stat_done", "y_stored"))
        gn_step, gn_pe, gn_act = sem("gn_step"), sem("gn_pe"), sem("gn_act")
        chunk_in = [sem(f"chunk_in{i}") for i in range(2)]
        xm_ready, x1_ready, kq_ready, v_ready, kq_copied, v_copied = map(
            sem, ("xm_ready", "x1_ready", "kq_ready", "v_ready", "kq_copied", "v_copied"))
        a_done, kq_res, b_done, kq_parts, x1_stored, q_stored = map(
            sem, ("a_done", "kq_res", "b_done", "kq_parts", "x1_stored", "q_stored"))
        q_in, x1_in = sem("q_in"), sem("x1_in")
        rows_ready, max_step, nmax_step, nmax_t, nmax_in = map(
            sem, ("rows_ready", "max_step", "nmax_step", "nmax_t", "nmax_in"))
        cols_ready, prob_ready, pv_done, den_step, o_norm, o_turned, o_added, out_stored = map(
            sem, ("cols_ready", "prob_ready", "pv_done", "den_step", "o_norm", "o_turned", "o_added", "out_stored"))

        passed = {e.engine: sem(f"passed_{n}") for n, e in (("sp", nc.sync), ("pe", nc.tensor), ("act", nc.scalar), ("dve", nc.vector))}
        CONSTS = [0]

        def peeled(b):
            return 2 if isinstance(b, int) and b == 0 else 1

        def chunk_pairs(eng, b):
            if isinstance(b, int) and b == 0:
                yield 0
                with eng.Fori(1, CHUNKS // 2) as pair:
                    yield pair
            else:
                with eng.Fori(0, CHUNKS // 2) as pair:
                    yield pair

        def c_count(tokens):
            return sum(1 + (t not in POOL_SUMS and 0 < t < TOK - 1) for t in range(TOK - tokens, TOK))

        def wait_alone(eng, sem, value):
            wait(eng, sem, value)
            if not isinstance(value, int):
                eng.sem_inc(passed[eng.engine], 1)

        block = ctx.enter_context(nc.Block())

        @block.sync
        def _(sp):
            n = 0
            src_dst = [(ident[:, :], ident_in), (groupmean[:, :], group_in),
                       (s_qk[0:96, 2 * CH:4 * CH].rearrange("p (j x) -> p j x", j=TILES), spread_in), (statesum[:, :, :], sum_in)]
            src_dst.append((w_in[:, :], W_in))
            for r in range(2):
                src_dst.append((w_out_raw[DIN * r:DIN * r + DIN, :], W_out))
                src_dst.append((b2_col[DIN * r:DIN * r + DIN, :], b_dt.rearrange("(d o) -> d o", o=1)))
            for r in range(3):
                src_dst.append((bq_col[32 * r:32 * r + 32, :], bq.rearrange("(d o) -> d o", o=1)))
                src_dst.append((bk_col[32 * r:32 * r + 32, :], bk.rearrange("(d o) -> d o", o=1)))
            src_dst += [
                (s_small[0:DIN, 0:34], W_x), (s_small[0:2, 64:128], W_dt),
                (s_small[0:GCN, 128:192], Ds.rearrange("(o d) -> o d", o=1).to_broadcast([GCN, DIN])),
                (s_qk[0:32, 0:CH], Wq), (s_qk[0:32, CH:2 * CH], Wk),
                (s_v[:, 0:CH], Wv[0:P, :]), (s_v[:, CH:2 * CH], Wv[P:2 * P, :]),
                (bv_row[:, :], bv.rearrange("(o d) -> o d", o=1)),
                (gamma_col[:, :], gamma.rearrange("(o d) -> o d", o=1).to_broadcast([P, 1])),
            ]
            for dst, src in src_dst:
                sp.dma_start(dst, src).then_inc(consts_in, DMA)
                n += 1
            with nc.allow_non_contiguous_dma(reason="small parameters, once"):
                sp.dma_start(a_col[:, :], A_logs.rearrange("(j d) n -> (d n) j", d=8)).then_inc(consts_in, DMA)
                sp.dma_start(gnw[:, :], gn_w.rearrange("(h p) -> p h", p=P)).then_inc(consts_in, DMA)
                sp.dma_start(gnb[:, :], gn_b.rearrange("(h p) -> p h", p=P)).then_inc(consts_in, DMA)
            CONSTS[0] = (n + 3) * DMA

            def load_xa(b, i):
                sp.dma_start(xa[:, :, :], x_tok[b, :, :, bass.ds(i * PB, PB)]).then_inc(xa_in, DMA)

            def load_q(a, i, images, buf=0, used_by=0):
                wait_alone(sp, q_stored, images * CHUNKS * 2 * DMA)
                wait_alone(sp, cols_ready, KG * (a - used_by))
                sp.dma_start(qa[buf][0:96, :], qa_dram[:, bass.ds(i * PB, PB)]).then_inc(q_in, DMA)
                sp.dma_start(qb[buf][:, :], qb_dram[:, bass.ds(i * PB, PB)]).then_inc(q_in, DMA)

            def load_x1(a, i, images):
                wait_alone(sp, x1_stored, images * CHUNKS * DMA)
                wait_alone(sp, o_added, a)
                sp.dma_start(x1b[:, :, :], x1_dram[:, :, bass.ds(i * PB, PB)]).then_inc(x1_in, DMA)

            def move_parts(k, h):
                for n, (part, ready) in enumerate(((top, top_ready), (mid, mid_ready), (low, low_ready))):
                    wait_alone(sp, ready, k + 1)
                    if n == 0:
                        wait_alone(sp, delta_spread, 16 * k - 8 * (1 - h))
                        wait_alone(sp, du_spread, 16 * k - 8 * (1 - h))
                    for th in range(2):
                        r = DIN * th + 32 * h
                        sp.dma_start(parts[h][32 * n:32 * n + 32, :, th * BANK:(th + 1) * BANK],
                                     part[r:r + 32, :, :]).then_inc(parts_in[h], DMA)

            def store_y(k, i):
                wait_alone(sp, yo_copied, k + 1)
                sp.dma_start(y_dram[:, :, bass.ds(i * PB, PB)], yo[:, :, :]).then_inc(y_stored, DMA)

            def store_out(a, b, i):
                wait_alone(sp, o_added, a + 1)
                sp.dma_start(out_v[b, :, :, bass.ds(i * PB, PB)], o_c[:, :, :]).then_inc(out_stored, DMA)

            def load_xb(k, b, i):
                wait_alone(sp, skip_done, k)
                wait_alone(sp, z_ready, k)
                sp.dma_start(xb[:, :, :], x_tok[b, :, :, bass.ds(i * PB, PB)]).then_inc(xb_in, DMA)

            def next_xa(k, b, i):
                wait_alone(sp, b_ready, 2 * k + 2)
                load_xa(b, i)

            def iteration(k, b, i, head, att, load_next):
                if att:
                    load_x1(att[0], att[2], b)
                move_parts(k + 1, 0)
                if att and not (isinstance(i, int) and i == BLOCKS - 1):
                    load_q(att[0] + 1, att[2] + 1, b)
                move_parts(k + 1, 1)
                if att:
                    store_out(*att)
                if not head:
                    store_y(k - 1, i - 1)
                load_next()

            def phase(b, att):
                k0 = b * BLOCKS
                a0 = k0 - BLOCKS

                def block(i, load_next):
                    iteration(k0 + i, b, i, isinstance(i, int) and i == 0, (a0 + i, b - 1, i) if att else None, load_next)

                def next_here(i):
                    next_xa(k0 + i + 1, b, i + 2)
                    load_xb(k0 + i + 1, b, i + 1)

                if att:
                    load_q(a0, 0, b)
                for i in range(peeled(b)):
                    block(i, lambda: next_here(i))
                with sp.Fori(peeled(b), BLOCKS - 2) as i:
                    block(i, lambda: next_here(i))
                i = BLOCKS - 2
                block(i, lambda: (next_xa(k0 + i + 1, clamp(b), 0), load_xb(k0 + i + 1, b, i + 1)))
                i = BLOCKS - 1
                block(i, lambda: (next_xa(k0 + i + 1, clamp(b), 1), load_xb(k0 + i + 1, clamp(b), 0)))
                store_y(k0 + BLOCKS - 1, BLOCKS - 1)

            def clamp(b):
                return min(b + 1, IMAGES - 1) if isinstance(b, int) else b + 1

            def prep(b):
                k_end = BLOCKS * (b + 1)
                wait_alone(sp, y_stored, DMA * k_end)
                for pair in chunk_pairs(sp, b):
                    c0 = pair * 2
                    for par in range(2):
                        c = c0 + par
                        n_c = b * CHUNKS + c0
                        wait_alone(sp, xm_ready, 2 * n_c) if par == 0 else None
                        cols = bass.ds(c * CHUNK, CHUNK)
                        sp.dma_start(yc[par], y_dram[:, :, cols]).then_inc(chunk_in[par], DMA)
                        sp.dma_start(xc[par], x_v[b, :, :, cols]).then_inc(chunk_in[par], DMA)
                    for par in range(2):
                        c = c0 + par
                        n_c = b * CHUNKS + c
                        cols = bass.ds(c * CHUNK, CHUNK)
                        wait_alone(sp, x1_ready, 2 * n_c + 2)
                        sp.dma_start(x1_dram[:, :, cols], x1c[par]).then_inc(x1_stored, DMA)
                        wait_alone(sp, kq_parts, 6 * n_c + 6)
                        sp.dma_start(qa_dram[:, cols], qac).then_inc(q_stored, DMA)
                        sp.dma_start(qb_dram[:, cols], qbc).then_inc(q_stored, DMA)

            def alone_step(a, i, par):
                wait_alone(sp, q_in, 2 * DMA * (a + 1))
                load_q(a + 1, i + 1, IMAGES, 1 - par, used_by=1)
                store_out(a, IMAGES - 1, i)
                load_x1(a + 1, i + 1, IMAGES)

            load_xa(0, 0)
            sp.dma_start(xb[:, :, :], x_tok[0, :, :, 0:PB]).then_inc(xb_in, DMA)
            wait_alone(sp, setup_ready, 1)
            for h in range(2):
                move_parts(0, h)
            wait_alone(sp, b_ready, 2)
            load_xa(0, 1)
            phase(0, False)
            prep(0)
            phase(1, True)
            with sp.Fori(2, IMAGES - 1) as b:
                prep(b - 1)
                phase(b, True)
            prep(IMAGES - 2)
            phase(IMAGES - 1, True)
            prep(IMAGES - 1)
            last = ALL - BLOCKS
            load_q(last, 0, IMAGES)
            load_x1(last, 0, IMAGES)
            for par in range(2):
                alone_step(last + par, par, par)
            with sp.Fori(1, BLOCKS // 2 - 1) as pair:
                for par in range(2):
                    alone_step(last + pair * 2 + par, pair * 2 + par, par)
            alone_step(ALL - 2, BLOCKS - 2, 0)
            store_out(ALL - 1, IMAGES - 1, BLOCKS - 1)
            sp.wait_ge(out_stored, DMA * ALL)
            sp.wait_ge(y_stored, DMA * ALL)
            sp.wait_ge(x1_stored, DMA * IMAGES * CHUNKS)
            sp.wait_ge(q_stored, 2 * DMA * IMAGES * CHUNKS)
            sp.wait_ge(xa_in, DMA * (ALL + 2))
            sp.wait_ge(xb_in, DMA * (ALL + 1))
            for h in range(2):
                sp.wait_ge(parts_in[h], 6 * DMA * (ALL + 1))

        @block.tensor
        def _(pe):
            mm = pe.matmul

            def project(dst, weights, xt, tokens, done):
                for n, t in enumerate(tokens):
                    last = mm(dst[:, n * PB:(n + 1) * PB], weights, xt[:, t, :], start=True, stop=True)
                last.then_inc(done, 1)

            def project_halves(dst, weights, xt, done, **flags):
                flags = flags or dict(start=True, stop=True)
                for t in range(TOK):
                    h = t // HT
                    last = mm(dst[DIN * h:DIN * h + DIN, (t % HT) * PB:(t % HT + 1) * PB], weights, xt[:, t, :], **flags)
                last.then_inc(done, 1)

            def dts(k):
                wait(pe, xa_in, DMA * (k + 1))
                project_halves(p_c, w_dbc[:, 0, 0:DIN], xa, dts_ready)

            def u(k):
                pe.wait_ge(abs_relu, 2 * k + 2)
                project_halves(p_c, w_in[:, 0:DIN], xa, u_ready)

            def b_states(k, th):
                wait(pe, b_copied, 2 * k + th)
                project(p_c, w_dbc[:, 1, :], xa, range(HT * th, HT * th + HT), b_ready)

            def c_states(k, th):
                wait(pe, xb_in, DMA * (k + 1))
                pe.wait_ge(du_ready, k + 2)
                wait(pe, c_copied, 2 * k + th)
                project(p_c, w_dbc[:, 2, :], xb, range(HT * th, HT * th + HT), c_ready)

            def z_gate(k):
                pe.wait_ge(b_copied, 2 * (k + 1) + 2)
                project_halves(p_c, w_in[:, DIN:2 * DIN], xb, z_ready)

            def y_out(k):
                wait_alone(pe, gated, k + 1)
                for t in range(TOK):
                    r, h = 32 * (t % HT), t // HT
                    last = mm(p_c[r:r + 32, h * PB:(h + 1) * PB], w_out[:, h, :],
                              yz[:, (t % HT) * PB:(t % HT + 1) * PB], start=True, stop=True)
                last.then_inc(yo_ready, 1)

            def spread_delta(k, h, i):
                n = 16 * k + 8 * h + i
                th, j = 1 - i // TILES, i % TILES
                if i == 0:
                    wait(pe, parts_in[h], 6 * DMA * (k + 1))
                wait(pe, decay_ready, n - 1)
                mm(p_delta[i % 2][:, :], spread[:, j, :], parts[h][:, 0, th * BANK:(th + 1) * BANK],
                   start=True, stop=True).then_inc(delta_spread, 1)

            def spread_du(k, h, i):
                n = 16 * k + 8 * h + i
                th, j = 1 - i // TILES, i % TILES
                if i == 0:
                    wait(pe, parts_in[h], 6 * DMA * (k + 1))
                wait(pe, inject_ready, n - 1)
                mm(p_du[i % 2][:, :], spread[:, j, :], parts[h][:, 1, th * BANK:(th + 1) * BANK],
                   start=True, stop=True).then_inc(du_spread, 1)

            def sum_states(k, h, th):
                unit = 2 * k + h
                if h == 0:
                    wait(pe, gated, k)
                wait(pe, c_step, SC * unit + (SC if th == 0 else c_count(HT)))
                region = p_y[DIN * th:DIN * th + DIN, :]
                for j in range(TILES):
                    last = mm(region, statesum[:, TILES * h + j, :], fwd[h][:, HT * th:HT * th + HT, j, :],
                              start=(h == 0 and j == 0), stop=(h == 1 and j == TILES - 1))
                last.then_inc(y_summed, 1)

            def skip_term(k):
                project_halves(p_y, w_skip[:, :], xb, skip_done, start=False, stop=False, skip_group_check=True)

            def key_rows(a, g, bank=p_s, buf=0, free=None):
                if g == 0:
                    wait(pe, q_in, 2 * DMA * (a + 1))
                if g == 0 and bank is p_s:
                    wait(pe, o_added, a)
                wait(pe, max_step, KG * a + g if free is None else free)
                cols = slice(g * BANK, (g + 1) * BANK)
                mm(bank[:, :], qa[buf][0:96, :], ka[0:96, cols], start=True, stop=False)
                mm(bank[:, :], qb[buf][:, :], kb[:, cols], start=False, stop=True).then_inc(rows_ready, 1)

            def turn_max(a, bank=p_s):
                pe.wait_ge(nmax_step, 5 * a + 5)
                pe.wait_ge(max_step, KG * a + KG)
                pe.transpose(bank[0:3, 0:PB // 2].bitcast(BF16), nparts[:, :], identb[:, :]).then_inc(nmax_t, 1)

            def key_cols(a, g, buf=0):
                pe.wait_ge(nmax_in, a + 1)
                wait(pe, prob_ready, KG * a + g)
                for m in range(4):
                    keys = slice(g * BANK + m * P, g * BANK + (m + 1) * P)
                    region = p_s[:, m * PB:(m + 1) * PB]
                    mm(region, ka[:, keys], qa[buf][:, :], start=True, stop=False)
                    last = mm(region, kb[:, keys], qb[buf][:, :], start=False, stop=True)
                last.then_inc(cols_ready, 1)

            def value_product(a, g, m):
                if g == 0 and m == 0:
                    wait(pe, o_norm, a)
                if m == 0:
                    pe.wait_ge(prob_ready, KG * a + g + 1)
                last = mm(p_o[:, 0:VC], prob[g % 2][:, m * PB:(m + 1) * PB], v_t[:, 4 * g + m, :],
                          start=(g == 0 and m == 0), stop=(g == KG - 1 and m == 3))
                if m == 3:
                    last.then_inc(pv_done, 1)

            def values(a, g):
                for m in range(4):
                    value_product(a, g, m)

            def turn_out(a, bank=p_s):
                pe.wait_ge(o_norm, a + 1)
                if bank is not p_s:
                    wait(pe, o_added, a)
                for h in range(2):
                    last = pe.transpose(bank[:, h * PB:(h + 1) * PB], o_n[:, h * P:(h + 1) * P], ident[:, :])
                last.then_inc(o_turned, 1)

            def iteration(k, head, att, rows):
                has = att is not None
                if head:
                    wait(pe, yo_copied, k)
                wait(pe, gz_ready, k)
                pe.wait_ge(b_copied, 2 * k + 2)
                spread_du(k, 0, 0)
                spread_du(k, 0, 1)
                dts(k + 1)
                pieces = []
                if has:
                    pieces = [lambda: key_cols(att, 0), lambda: key_cols(att, 1)]
                    pieces += [lambda m=m: value_product(att, 0, m) for m in range(4)]
                for i in range(2, 8):
                    spread_du(k, 0, i)
                    if pieces:
                        pieces.pop(0)()
                for j in range(8):
                    spread_delta(k, 1, j)
                    if has and j:
                        if j + 1 < KG:
                            key_cols(att, j + 1)
                        values(att, j)
                    if j == 1:
                        u(k + 1)
                    if j == 4 and not head:
                        sum_states(k - 1, 1, 1)
                    if j == 5:
                        c_states(k, 0)
                if not head:
                    sum_states(k - 1, 1, 0)
                c_states(k, 1)
                for i in range(8):
                    spread_du(k, 1, i)
                    if i == 3 and has:
                        turn_out(att)
                    if i == 5 and not head:
                        pe.wait_ge(c_copied, 2 * k + 2)
                        y_out(k - 1)
                if head:
                    pe.wait_ge(c_copied, 2 * k + 2)
                else:
                    wait(pe, yo_copied, k)
                for j in range(8):
                    if rows:
                        key_rows(att + 1, j)
                    if j == 0:
                        b_states(k + 1, 0)
                    if j == 1:
                        b_states(k + 1, 1)
                    if j == 2:
                        z_gate(k)
                    if j >= 2:
                        spread_delta(k + 1, 0, j - 2)
                    if j == 5:
                        sum_states(k, 0, 1)
                spread_delta(k + 1, 0, 6)
                spread_delta(k + 1, 0, 7)
                sum_states(k, 0, 0)
                if rows:
                    turn_max(att + 1)
                skip_term(k)

            def tail(k):
                sum_states(k, 1, 1)
                sum_states(k, 1, 0)
                pe.wait_ge(gz_ready, k + 1)
                y_out(k)

            def prep(b):
                pe.wait_ge(gn_step, 12 * b + 4)
                wait(pe, yo_copied, BLOCKS * (b + 1))
                mm(p_c[:, 0:4], groupmean[:, :], gst[:, :, :].rearrange("p a c -> p (a c)"),
                   start=True, stop=True).then_inc(gn_pe, 1)
                for pair in chunk_pairs(pe, b):
                    c0 = pair * 2
                    for par in range(2):
                        n_c = b * CHUNKS + c0 + par
                        pe.wait_ge(x1_ready, 2 * n_c + 2)
                        wait(pe, kq_copied, 2 * n_c)
                        pe.wait_ge(decay_ready, 16 * BLOCKS * (b + 1) + 8)
                        for bank, w in ((p_delta[0], wk_t), (p_delta[1], wq_t)):
                            for h in range(2):
                                last = mm(bank[0:96, :], w[:, h, :], x1c[par][:, h, :], start=(h == 0), stop=(h == 1))
                            last.then_inc(kq_ready, 1)
                        wait(pe, v_copied, 2 * n_c)
                        for m in range(4):
                            region = p_du[m // 2][:, (m % 2) * CH:(m % 2 + 1) * CH]
                            for h in range(2):
                                mm(region, x1c[par][:, h, m * P:(m + 1) * P], wv_t[:, h, :], start=(h == 0), stop=False)
                            last = mm(region, ones_row[:, :], bv_row[:, :], start=False, stop=True)
                            if m % 2:
                                last.then_inc(v_ready, 1)
                wait_alone(pe, kq_copied, 2 * CHUNKS * (b + 1))
                wait_alone(pe, v_copied, 2 * CHUNKS * (b + 1))

            pe.wait_ge(consts_in, CONSTS[0])
            pe.transpose(p_c[0:DIN, 0:GCN], w_in[:, 0:DIN], ident[0:GCN, 0:GCN]).then_inc(setup_pe, 1)
            pe.transpose(p_y[0:2, 0:DIN], s_small[0:DIN, 0:2], ident[0:DIN, 0:DIN]).then_inc(setup_pe, 1)
            for n, bank in ((0, p_s), (1, p_o)):
                for h in range(2):
                    last = pe.transpose(bank[:, h * 32:(h + 1) * 32], s_qk[0:32, n * CH + h * P:n * CH + (h + 1) * P],
                                        ident[0:32, 0:32])
            last.then_inc(setup_pe, 1)
            for h in range(2):
                for c in range(2):
                    last = pe.transpose(p_du[h][:, c * P:(c + 1) * P], s_v[:, c * CH + h * P:c * CH + (h + 1) * P],
                                        ident[:, :])
            last.then_inc(setup_pe, 1)
            pe.wait_ge(setup_dve, 2)
            mm(p_delta[0][0:DIN, 0:DIN], s_mid[0:2, 64:128], s_small[0:2, 64:128], start=True, stop=True).then_inc(setup_pe, 1)
            pe.wait_ge(setup_dve, 4)
            mm(p_delta[1][0:GCN, 0:3 * P], s_mid[0:DIN, 128:128 + GCN], s_mid[0:DIN, 256:640], start=True, stop=True).then_inc(setup_pe, 1)
            pe.wait_ge(setup_ready, 1)
            dts(0)
            u(0)
            pe.wait_ge(du_ready, 1)
            b_states(0, 0)
            b_states(0, 1)
            for i in range(8):
                spread_delta(0, 0, i)

            def first_rows(a):
                for g in range(KG):
                    key_rows(a, g)
                turn_max(a)

            def phase(b, att):
                k0 = b * BLOCKS
                if att:
                    first_rows(k0 - BLOCKS)
                for i in range(peeled(b)):
                    iteration(k0 + i, i == 0, k0 - BLOCKS + i if att else None, att)
                with pe.Fori(peeled(b), BLOCKS - 1) as i:
                    iteration(k0 + i, False, k0 - BLOCKS + i if att else None, att)
                iteration(k0 + BLOCKS - 1, False, k0 - 1 if att else None, False)
                tail(k0 + BLOCKS - 1)

            def alone(a, par, rows):
                key_cols(a, 0, par)
                for g in range(KG):
                    if rows:
                        key_rows(a + 1, g, p_delta[g % 2], 1 - par, KG * (a + 1) + max(g - 1, 0))
                    if g + 1 < KG:
                        key_cols(a, g + 1, par)
                    values(a, g)
                if rows:
                    turn_max(a + 1, p_y)
                turn_out(a, p_du[0])

            phase(0, False)
            prep(0)
            phase(1, True)
            with pe.Fori(2, IMAGES) as b:
                prep(b - 1)
                phase(b, True)
            prep(IMAGES - 1)
            first_rows(ALL - BLOCKS)
            with pe.Fori(0, BLOCKS // 2 - 1) as pair:
                for par in range(2):
                    alone(pair * 2 + (ALL - BLOCKS + par), par, True)
            alone(ALL - 2, 0, True)
            alone(ALL - 1, 1, False)

        @block.scalar
        def _(act):
            f = nc.scalar.activation

            def abs_and_relu(k):
                act.wait_ge(dts_ready, k + 1)
                wait(act, sp_step, 5 * k)
                f(t_e[:, :], p_c[:, :], ACT.Abs, bias=b2_col[:, :]).then_inc(abs_relu, 1)
                f(t_r[:, :], p_c[:, :], ACT.Relu, bias=b2_col[:, :]).then_inc(abs_relu, 1)

            def exp_abs(k):
                act.wait_ge(abs_relu, 2 * k + 2)
                f(t_e[:, :], t_e[:, :], ACT.Exp, scale=-1.0).then_inc(e_ready, 1)

            def log_part(k):
                act.wait_ge(e_ready, k + 1)
                f(t_l[:, :], t_e[:, :], ACT.Ln, bias=1.0).then_inc(ln_ready, 1)

            def square(k):
                act.wait_ge(sp_step, 5 * k + 2)
                f(t_l[:, :], t_e[:, :], ACT.Square, scale=0.5 ** 0.5).then_inc(square_ready, 1)

            def top_part(k):
                act.wait_ge(du_ready, k + 1)
                for h in range(2):
                    wait(act, parts_in[h], 6 * DMA * k)
                f(top[:, :, :], t_d[:, :, :], ACT.Copy).then_inc(top_ready, 1)

            def mid_part(k):
                act.wait_ge(res_ready, k + 1)
                f(mid[:, :, :], t_rest[:, :, :], ACT.Copy).then_inc(mid_ready, 1)

            def decays(k, h, i):
                n = 16 * k + 8 * h + i
                th, j = 1 - i // TILES, i % TILES
                act.wait_ge(delta_spread, n + 1)
                if i == 0:
                    wait(act, fwd_step, FWD * (2 * k + h - 1))
                    wait(act, bwd_step, BWD * (2 * k + h - 1))
                f(decay[h][:, HT * th:HT * th + HT, j, :],
                  p_delta[i % 2][:, :].rearrange("p (t x) -> p t x", t=HT), ACT.Exp,
                  scale=a_col[:, TILES * h + j:TILES * h + j + 1]).then_inc(decay_ready, 1)

            def copy_b(k, th):
                act.wait_ge(b_ready, 2 * k + th + 1)
                if th == 0:
                    wait(act, inject_ready, 16 * k)
                f(b_rep[:, HT * th:HT * th + HT, :], p_c[:, :].rearrange("p (t x) -> p t x", t=HT),
                  ACT.Copy).then_inc(b_copied, 1)

            def copy_c(k, th):
                act.wait_ge(c_ready, 2 * k + th + 1)
                if th == 0:
                    wait(act, c_step, 2 * SC * k)
                f(c_rep[:, HT * th:HT * th + HT, :], p_c[:, :].rearrange("p (t x) -> p t x", t=HT),
                  ACT.Copy).then_inc(c_copied, 1)

            def gelu_z(k):
                act.wait_ge(z_ready, k + 1)
                wait(act, gated, k)
                f(gz[:, :], p_c[:, :], ACT.Gelu).then_inc(gz_ready, 1)
                act.preload_act_table_set("natural_log_exp_and_others")

            def copy_yo(k):
                act.wait_ge(yo_ready, k + 1)
                wait(act, y_stored, DMA * k)
                wait(act, stat_done, 2 * k)
                f(yo[:, :, :], p_c[:, 0:2 * PB].rearrange("p (h x) -> p h x", h=2), ACT.Copy).then_inc(yo_copied, 1)

            def put_max(a, bank=p_s, buf=0):
                act.wait_ge(nmax_t, a + 1)
                f(qa[buf][96:99, :], bank[0:3, 0:PB // 2].bitcast(BF16), ACT.Copy).then_inc(nmax_in, 1)

            def probs(a, g):
                act.wait_ge(cols_ready, KG * a + g + 1)
                wait(act, pv_done, KG * a + max(g - 1, 0))
                f(prob[g % 2][:, :], p_s[:, :], ACT.Exp).then_inc(prob_ready, 1)

            def norm_o(a):
                act.wait_ge(den_step, 2 * a + 2)
                wait(act, o_turned, a)
                f(o_n[:, :], p_o[:, 0:CH], ACT.Copy, scale=rden[:, 1:2]).then_inc(o_norm, 1)

            def iteration(k, head, att, rows):
                has = att is not None
                abs_and_relu(k + 1)
                exp_abs(k + 1)
                log_part(k + 1)
                if has:
                    probs(att, 0)
                    probs(att, 1)
                for j in range(8):
                    decays(k, 1, j)
                    if has and 1 <= j < KG - 1:
                        probs(att, j + 1)
                    if j == 1:
                        square(k + 1)
                    if j == 5:
                        top_part(k + 1)
                mid_part(k + 1)
                copy_c(k, 0)
                copy_c(k, 1)
                if has:
                    norm_o(att)
                if not head:
                    copy_yo(k - 1)
                copy_b(k + 1, 0)
                copy_b(k + 1, 1)
                gelu_z(k)
                for j in range(8):
                    decays(k + 1, 0, j)
                if rows:
                    put_max(att + 1)

            def prep(b):
                act.wait_ge(gn_step, 12 * b + 8)
                f(gsd[:, :], gvar[:, :], ACT.Sqrt).then_inc(gn_act, 1)
                act.preload_act_table_set("natural_log_exp_and_others")
                act.wait_ge(gn_step, 12 * b + 12)
                for pair in chunk_pairs(act, b):
                    c0 = pair * 2
                    for par in range(2):
                        n_c = b * CHUNKS + c0 + par
                        wait(act, x1_stored, DMA * (b * CHUNKS + c0))
                        wait(act, v_ready, 2 * (b * CHUNKS + c0))
                        for h in range(2):
                            act.wait_ge(xm_ready, 2 * n_c + h + 1)
                            f(x1c[par][:, h, :], xm[par][:, h, :], ACT.Identity, bias=gbias[:, h:h + 1]).then_inc(x1_ready, 1)
                        act.wait_ge(kq_ready, 2 * n_c + 1)
                        wait(act, kq_res, 2 * n_c)
                        f(kf, p_delta[0][0:96, :], ACT.Identity, bias=bk_col[:, :]).then_inc(kq_copied, 1)
                        act.wait_ge(kq_ready, 2 * n_c + 2)
                        f(qf, p_delta[1][0:96, :], ACT.Identity, bias=bq_col[:, :]).then_inc(kq_copied, 1)
                        cols = bass.ds((c0 + par) * CHUNK, CHUNK)
                        act.wait_ge(kq_copied, 2 * n_c + 2)
                        wait(act, kq_parts, 6 * n_c)
                        wait(act, q_stored, 2 * DMA * n_c)
                        f(ka[0:96, cols], kf, ACT.Copy).then_inc(a_done, 1)
                        f(qac, qf, ACT.Copy).then_inc(a_done, 1)
                        act.wait_ge(kq_res, 2 * n_c + 1)
                        f(kb[:, cols], kres, ACT.Copy).then_inc(b_done, 1)
                        act.wait_ge(kq_res, 2 * n_c + 2)
                        f(qbc, qres, ACT.Copy).then_inc(b_done, 1)
                        for m in range(2):
                            act.wait_ge(v_ready, 2 * n_c + m + 1)
                            f(v_t[:, bass.ds((c0 + par) * 4 + 2 * m, 2), 0:CH],
                              p_du[m][:, :].rearrange("p (m c) -> p m c", m=2), ACT.Copy).then_inc(v_copied, 1)
                wait_alone(act, v_ready, 2 * CHUNKS * (b + 1))
                wait_alone(act, x1_stored, DMA * CHUNKS * (b + 1))

            act.wait_ge(consts_in, CONSTS[0])
            act.preload_act_table_set("natural_log_exp_and_others")
            f(a_col[:, :], a_col[:, :], ACT.Exp).then_inc(setup_act, 1)
            act.wait_ge(setup_ready, 1)
            abs_and_relu(0)
            exp_abs(0)
            log_part(0)
            square(0)
            top_part(0)
            mid_part(0)
            copy_b(0, 0)
            copy_b(0, 1)
            for i in range(8):
                decays(0, 0, i)

            def phase(b, att):
                k0 = b * BLOCKS
                if att:
                    put_max(k0 - BLOCKS)
                for i in range(peeled(b)):
                    iteration(k0 + i, i == 0, k0 - BLOCKS + i if att else None, att)
                with act.Fori(peeled(b), BLOCKS - 1) as i:
                    iteration(k0 + i, False, k0 - BLOCKS + i if att else None, att)
                iteration(k0 + BLOCKS - 1, False, k0 - 1 if att else None, False)
                copy_yo(k0 + BLOCKS - 1)

            def alone(a, par, rows):
                for g in range(KG):
                    probs(a, g)
                if rows:
                    put_max(a + 1, p_y, 1 - par)
                norm_o(a)

            phase(0, False)
            prep(0)
            phase(1, True)
            with act.Fori(2, IMAGES) as b:
                prep(b - 1)
                phase(b, True)
            prep(IMAGES - 1)
            put_max(ALL - BLOCKS)
            with act.Fori(0, BLOCKS // 2 - 1) as pair:
                for par in range(2):
                    alone(pair * 2 + (ALL - BLOCKS + par), par, True)
            alone(ALL - 2, 0, True)
            alone(ALL - 1, 1, False)

        @block.vector
        def _(dve):
            tt = nc.vector.tensor_tensor

            def softplus_steps(k):
                def back():
                    dve.wait_ge(e_ready, k + 1)
                    nc.vector.tensor_scalar(t_c[:, :], t_e[:, :], 1.0, -1.0, ALU.add, ALU.add).then_inc(sp_step, 1)

                def less_log():
                    dve.wait_ge(sp_step, 5 * k + 1)
                    dve.wait_ge(ln_ready, k + 1)
                    tt(t_c[:, :], t_c[:, :], t_l[:, :], ALU.subtract).then_inc(sp_step, 1)

                def hold():
                    dve.wait_ge(sp_step, 5 * k + 2)
                    dve.wait_ge(square_ready, k + 1)
                    nc.vector.scalar_tensor_tensor(t_c[:, :], t_c[:, :], 0.0, t_l[:, :], ALU.max, ALU.min).then_inc(sp_step, 1)

                def less_g():
                    dve.wait_ge(sp_step, 5 * k + 3)
                    tt(t_l[:, :], t_e[:, :], t_c[:, :], ALU.subtract).then_inc(sp_step, 1)

                def plus_relu():
                    dve.wait_ge(sp_step, 5 * k + 4)
                    tt(t_d[:, 0, :], t_l[:, :], t_r[:, :], ALU.add).then_inc(sp_step, 1)

                def times_u():
                    dve.wait_ge(sp_step, 5 * k + 5)
                    dve.wait_ge(u_ready, k + 1)
                    tt(t_d[:, 1, :], t_d[:, 0, :], p_c[:, :], ALU.mult).then_inc(du_ready, 1)

                def rest():
                    dve.wait_ge(top_ready, k + 1)
                    tt(t_rest[:, :, :], t_d[:, :, :], top[:, :, :], ALU.subtract).then_inc(res_ready, 1)

                def last_part():
                    dve.wait_ge(mid_ready, k + 1)
                    tt(low[:, :, :], t_rest[:, :, :], mid[:, :, :], ALU.subtract).then_inc(low_ready, 1)

                return [back, less_log, hold, less_g, plus_relu, times_u, rest, last_part]

            def inject_item(k, h, i):
                n = 16 * k + 8 * h + i
                th, j = 1 - i // TILES, i % TILES
                if i == 0:
                    wait(dve, fwd_step, FWD * (2 * k + h))
                    wait(dve, bwd_step, BWD * (2 * k + h - 1) + 2 * (HT - 1))
                    dve.wait_ge(b_copied, 2 * k + 2)
                if i == TILES:
                    wait(dve, bwd_step, BWD * (2 * k + h - 1) + FWD)
                dve.wait_ge(du_spread, n + 1)
                ts = slice(HT * th, HT * th + HT)
                tt(inject[:, ts, j, :], p_du[i % 2][:, :].rearrange("p (t x) -> p t x", t=HT),
                   b_rep[:, ts, :], ALU.mult).then_inc(inject_ready, 1)

            def forward(k, h):
                unit = 2 * k + h
                steps = []

                def scale(t):
                    if t == 1:
                        dve.wait_ge(decay_ready, 8 * unit + 8)
                        dve.wait_ge(inject_ready, 8 * unit + 8)
                        wait(dve, y_summed, 2 * (unit - 1))
                        prev = inject[:, 0, :, :]
                    else:
                        wait(dve, fwd_step, FWD * unit + 2 * (t - 1))
                        prev = fwd[h][:, t - 1, :, :]
                    tt(fwd[h][:, t, :, :], decay[h][:, t, :, :], prev, ALU.mult).then_inc(fwd_step, 1)

                def add(t):
                    wait(dve, fwd_step, FWD * unit + 2 * (t - 1) + 1)
                    tt(fwd[h][:, t, :, :], fwd[h][:, t, :, :], inject[:, t, :, :], ALU.add).then_inc(fwd_step, 1)

                def both_at_end():
                    dve.wait_ge(fwd_step, FWD * unit + 14)
                    tt(fwd[h][:, TOK - 1, :, :], fwd[h][:, TOK - 1, :, :], inject[:, TOK - 1, :, :],
                       ALU.add).then_inc(fwd_step, 1)

                for t in range(1, TOK):
                    steps += [lambda t=t: scale(t), lambda t=t: add(t)]
                return steps + [both_at_end]

            def sum_and_c(k, h):
                unit = 2 * k + h
                steps = []
                count = 0
                for t in reversed(range(TOK)):
                    mine = 0 < t < TOK - 1 and t not in POOL_SUMS
                    if mine:
                        count += 1

                        def both(t=t):
                            wait(dve, bwd_step, BWD * unit + 2 * (TOK - 1 - t))
                            dve.wait_ge(fwd_step, FWD * unit + FWD)
                            tt(fwd[h][:, t, :, :], fwd[h][:, t, :, :], bwd[:, t, :, :], ALU.add).then_inc(c_step, 1)
                        steps.append(both)

                    def times_c(t=t, mine=mine, count=count):
                        if mine:
                            wait(dve, c_step, SC * unit + count)
                        elif t in POOL_SUMS or t == 0:
                            wait(dve, bwd_step, BWD * unit + 15 + (len(POOL_SUMS) - sorted(POOL_SUMS).index(t) if t else 0))
                        else:
                            dve.wait_ge(fwd_step, FWD * unit + FWD)
                            dve.wait_ge(c_copied, 2 * k + 2)
                        tt(fwd[h][:, t, :, :], fwd[h][:, t, :, :],
                           c_rep[:, t, :].unsqueeze(1).to_broadcast([P, TILES, PB]), ALU.mult).then_inc(c_step, 1)
                    steps.append(times_c)
                    count += 1
                assert count == SC
                return steps

            def gate(k):
                dve.wait_ge(y_summed, 4 * k + 4)
                dve.wait_ge(gz_ready, k + 1)
                wait(dve, yo_ready, k)
                tt(yz[:, :], p_y[:, :], gz[:, :], ALU.mult).then_inc(gated, 1)

            def channel_stats(k, i):
                dve.wait_ge(yo_copied, k + 1)
                for h in range(2):
                    nc.vector.bn_stats(stats[:, h, i, :], yo[:, h, :]).then_inc(stat_done, 1)

            def max_item(a, g, bank=p_s):
                dve.wait_ge(rows_ready, KG * a + g + 1)
                nc.vector.tensor_reduce(mx8[:, g:g + 1], bank[:, :], AX.X, ALU.max).then_inc(max_step, 1)

            def max_steps(a):
                def whole():
                    dve.wait_ge(max_step, KG * a + KG)
                    nc.vector.tensor_reduce(nmax[:, :], mx8[:, :], AX.X, ALU.max, negate=True).then_inc(nmax_step, 1)

                def first():
                    dve.wait_ge(nmax_step, 5 * a + 1)
                    nc.vector.tensor_copy(nparts[:, 0:1], nmax[:, :]).then_inc(nmax_step, 1)

                def rest():
                    dve.wait_ge(nmax_step, 5 * a + 2)
                    tt(nres[:, :], nmax[:, :], nparts[:, 0:1], ALU.subtract).then_inc(nmax_step, 1)

                def second():
                    dve.wait_ge(nmax_step, 5 * a + 3)
                    nc.vector.tensor_copy(nparts[:, 1:2], nres[:, :]).then_inc(nmax_step, 1)

                def third():
                    dve.wait_ge(nmax_step, 5 * a + 4)
                    tt(nparts[:, 2:3], nres[:, :], nparts[:, 1:2], ALU.subtract).then_inc(nmax_step, 1)

                return [whole, first, rest, second, third]

            def denominators(a):
                dve.wait_ge(pv_done, KG * a + KG)
                nc.vector.reciprocal(rden[:, 0:1], p_o[:, CH:CH + 1]).then_inc(den_step, 1)
                dve.wait_ge(den_step, 2 * a + 1)
                tt(rden[:, 1:2], rden[:, 0:1], gamma_col[:, :], ALU.mult).then_inc(den_step, 1)

            def add_residual(a, bank=p_s):
                dve.wait_ge(o_turned, a + 1)
                wait(dve, x1_in, DMA * (a + 1))
                wait(dve, out_stored, DMA * a)
                tt(o_c[:, :, :], bank[:, 0:2 * PB].rearrange("p (h x) -> p h x", h=2), x1b[:, :, :],
                   ALU.add).then_inc(o_added, 1)

            def interleave(main, fill, after):
                fill = list(zip(after, fill))
                for n, step in enumerate(main):
                    step()
                    while fill and fill[0][0] <= n + 1:
                        fill.pop(0)[1]()
                for _, step in fill:
                    step()

            def alternate(first, second):
                both = []
                while first or second:
                    both += first[:1] + second[:1]
                    first, second = first[1:], second[1:]
                return both

            def iteration(k, i, head, att, rows):
                has = att is not None
                for n in range(8):
                    inject_item(k, 0, n)
                main = alternate(forward(k, 0), [] if head else sum_and_c(k - 1, 1))
                interleave(main, softplus_steps(k + 1), (2, 4, 7, 9, 11, 13, 17, 23))
                items = [lambda n=n: inject_item(k, 1, n) for n in range(8)]
                fill = []
                if has:
                    fill += [(1, lambda: denominators(att)), (8, lambda: add_residual(att))]
                if not head:
                    fill.append((4, lambda: gate(k - 1)))
                fill.sort(key=lambda at_step: at_step[0])
                interleave(items, [step for _, step in fill], [at for at, _ in fill])
                main = alternate(forward(k, 1), sum_and_c(k, 0))
                fill = [(3 * g + 1, lambda g=g: max_item(att + 1, g)) for g in range(KG)] if rows else []
                if not head:
                    fill.append((15, lambda: channel_stats(k - 1, i - 1)))
                if rows:
                    fill += [(99, step) for step in max_steps(att + 1)]
                fill.sort(key=lambda at_step: at_step[0])
                interleave(main, [step for _, step in fill], [at for at, _ in fill])

            def tail(k):
                for step in sum_and_c(k, 1):
                    step()
                gate(k)
                channel_stats(k, BLOCKS - 1)

            def prep(b):
                g0 = 12 * b
                step = [0]

                def chain(ins):
                    ins.then_inc(gn_step, 1)
                    step[0] += 1
                    wait_alone(dve, gn_step, g0 + step[0])

                wait_alone(dve, stat_done, 2 * BLOCKS * (b + 1))
                for h in range(2):
                    chain(nc.vector.bn_aggr(mv[:, h, :], stats[:, h, :, :].rearrange("p n s -> p (n s)")))
                chain(tt(gst[:, :, 1], mv[:, :, 0], mv[:, :, 0], ALU.mult))
                nc.vector.tensor_copy(gst[:, :, 0], mv[:, :, 0])
                chain(tt(gst[:, :, 1], gst[:, :, 1], mv[:, :, 1], ALU.add))
                dve.wait_ge(gn_pe, b + 1)
                chain(nc.vector.tensor_copy(gsum[:, :, :], p_c[:, 0:4].rearrange("p (h s) -> p h s", h=2)))
                chain(tt(gvar[:, :], gsum[:, :, 0], gsum[:, :, 0], ALU.mult))
                chain(tt(gvar[:, :], gsum[:, :, 1], gvar[:, :], ALU.subtract))
                chain(nc.vector.tensor_scalar(gvar[:, :], gvar[:, :], GN_EPS, None, ALU.add))
                dve.wait_ge(gn_act, b + 1)
                chain(nc.vector.reciprocal(gsd[:, :], gsd[:, :]))
                chain(tt(gscale[:, :], gsd[:, :], gnw[:, :], ALU.mult))
                chain(tt(gbias[:, :], gsum[:, :, 0], gscale[:, :], ALU.mult))
                chain(tt(gbias[:, :], gnb[:, :], gbias[:, :], ALU.subtract))
                for pair in chunk_pairs(dve, b):
                    c0 = pair * 2
                    for par in range(2):
                        n_c = b * CHUNKS + c0 + par
                        cols = bass.ds((c0 + par) * CHUNK, CHUNK)
                        dve.wait_ge(chunk_in[par], DMA * (b * CHUNKS + c0) + 2 * DMA)
                        wait(dve, x1_ready, 2 * (b * CHUNKS + c0))
                        for h in range(2):
                            nc.vector.scalar_tensor_tensor(xm[par][:, h, :], yc[par][:, h, :], gscale[:, h:h + 1],
                                                           xc[par][:, h, :], ALU.mult, ALU.add).then_inc(xm_ready, 1)
                        dve.wait_ge(a_done, 2 * n_c + 1)
                        wait(dve, b_done, 2 * n_c)
                        tt(kres, kf, ka[0:96, cols], ALU.subtract).then_inc(kq_res, 1)
                        dve.wait_ge(a_done, 2 * n_c + 2)
                        tt(qres, qf, qac, ALU.subtract).then_inc(kq_res, 1)
                        dve.wait_ge(b_done, 2 * n_c + 1)
                        dve.wait_ge(kq_res, 2 * n_c + 2)
                        nc.vector.tensor_copy(kb[32:64, cols], ka[32:64, cols]).then_inc(kq_parts, 1)
                        nc.vector.tensor_copy(ka[64:96, cols], kb[64:96, cols]).then_inc(kq_parts, 1)
                        dve.wait_ge(kq_parts, 6 * n_c + 2)
                        tt(kb[64:96, cols], kres[64:96, :], kb[64:96, cols], ALU.subtract).then_inc(kq_parts, 1)
                        dve.wait_ge(b_done, 2 * n_c + 2)
                        nc.vector.tensor_copy(qbc[64:96, :], qac[64:96, :]).then_inc(kq_parts, 1)
                        nc.vector.tensor_copy(qac[32:64, :], qbc[32:64, :]).then_inc(kq_parts, 1)
                        dve.wait_ge(kq_parts, 6 * n_c + 5)
                        tt(qbc[32:64, :], qres[32:64, :], qbc[32:64, :], ALU.subtract).then_inc(kq_parts, 1)
                wait_alone(dve, b_done, 2 * CHUNKS * (b + 1))
                wait_alone(dve, q_stored, 2 * DMA * CHUNKS * (b + 1))

            cp = nc.vector.tensor_copy
            dve.wait_ge(consts_in, CONSTS[0])
            dve.wait_ge(setup_pe, 1)
            cp(s_mid[0:DIN, 128:128 + GCN], p_c[0:DIN, 0:GCN]).then_inc(setup_dve, 1)
            dve.wait_ge(setup_pe, 2)
            cp(s_mid[0:2, 64:128], p_y[0:2, 0:DIN]).then_inc(setup_dve, 1)
            for n in range(2):
                cp(s_mid[0:DIN, 384 + n * P:384 + (n + 1) * P].rearrange("p (d n) -> p d n", d=8),
                   s_small[0:DIN, 2 + n * NST:2 + (n + 1) * NST].unsqueeze(1).to_broadcast([DIN, 8, NST]))
            dve.wait_ge(setup_pe, 5)
            last = cp(s_mid[0:DIN, 256:256 + DIN], p_delta[0][0:DIN, 0:DIN]).then_inc(setup_dve, 1)
            last = cp(s_mid[0:DIN, 256 + DIN:256 + P], p_delta[0][0:DIN, 0:DIN]).then_inc(setup_dve, 1)
            dve.wait_ge(setup_pe, 6)
            cp(w_dbc[:, :, :], p_delta[1][0:GCN, 0:3 * P].rearrange("p (n c) -> p n c", n=3)).then_inc(setup_dve, 1)
            nc.vector.tensor_scalar(s_small[0:GCN, 128:192], s_small[0:GCN, 128:192], 2.0, None, ALU.mult).then_inc(setup_dve, 1)
            dve.wait_ge(setup_dve, 6)
            tt(w_skip[:, :], w_in[:, 0:DIN], s_small[0:GCN, 128:192], ALU.mult).then_inc(setup_dve, 1)
            nc.vector.tensor_scalar(b2_col[:, :], b2_col[:, :], 2.0, None, ALU.mult).then_inc(setup_dve, 1)
            dve.wait_ge(setup_act, 1)
            nc.vector.tensor_scalar(a_col[:, :], a_col[:, :], -1.0, None, ALU.mult).then_inc(setup_dve, 1)
            for bank, w in ((p_s, wq_t), (p_o, wk_t)):
                for r in range(3):
                    cp(w[:, :, 32 * r:32 * r + 32], bank[:, 0:64].rearrange("p (h d) -> p h d", h=2)).then_inc(setup_dve, 1)
            for h in range(2):
                cp(wv_t[:, h, :], p_du[h][:, 0:CH]).then_inc(setup_dve, 1)
            cp(identb[:, :], ident[:, :]).then_inc(setup_dve, 1)
            cp(spread[:, :, :], s_qk[0:96, 2 * CH:4 * CH].rearrange("p (j x) -> p j x", j=TILES)).then_inc(setup_dve, 1)
            nc.vector.memset(ones_row[:, :], 1.0).then_inc(setup_dve, 1)
            for h in range(2):
                d = slice(DIN * h, DIN * h + DIN)
                other = slice(DIN * (1 - h), DIN * (1 - h) + DIN)
                cp(w_out[d, h, :], w_out_raw[d, :]).then_inc(setup_dve, 1)
                nc.vector.memset(w_out[other, h, :], 0.0).then_inc(setup_dve, 1)
            nc.vector.memset(ka[96:99, :], 1.0).then_inc(setup_dve, 1)
            nc.vector.memset(v_t[:, :, CH:CH + 1], 1.0).then_inc(setup_dve, 1)
            dve.wait_ge(setup_dve, 26)
            nc.vector.memset(nres[:, :], 0.0).then_inc(setup_ready, 1)
            for step in softplus_steps(0):
                step()

            def find_max(a, banks=(p_s, p_s)):
                for g in range(KG):
                    max_item(a, g, banks[g % 2])
                for step in max_steps(a):
                    step()

            def phase(b, att):
                k0 = b * BLOCKS
                if att:
                    find_max(k0 - BLOCKS)
                for i in range(peeled(b)):
                    iteration(k0 + i, i, i == 0, k0 - BLOCKS + i if att else None, att)
                with dve.Fori(peeled(b), BLOCKS - 1) as i:
                    iteration(k0 + i, i, False, k0 - BLOCKS + i if att else None, att)
                iteration(k0 + BLOCKS - 1, BLOCKS - 1, False, k0 - 1 if att else None, False)
                tail(k0 + BLOCKS - 1)

            def alone(a, rows):
                if rows:
                    find_max(a + 1, p_delta)
                denominators(a)
                add_residual(a, p_du[0])

            phase(0, False)
            prep(0)
            phase(1, True)
            with dve.Fori(2, IMAGES) as b:
                prep(b - 1)
                phase(b, True)
            prep(IMAGES - 1)
            find_max(ALL - BLOCKS)
            with dve.Fori(0, BLOCKS // 2 - 1) as pair:
                for par in range(2):
                    alone(pair * 2 + (ALL - BLOCKS + par), True)
            alone(ALL - 2, True)
            alone(ALL - 1, False)

        @block.gpsimd
        def _(pool):
            tt = nc.gpsimd.tensor_tensor

            def backward(k, h):
                unit = 2 * k + h
                for t in reversed(range(TOK - 1)):
                    n = BWD * unit + 2 * (TOK - 2 - t)
                    if t == TOK - 2:
                        pool.wait_ge(decay_ready, 8 * unit + 4)
                        pool.wait_ge(inject_ready, 8 * unit + 4)
                    if t == HT - 1:
                        pool.wait_ge(decay_ready, 8 * unit + 8)
                        pool.wait_ge(inject_ready, 8 * unit + 8)
                    later = inject[:, TOK - 1, :, :] if t == TOK - 2 else bwd[:, t + 1, :, :]
                    if 0 < t and t not in POOL_SUMS:
                        wait(pool, c_step, SC * (unit - 1) + c_count(TOK - t) - 1)
                    wait(pool, bwd_step, n)
                    tt(bwd[:, t, :, :], decay[h][:, t, :, :], later, ALU.mult).then_inc(bwd_step, 1)
                    pool.wait_ge(bwd_step, n + 1)
                    tt(bwd[:, t, :, :], bwd[:, t, :, :], inject[:, t, :, :], ALU.add).then_inc(bwd_step, 1)
                pool.wait_ge(bwd_step, BWD * unit + 14)
                wait(pool, y_summed, 2 * (unit - 1))
                tt(fwd[h][:, 0, :, :], bwd[:, 0, :, :], inject[:, 0, :, :], ALU.add).then_inc(bwd_step, 1)
                pool.wait_ge(fwd_step, FWD * unit + FWD)
                for t in sorted(POOL_SUMS, reverse=True):
                    tt(fwd[h][:, t, :, :], fwd[h][:, t, :, :], bwd[:, t, :, :], ALU.add).then_inc(bwd_step, 1)

            pool.wait_ge(setup_ready, 1)
            for h in range(2):
                backward(0, h)
            with pool.Fori(1, ALL) as k:
                for h in range(2):
                    backward(k, h)


def constants():
    spread = np.zeros((96, TILES, P), np.float32)
    for part in range(3):
        for j in range(TILES):
            for d in range(8):
                spread[32 * part + 8 * j + d, j, NST * d:NST * d + NST] = 1
    total = np.zeros((P, 2 * TILES, DIN), np.float32)
    for j in range(2 * TILES):
        for d in range(8):
            total[NST * d:NST * d + NST, j, 8 * j + d] = 1
    group = np.zeros((P, P), np.float32)
    for g in range(2):
        group[64 * g:64 * g + 64, 64 * g:64 * g + 64] = 1 / 64
    return {"ident": np.eye(P, dtype=np.float32), "spread": spread, "sum": total, "group": group}


_INS = ["x", "L0_conv_W_in", "L0_conv_W_x", "L0_conv_W_dt", "L0_conv_b_dt", "L0_conv_A_logs", "L0_conv_Ds",
        "L0_conv_W_out", "L0_conv_gn_w", "L0_conv_gn_b", "L1_conv_Wq", "L1_conv_bq", "L1_conv_Wk", "L1_conv_bk",
        "L1_conv_Wv", "L1_conv_bv", "L1_conv_gamma"]


def kernel(**inputs):
    import concourse.bacc as bacc
    from concourse.bass_utils import run_bass_kernel_spmd

    nc = bacc.Bacc("TRN2", target_bir_lowering=False, num_devices=1, dynamic_dma_scratch_size=1024)
    arrays, args = {}, []
    data = [(name, np.ascontiguousarray(np.atleast_1d(inputs[name]))) for name in _INS]
    for name, a in data + list(constants().items()):
        arrays[f"in_{name}"] = a
        args.append(nc.dram_tensor(f"in_{name}", a.shape, mybir.dt.from_np(a.dtype), kind="ExternalInput").ap())
    out = nc.dram_tensor("out", (IMAGES, CH, 64, 64), F32, kind="ExternalOutput").ap()
    build(nc, *args, out)
    r = run_bass_kernel_spmd(nc, [arrays], core_ids=[0])
    return r.results[0]["out"]
```

```python
import numpy as np
from contextlib import ExitStack

import concourse.bass as bass
from concourse import mybir

F32 = mybir.dt.float32
BF16 = mybir.dt.bfloat16
ALU = mybir.AluOpType
ACT = mybir.ActivationFunctionType
AX = mybir.AxisListType

P = 128
IMAGES, CH, PIX = 4, 256, 64 * 64
TOK, GCN, DIN, NST = 8, 32, 64, 16
PB = 128
BLOCKS = PIX // PB
ALL = IMAGES * BLOCKS
TILES = 4
HT = TOK // 2
BANK = 512
KG = PIX // BANK
CHUNK = 512
CHUNKS = PIX // CHUNK
VC = CH + 1
GN_EPS = 1e-5
POOL_SUMS = (1, 2, 3, 4, 5)
FWD, BWD = 14, 14 + len(POOL_SUMS)
SC = TOK + (TOK - 2 - len(POOL_SUMS))
DMA = 16


def wait(eng, sem, value):
    if isinstance(value, int) and value <= 0:
        return
    assert isinstance(value, int) or value.min_val > 0
    eng.wait_ge(sem, value)


def build(nc, x, W_in, W_x, W_dt, b_dt, A_logs, Ds, W_out, gn_w, gn_b, Wq, bq, Wk, bk, Wv, bv, gamma,
          ident_in, spread_in, sum_in, group_in, out):
    ctx = ExitStack()
    with ctx:
        def sb(name, shape, dt=F32):
            return ctx.enter_context(nc.sbuf_tensor(name, shape, dt))

        def ps(name, shape, dt=F32):
            return ctx.enter_context(nc.psum_tensor(name, shape, dt))

        def sem(name):
            return ctx.enter_context(nc.semaphore(name))

        x_v = x.rearrange("b (h p) y z -> b p h (y z)", p=P)
        x_tok = x.rearrange("b (t g) y z -> b g t (y z)", g=GCN)
        out_v = out.rearrange("b (h p) y z -> b p h (y z)", p=P)
        y_dram = nc.dram_tensor("y_scratch", (P, 2, PIX), F32, kind="Internal").ap()
        x1_dram = nc.dram_tensor("x1_scratch", (P, 2, PIX), F32, kind="Internal").ap()
        qa_dram = nc.dram_tensor("qa_scratch", (96, PIX), BF16, kind="Internal").ap()
        qb_dram = nc.dram_tensor("qb_scratch", (96, PIX), BF16, kind="Internal").ap()

        ident = sb("ident", [P, P])
        identb = sb("identb", [P, P], BF16)
        spread = sb("spread", [96, TILES, P], BF16)
        statesum = sb("statesum", [P, 2 * TILES, DIN])
        groupmean = sb("groupmean", [P, P])
        w_in = sb("w_in", [GCN, 2 * DIN])
        w_out_raw = sb("w_out_raw", [P, GCN])
        w_skip = sb("w_skip", [GCN, DIN])
        w_dbc = sb("w_dbc", [GCN, 3, P])
        w_out = sb("w_out", [P, 2, GCN])
        a_col = sb("a_col", [P, 2 * TILES])
        b2_col = sb("b2_col", [P, 1])
        gnw = sb("gnw", [P, 2])
        gnb = sb("gnb", [P, 2])
        wq_t = sb("wq_t", [P, 2, 96])
        wk_t = sb("wk_t", [P, 2, 96])
        wv_t = sb("wv_t", [P, 2, CH])
        bq_col = sb("bq_col", [96, 1])
        bk_col = sb("bk_col", [96, 1])
        bv_rep = sb("bv_rep", [P, CH])
        gamma_col = sb("gamma_col", [P, 1])

        xa = sb("xa", [GCN, TOK, PB])
        xb = sb("xb", [GCN, TOK, PB])
        t_e = sb("t_e", [P, HT * PB])
        t_r = sb("t_r", [P, HT * PB])
        t_l = sb("t_l", [P, HT * PB])
        t_c = sb("t_c", [P, HT * PB])
        t_d = sb("t_d", [P, 2, HT * PB])
        t_rest = sb("t_rest", [P, 2, HT * PB])
        top = sb("top", [P, 2, HT * PB], BF16)
        mid = sb("mid", [P, 2, HT * PB], BF16)
        low = sb("low", [P, 2, HT * PB], BF16)
        parts = [sb(f"parts{h}", [96, 2, TOK * PB], BF16) for h in range(2)]
        b_rep = sb("b_rep", [P, TOK, PB])
        c_rep = sb("c_rep", [P, TOK, PB])
        decay = [sb(f"decay{h}", [P, TOK, TILES, PB]) for h in range(2)]
        inject = sb("inject", [P, TOK, TILES, PB])
        fwd = [sb(f"fwd{h}", [P, TOK, TILES, PB]) for h in range(2)]
        twice = sb("twice", [P, TILES, PB])
        bwd = sb("bwd", [P, TOK, TILES, PB])
        gz = sb("gz", [P, HT * PB])
        yz = sb("yz", [P, HT * PB])
        yo = sb("yo", [P, 2, PB])
        stats = sb("stats", [P, 2, BLOCKS, 6])
        mv = sb("mv", [P, 2, 2])
        gst = sb("gst", [P, 2, 2])
        gsum = sb("gsum", [P, 2, 2])
        gvar = sb("gvar", [P, 2])
        gsd = sb("gsd", [P, 2])
        gscale = sb("gscale", [P, 2])
        gbias = sb("gbias", [P, 2])
        ka = sb("ka", [99, PIX], BF16)
        kb = sb("kb", [96, PIX], BF16)
        v_t = sb("v_t", [P, PIX // P, VC])
        qa = [sb(f"qa{i}", [99, PB], BF16) for i in range(2)]
        qb = [sb(f"qb{i}", [96, PB], BF16) for i in range(2)]
        x1b = sb("x1b", [P, 2, PB])
        prob = [sb(f"prob{i}", [P, BANK]) for i in range(2)]
        mx8 = sb("mx8", [P, KG])
        nmax = sb("nmax", [P, 1])
        nres = sb("nres", [P, 1])
        nparts = sb("nparts", [P, 3], BF16)
        rden = sb("rden", [P, 2])
        o_n = sb("o_n", [P, CH])
        o_c = sb("o_c", [P, 2, PB])

        d0 = inject[:, :, :, :].rearrange("p t j x -> p (t j x)")
        d1 = decay[1][:, :, :, :].rearrange("p t j x -> p (t j x)")
        f0 = fwd[0][:, :, :, :].rearrange("p t j x -> p (t j x)")
        s_small, s_qk, s_v, s_mid = (f0[:, i * 1024:(i + 1) * 1024] for i in range(4))

        def halves(ap):
            return ap.rearrange("p (h x) -> p h x", h=2)

        yc = [halves(d0[:, i * 1024:(i + 1) * 1024]) for i in range(2)]
        xc = [halves(d0[:, (2 + i) * 1024:(3 + i) * 1024]) for i in range(2)]
        xm = [halves(d1[:, i * 1024:(i + 1) * 1024]) for i in range(2)]
        x1c = [halves(d1[:, (2 + i) * 1024:(3 + i) * 1024]) for i in range(2)]
        kf = f0[0:96, 0:CHUNK]
        qf = f0[0:96, CHUNK:2 * CHUNK]
        kres = f0[0:96, 2 * CHUNK:3 * CHUNK]
        qres = f0[0:96, 3 * CHUNK:4 * CHUNK]
        qac = fwd[1][0:96, 0, 0:2, :].rearrange("p j x -> p (j x)").bitcast(BF16)
        qbc = fwd[1][0:96, 0, 2:4, :].rearrange("p j x -> p (j x)").bitcast(BF16)

        p_delta = [ps(f"p_delta{i}", [P, BANK]) for i in range(2)]
        p_du = [ps(f"p_du{i}", [P, BANK]) for i in range(2)]
        p_c = ps("p_c", [P, BANK])
        p_y = ps("p_y", [P, BANK])
        p_s = ps("p_s", [P, BANK])
        p_o = ps("p_o", [P, BANK])

        consts_in = sem("consts_in")
        setup_pe, setup_dve, setup_act, setup_ready = sem("setup_pe"), sem("setup_dve"), sem("setup_act"), sem("setup_ready")
        xa_in, xb_in = sem("xa_in"), sem("xb_in")
        dts_ready, u_ready, b_ready, c_ready, z_ready, yo_ready = map(
            sem, ("dts_ready", "u_ready", "b_ready", "c_ready", "z_ready", "yo_ready"))
        abs_relu, e_ready, ln_ready, square_ready, top_ready, mid_ready = map(
            sem, ("abs_relu", "e_ready", "ln_ready", "square_ready", "top_ready", "mid_ready"))
        sp_step, du_ready, res_ready, low_ready = map(sem, ("sp_step", "du_ready", "res_ready", "low_ready"))
        parts_in = [sem(f"parts_in{h}") for h in range(2)]
        b_copied, c_copied, gz_ready, yo_copied = map(sem, ("b_copied", "c_copied", "gz_ready", "yo_copied"))
        delta_spread, du_spread, decay_ready, inject_ready = map(
            sem, ("delta_spread", "du_spread", "decay_ready", "inject_ready"))
        fwd_step, bwd_step, c_step, y_summed, skip_done, gated, stat_done, y_stored = map(
            sem, ("fwd_step", "bwd_step", "c_step", "y_summed", "skip_done", "gated", "stat_done", "y_stored"))
        twice_ready = sem("twice_ready")
        gn_step, gn_pe, gn_act = sem("gn_step"), sem("gn_pe"), sem("gn_act")
        chunk_in = [sem(f"chunk_in{i}") for i in range(2)]
        xm_ready, x1_ready, kq_ready, v_ready, kq_copied, v_copied = map(
            sem, ("xm_ready", "x1_ready", "kq_ready", "v_ready", "kq_copied", "v_copied"))
        a_done, kq_res, b_done, kq_parts, q_stored = map(sem, ("a_done", "kq_res", "b_done", "kq_parts", "q_stored"))
        x1_stored = [sem(f"x1_stored{i}") for i in range(2)]
        q_in, x1_in = sem("q_in"), sem("x1_in")
        rows_ready, max_step, nmax_step, nmax_t, nmax_in = map(
            sem, ("rows_ready", "max_step", "nmax_step", "nmax_t", "nmax_in"))
        cols_ready, prob_ready, pv_done, den_step, o_norm, o_turned, o_added, out_stored = map(
            sem, ("cols_ready", "prob_ready", "pv_done", "den_step", "o_norm", "o_turned", "o_added", "out_stored"))

        passed = {e.engine: sem(f"passed_{n}") for n, e in (("sp", nc.sync), ("pe", nc.tensor), ("act", nc.scalar), ("dve", nc.vector))}
        CONSTS = [0]

        def peeled(b):
            return 2 if isinstance(b, int) and b == 0 else 1

        def chunk_pairs(eng, b):
            first = 1 if isinstance(b, int) and b == 0 else 0
            for pair in range(first):
                yield pair, True
            with eng.Fori(first, CHUNKS // 2 - 1) as pair:
                yield pair, True
            yield CHUNKS // 2 - 1, False

        C_STEPS = []
        for t in (TOK - 2, TOK - 1, *reversed(range(TOK - 2))):
            if 0 < t < TOK - 1 and t not in POOL_SUMS:
                C_STEPS.append(("sum", t))
            C_STEPS.append(("times C", t))
        assert len(C_STEPS) == SC

        def wait_alone(eng, sem, value):
            wait(eng, sem, value)
            if not isinstance(value, int):
                eng.sem_inc(passed[eng.engine], 1)

        block = ctx.enter_context(nc.Block())

        @block.sync
        def _(sp):
            n = 0
            src_dst = [(ident[:, :], ident_in), (groupmean[:, :], group_in),
                       (s_qk[0:96, 2 * CH:4 * CH].rearrange("p (j x) -> p j x", j=TILES), spread_in), (statesum[:, :, :], sum_in)]
            src_dst.append((w_in[:, :], W_in))
            for r in range(2):
                src_dst.append((w_out_raw[DIN * r:DIN * r + DIN, :], W_out))
                src_dst.append((b2_col[DIN * r:DIN * r + DIN, :], b_dt.rearrange("(d o) -> d o", o=1)))
            for r in range(3):
                src_dst.append((bq_col[32 * r:32 * r + 32, :], bq.rearrange("(d o) -> d o", o=1)))
                src_dst.append((bk_col[32 * r:32 * r + 32, :], bk.rearrange("(d o) -> d o", o=1)))
            src_dst += [
                (s_small[0:DIN, 0:34], W_x), (s_small[0:2, 64:128], W_dt),
                (s_small[0:GCN, 128:192], Ds.rearrange("(o d) -> o d", o=1).to_broadcast([GCN, DIN])),
                (s_qk[0:32, 0:CH], Wq), (s_qk[0:32, CH:2 * CH], Wk),
                (s_v[:, 0:CH], Wv[0:P, :]), (s_v[:, CH:2 * CH], Wv[P:2 * P, :]),
                (bv_rep[:, :], bv.rearrange("(o d) -> o d", o=1).to_broadcast([P, CH])),
                (gamma_col[:, :], gamma.rearrange("(o d) -> o d", o=1).to_broadcast([P, 1])),
            ]
            for dst, src in src_dst:
                sp.dma_start(dst, src).then_inc(consts_in, DMA)
                n += 1
            with nc.allow_non_contiguous_dma(reason="small parameters, once"):
                sp.dma_start(a_col[:, :], A_logs.rearrange("(j d) n -> (d n) j", d=8)).then_inc(consts_in, DMA)
                sp.dma_start(gnw[:, :], gn_w.rearrange("(h p) -> p h", p=P)).then_inc(consts_in, DMA)
                sp.dma_start(gnb[:, :], gn_b.rearrange("(h p) -> p h", p=P)).then_inc(consts_in, DMA)
            CONSTS[0] = (n + 3) * DMA

            def load_xa(b, i):
                sp.dma_start(xa[:, :, :], x_tok[b, :, :, bass.ds(i * PB, PB)]).then_inc(xa_in, DMA)

            def load_q(a, i, images, buf=0, used_by=0):
                wait_alone(sp, q_stored, images * CHUNKS * 2 * DMA)
                wait_alone(sp, cols_ready, KG * (a - used_by))
                sp.dma_start(qa[buf][0:96, :], qa_dram[:, bass.ds(i * PB, PB)]).then_inc(q_in, DMA)
                sp.dma_start(qb[buf][:, :], qb_dram[:, bass.ds(i * PB, PB)]).then_inc(q_in, DMA)

            def load_x1(a, i, images):
                for par in range(2):
                    wait_alone(sp, x1_stored[par], images * (CHUNKS // 2) * DMA)
                wait_alone(sp, o_added, a)
                sp.dma_start(x1b[:, :, :], x1_dram[:, :, bass.ds(i * PB, PB)]).then_inc(x1_in, DMA)

            def move_parts(k, h):
                for n, (part, ready) in enumerate(((top, top_ready), (mid, mid_ready), (low, low_ready))):
                    wait_alone(sp, ready, k + 1)
                    if n == 0:
                        wait_alone(sp, delta_spread, 16 * k - 8 * (1 - h))
                        wait_alone(sp, du_spread, 16 * k - 8 * (1 - h))
                    for th in range(2):
                        r = DIN * th + 32 * h
                        sp.dma_start(parts[h][32 * n:32 * n + 32, :, th * BANK:(th + 1) * BANK],
                                     part[r:r + 32, :, :]).then_inc(parts_in[h], DMA)

            def store_y(k, i):
                wait_alone(sp, yo_copied, k + 1)
                sp.dma_start(y_dram[:, :, bass.ds(i * PB, PB)], yo[:, :, :]).then_inc(y_stored, DMA)

            def store_out(a, b, i):
                wait_alone(sp, o_added, a + 1)
                sp.dma_start(out_v[b, :, :, bass.ds(i * PB, PB)], o_c[:, :, :]).then_inc(out_stored, DMA)

            def load_xb(k, b, i):
                wait_alone(sp, skip_done, k)
                wait_alone(sp, z_ready, k)
                sp.dma_start(xb[:, :, :], x_tok[b, :, :, bass.ds(i * PB, PB)]).then_inc(xb_in, DMA)

            def next_xa(k, b, i):
                wait_alone(sp, b_ready, 2 * k + 2)
                load_xa(b, i)

            def iteration(k, b, i, head, att, load_next):
                if att:
                    load_x1(att[0], att[2], b)
                move_parts(k + 1, 0)
                if att and not (isinstance(i, int) and i == BLOCKS - 1):
                    load_q(att[0] + 1, att[2] + 1, b)
                move_parts(k + 1, 1)
                if att:
                    store_out(*att)
                if not head:
                    store_y(k - 1, i - 1)
                load_next()

            def phase(b, att):
                k0 = b * BLOCKS
                a0 = k0 - BLOCKS

                def block(i, load_next):
                    iteration(k0 + i, b, i, isinstance(i, int) and i == 0, (a0 + i, b - 1, i) if att else None, load_next)

                def next_here(i):
                    next_xa(k0 + i + 1, b, i + 2)
                    load_xb(k0 + i + 1, b, i + 1)

                if att:
                    load_q(a0, 0, b)
                for i in range(peeled(b)):
                    block(i, lambda: next_here(i))
                with sp.Fori(peeled(b), BLOCKS - 2) as i:
                    block(i, lambda: next_here(i))
                i = BLOCKS - 2
                block(i, lambda: (next_xa(k0 + i + 1, clamp(b), 0), load_xb(k0 + i + 1, b, i + 1)))
                i = BLOCKS - 1
                block(i, lambda: (next_xa(k0 + i + 1, clamp(b), 1), load_xb(k0 + i + 1, clamp(b), 0)))
                store_y(k0 + BLOCKS - 1, BLOCKS - 1)

            def clamp(b):
                return min(b + 1, IMAGES - 1) if isinstance(b, int) else b + 1

            def prep(b):
                k_end = BLOCKS * (b + 1)
                wait_alone(sp, y_stored, DMA * k_end)

                def load_chunk(c, par):
                    n_c = b * CHUNKS + c
                    wait_alone(sp, xm_ready, 2 * (n_c - 1))
                    cols = bass.ds(c * CHUNK, CHUNK)
                    sp.dma_start(yc[par], y_dram[:, :, cols]).then_inc(chunk_in[par], DMA)
                    sp.dma_start(xc[par], x_v[b, :, :, cols]).then_inc(chunk_in[par], DMA)

                for par in range(2):
                    load_chunk(par, par)
                for pair, more in chunk_pairs(sp, b):
                    for par in range(2):
                        c = pair * 2 + par
                        n_c = b * CHUNKS + c
                        cols = bass.ds(c * CHUNK, CHUNK)
                        wait_alone(sp, x1_ready, 2 * n_c + 2)
                        sp.dma_start(x1_dram[:, :, cols], x1c[par]).then_inc(x1_stored[par], DMA)
                        if more:
                            load_chunk(c + 2, par)
                        wait_alone(sp, kq_parts, 6 * n_c + 6)
                        sp.dma_start(qa_dram[:, cols], qac).then_inc(q_stored, DMA)
                        sp.dma_start(qb_dram[:, cols], qbc).then_inc(q_stored, DMA)

            def load_q_ahead(a, i, buf):
                wait_alone(sp, q_in, 2 * DMA * a)
                load_q(a, i, IMAGES, buf, used_by=1)

            def alone_step(a, i, par, more):
                if more:
                    load_q_ahead(a + 2, i + 2, par)
                store_out(a, IMAGES - 1, i)
                load_x1(a + 1, i + 1, IMAGES)

            load_xa(0, 0)
            sp.dma_start(xb[:, :, :], x_tok[0, :, :, 0:PB]).then_inc(xb_in, DMA)
            wait_alone(sp, setup_ready, 1)
            for h in range(2):
                move_parts(0, h)
            wait_alone(sp, b_ready, 2)
            load_xa(0, 1)
            phase(0, False)
            prep(0)
            phase(1, True)
            with sp.Fori(2, IMAGES - 1) as b:
                prep(b - 1)
                phase(b, True)
            prep(IMAGES - 2)
            phase(IMAGES - 1, True)
            prep(IMAGES - 1)
            last = ALL - BLOCKS
            load_q(last, 0, IMAGES)
            load_x1(last, 0, IMAGES)
            load_q_ahead(last + 1, 1, 1)
            with sp.Fori(0, BLOCKS // 2 - 1) as pair:
                for par in range(2):
                    alone_step(last + pair * 2 + par, pair * 2 + par, par, True)
            alone_step(ALL - 2, BLOCKS - 2, 0, False)
            store_out(ALL - 1, IMAGES - 1, BLOCKS - 1)
            sp.wait_ge(out_stored, DMA * ALL)
            sp.wait_ge(y_stored, DMA * ALL)
            for par in range(2):
                sp.wait_ge(x1_stored[par], DMA * IMAGES * CHUNKS // 2)
            sp.wait_ge(q_stored, 2 * DMA * IMAGES * CHUNKS)
            sp.wait_ge(xa_in, DMA * (ALL + 2))
            sp.wait_ge(xb_in, DMA * (ALL + 1))
            for h in range(2):
                sp.wait_ge(parts_in[h], 6 * DMA * (ALL + 1))

        @block.tensor
        def _(pe):
            mm = pe.matmul

            def project(dst, weights, xt, tokens, done):
                for n, t in enumerate(tokens):
                    last = mm(dst[:, n * PB:(n + 1) * PB], weights, xt[:, t, :], start=True, stop=True)
                last.then_inc(done, 1)

            def project_halves(dst, weights, xt, done, **flags):
                flags = flags or dict(start=True, stop=True)
                for t in range(TOK):
                    h = t // HT
                    last = mm(dst[DIN * h:DIN * h + DIN, (t % HT) * PB:(t % HT + 1) * PB], weights, xt[:, t, :], **flags)
                last.then_inc(done, 1)

            def dts(k):
                wait(pe, xa_in, DMA * (k + 1))
                project_halves(p_c, w_dbc[:, 0, 0:DIN], xa, dts_ready)

            def u(k):
                pe.wait_ge(abs_relu, 2 * k + 2)
                project_halves(p_c, w_in[:, 0:DIN], xa, u_ready)

            def b_states(k, th):
                wait(pe, b_copied, 2 * k + th)
                project(p_c, w_dbc[:, 1, :], xa, range(HT * th, HT * th + HT), b_ready)

            def c_states(k, th):
                wait(pe, xb_in, DMA * (k + 1))
                pe.wait_ge(du_ready, k + 2)
                wait(pe, c_copied, 2 * k + th)
                project(p_c, w_dbc[:, 2, :], xb, range(HT * th, HT * th + HT), c_ready)

            def z_gate(k):
                pe.wait_ge(b_copied, 2 * (k + 1) + 2)
                project_halves(p_c, w_in[:, DIN:2 * DIN], xb, z_ready)

            def y_out(k):
                wait_alone(pe, gated, k + 1)
                for t in range(TOK):
                    r, h = 32 * (t % HT), t // HT
                    last = mm(p_c[r:r + 32, h * PB:(h + 1) * PB], w_out[:, h, :],
                              yz[:, (t % HT) * PB:(t % HT + 1) * PB], start=True, stop=True)
                last.then_inc(yo_ready, 1)

            def spread_delta(k, h, i):
                n = 16 * k + 8 * h + i
                th, j = 1 - i // TILES, i % TILES
                if i == 0:
                    wait(pe, parts_in[h], 6 * DMA * (k + 1))
                wait(pe, decay_ready, n - 1)
                mm(p_delta[i % 2][:, :], spread[:, j, :], parts[h][:, 0, th * BANK:(th + 1) * BANK],
                   start=True, stop=True).then_inc(delta_spread, 1)

            def spread_du(k, h, i):
                n = 16 * k + 8 * h + i
                th, j = 1 - i // TILES, i % TILES
                if i == 0:
                    wait(pe, parts_in[h], 6 * DMA * (k + 1))
                wait(pe, inject_ready, n - 1)
                mm(p_du[i % 2][:, :], spread[:, j, :], parts[h][:, 1, th * BANK:(th + 1) * BANK],
                   start=True, stop=True).then_inc(du_spread, 1)

            def sum_states(k, h, th):
                unit = 2 * k + h
                if h == 0:
                    wait(pe, gated, k)
                wait(pe, c_step, SC * unit + (SC if th == 0 else C_STEPS.index(("times C", HT)) + 1))
                region = p_y[DIN * th:DIN * th + DIN, :]
                for j in range(TILES):
                    last = mm(region, statesum[:, TILES * h + j, :], fwd[h][:, HT * th:HT * th + HT, j, :],
                              start=(h == 0 and j == 0), stop=(h == 1 and j == TILES - 1))
                last.then_inc(y_summed, 1)

            def skip_term(k):
                project_halves(p_y, w_skip[:, :], xb, skip_done, start=False, stop=False, skip_group_check=True)

            def key_rows(a, g, banks=(p_o, p_s), buf=0):
                bank = banks[g % 2]
                if g == 0:
                    wait(pe, q_in, 2 * DMA * (a + 1))
                    wait(pe, max_step, KG * a)
                    if bank is p_o:
                        wait(pe, o_norm, a)
                if g == 1 and bank is p_s:
                    wait(pe, o_added, a)
                if g > 1:
                    wait(pe, max_step, KG * a + g - 1)
                cols = slice(g * BANK, (g + 1) * BANK)
                mm(bank[:, :], qa[buf][0:96, :], ka[0:96, cols], start=True, stop=False)
                mm(bank[:, :], qb[buf][:, :], kb[:, cols], start=False, stop=True).then_inc(rows_ready, 1)

            def turn_max(a, bank=p_s):
                pe.wait_ge(nmax_step, 5 * a + 5)
                pe.wait_ge(max_step, KG * a + KG)
                pe.transpose(bank[0:3, 0:PB // 2].bitcast(BF16), nparts[:, :], identb[:, :]).then_inc(nmax_t, 1)

            def key_cols(a, g, buf=0):
                pe.wait_ge(nmax_in, a + 1)
                wait(pe, prob_ready, KG * a + g)
                for m in range(4):
                    keys = slice(g * BANK + m * P, g * BANK + (m + 1) * P)
                    region = p_s[:, m * PB:(m + 1) * PB]
                    mm(region, ka[:, keys], qa[buf][:, :], start=True, stop=False)
                    last = mm(region, kb[:, keys], qb[buf][:, :], start=False, stop=True)
                last.then_inc(cols_ready, 1)

            def value_product(a, g, m):
                if g == 0 and m == 0:
                    wait(pe, o_norm, a)
                if m == 0:
                    pe.wait_ge(prob_ready, KG * a + g + 1)
                last = mm(p_o[:, 0:VC], prob[g % 2][:, m * PB:(m + 1) * PB], v_t[:, 4 * g + m, :],
                          start=(g == 0 and m == 0), stop=(g == KG - 1 and m == 3))
                if m == 3:
                    last.then_inc(pv_done, 1)

            def values(a, g):
                for m in range(4):
                    value_product(a, g, m)

            def turn_out(a, bank=p_s):
                pe.wait_ge(o_norm, a + 1)
                if bank is not p_s:
                    wait(pe, o_added, a)
                for h in range(2):
                    last = pe.transpose(bank[:, h * PB:(h + 1) * PB], o_n[:, h * P:(h + 1) * P], ident[:, :])
                last.then_inc(o_turned, 1)

            def iteration(k, head, att, rows, last=False):
                has = att is not None
                if head:
                    wait(pe, yo_copied, k)
                    spread_du(k, 0, 0)
                    spread_du(k, 0, 1)
                wait(pe, gz_ready, k)
                pe.wait_ge(b_copied, 2 * k + 2)
                dts(k + 1)
                if has:
                    key_cols(att, 0)
                for i in range(2, 8):
                    spread_du(k, 0, i)
                    if i == 3 and not head:
                        skip_term(k - 1)
                    if i == 5 and has:
                        key_cols(att, 1)
                    if i > 5 and has:
                        value_product(att, 0, 2 * i - 12)
                        value_product(att, 0, 2 * i - 11)
                for j in range(8):
                    spread_delta(k, 1, j)
                    if has and j:
                        if j + 1 < KG:
                            key_cols(att, j + 1)
                        values(att, j)
                    if j == 1:
                        u(k + 1)
                    if j == 4 and not head:
                        sum_states(k - 1, 1, 1)
                    if j == 5:
                        c_states(k, 0)
                spread_du(k, 1, 0)
                spread_du(k, 1, 1)
                if not head:
                    sum_states(k - 1, 1, 0)
                c_states(k, 1)
                for i in range(2, 8):
                    spread_du(k, 1, i)
                    if i == 3 and has:
                        turn_out(att)
                    if i == 5 and not head:
                        pe.wait_ge(c_copied, 2 * k + 2)
                        y_out(k - 1)
                if head:
                    pe.wait_ge(c_copied, 2 * k + 2)
                else:
                    wait(pe, yo_copied, k)
                for j in range(8):
                    if rows:
                        key_rows(att + 1, j)
                    if j == 0:
                        b_states(k + 1, 0)
                    if j == 1:
                        b_states(k + 1, 1)
                    if j == 2:
                        z_gate(k)
                    if j >= 2:
                        spread_delta(k + 1, 0, j - 2)
                    if j == 5:
                        sum_states(k, 0, 1)
                    if j == 7:
                        sum_states(k, 0, 0)
                spread_delta(k + 1, 0, 6)
                spread_delta(k + 1, 0, 7)
                if not last:
                    spread_du(k + 1, 0, 0)
                    spread_du(k + 1, 0, 1)
                if rows:
                    turn_max(att + 1)

            def tail(k):
                skip_term(k)
                sum_states(k, 1, 1)
                sum_states(k, 1, 0)
                pe.wait_ge(gz_ready, k + 1)
                y_out(k)

            def prep(b):
                pe.wait_ge(gn_step, 12 * b + 4)
                wait(pe, yo_copied, BLOCKS * (b + 1))
                mm(p_c[:, 0:4], groupmean[:, :], gst[:, :, :].rearrange("p a c -> p (a c)"),
                   start=True, stop=True).then_inc(gn_pe, 1)
                for pair, _ in chunk_pairs(pe, b):
                    c0 = pair * 2
                    for par in range(2):
                        n_c = b * CHUNKS + c0 + par
                        pe.wait_ge(x1_ready, 2 * n_c + 2)
                        wait(pe, kq_copied, 2 * n_c)
                        pe.wait_ge(decay_ready, 16 * BLOCKS * (b + 1) + 8)
                        for bank, w in ((p_delta[0], wk_t), (p_delta[1], wq_t)):
                            for h in range(2):
                                last = mm(bank[0:96, :], w[:, h, :], x1c[par][:, h, :], start=(h == 0), stop=(h == 1))
                            last.then_inc(kq_ready, 1)
                        wait(pe, v_copied, 2 * n_c)
                        for m in range(4):
                            region = p_du[m // 2][:, (m % 2) * CH:(m % 2 + 1) * CH]
                            for h in range(2):
                                last = mm(region, x1c[par][:, h, m * P:(m + 1) * P], wv_t[:, h, :],
                                          start=(h == 0), stop=(h == 1))
                            if m % 2:
                                last.then_inc(v_ready, 1)
                wait_alone(pe, kq_copied, 2 * CHUNKS * (b + 1))
                wait_alone(pe, v_copied, 2 * CHUNKS * (b + 1))

            pe.wait_ge(consts_in, CONSTS[0])
            pe.transpose(p_c[0:DIN, 0:GCN], w_in[:, 0:DIN], ident[0:GCN, 0:GCN]).then_inc(setup_pe, 1)
            pe.transpose(p_y[0:2, 0:DIN], s_small[0:DIN, 0:2], ident[0:DIN, 0:DIN]).then_inc(setup_pe, 1)
            for n, bank in ((0, p_s), (1, p_o)):
                for h in range(2):
                    last = pe.transpose(bank[:, h * 32:(h + 1) * 32], s_qk[0:32, n * CH + h * P:n * CH + (h + 1) * P],
                                        ident[0:32, 0:32])
            last.then_inc(setup_pe, 1)
            for h in range(2):
                for c in range(2):
                    last = pe.transpose(p_du[h][:, c * P:(c + 1) * P], s_v[:, c * CH + h * P:c * CH + (h + 1) * P],
                                        ident[:, :])
            last.then_inc(setup_pe, 1)
            pe.wait_ge(setup_dve, 2)
            mm(p_delta[0][0:DIN, 0:DIN], s_mid[0:2, 64:128], s_small[0:2, 64:128], start=True, stop=True).then_inc(setup_pe, 1)
            pe.wait_ge(setup_dve, 4)
            mm(p_delta[1][0:GCN, 0:3 * P], s_mid[0:DIN, 128:128 + GCN], s_mid[0:DIN, 256:640], start=True, stop=True).then_inc(setup_pe, 1)
            pe.wait_ge(setup_ready, 1)
            dts(0)
            u(0)
            pe.wait_ge(du_ready, 1)
            b_states(0, 0)
            b_states(0, 1)
            for i in range(8):
                spread_delta(0, 0, i)

            def first_rows(a):
                for g in range(KG):
                    key_rows(a, g)
                turn_max(a)

            def phase(b, att):
                k0 = b * BLOCKS
                if att:
                    first_rows(k0 - BLOCKS)
                for i in range(peeled(b)):
                    iteration(k0 + i, i == 0, k0 - BLOCKS + i if att else None, att)
                with pe.Fori(peeled(b), BLOCKS - 1) as i:
                    iteration(k0 + i, False, k0 - BLOCKS + i if att else None, att)
                iteration(k0 + BLOCKS - 1, False, k0 - 1 if att else None, False, last=True)
                tail(k0 + BLOCKS - 1)

            def alone(a, par, rows):
                key_cols(a, 0, par)
                for g in range(KG):
                    if rows:
                        key_rows(a + 1, g, p_delta, 1 - par)
                    if g + 1 < KG:
                        key_cols(a, g + 1, par)
                    values(a, g)
                if rows:
                    turn_max(a + 1, p_y)
                turn_out(a, p_du[0])

            phase(0, False)
            prep(0)
            phase(1, True)
            with pe.Fori(2, IMAGES) as b:
                prep(b - 1)
                phase(b, True)
            prep(IMAGES - 1)
            first_rows(ALL - BLOCKS)
            with pe.Fori(0, BLOCKS // 2 - 1) as pair:
                for par in range(2):
                    alone(pair * 2 + (ALL - BLOCKS + par), par, True)
            alone(ALL - 2, 0, True)
            alone(ALL - 1, 1, False)

        @block.scalar
        def _(act):
            f = nc.scalar.activation

            def abs_and_relu(k):
                act.wait_ge(dts_ready, k + 1)
                wait(act, sp_step, 5 * k)
                f(t_e[:, :], p_c[:, :], ACT.Abs, bias=b2_col[:, :]).then_inc(abs_relu, 1)
                f(t_r[:, :], p_c[:, :], ACT.Relu, bias=b2_col[:, :]).then_inc(abs_relu, 1)

            def exp_abs(k):
                act.wait_ge(abs_relu, 2 * k + 2)
                f(t_e[:, :], t_e[:, :], ACT.Exp, scale=-1.0).then_inc(e_ready, 1)

            def log_part(k):
                act.wait_ge(e_ready, k + 1)
                f(t_l[:, :], t_e[:, :], ACT.Ln, bias=1.0).then_inc(ln_ready, 1)

            def square(k):
                act.wait_ge(sp_step, 5 * k + 2)
                f(t_l[:, :], t_e[:, :], ACT.Square, scale=0.5 ** 0.5).then_inc(square_ready, 1)

            def top_part(k):
                act.wait_ge(du_ready, k + 1)
                for h in range(2):
                    wait(act, parts_in[h], 6 * DMA * k)
                f(top[:, :, :], t_d[:, :, :], ACT.Copy).then_inc(top_ready, 1)

            def mid_part(k):
                act.wait_ge(res_ready, k + 1)
                f(mid[:, :, :], t_rest[:, :, :], ACT.Copy).then_inc(mid_ready, 1)

            def decays(k, h, i):
                n = 16 * k + 8 * h + i
                th, j = 1 - i // TILES, i % TILES
                act.wait_ge(delta_spread, n + 1)
                if i == 0:
                    wait(act, fwd_step, FWD * (2 * k + h - 1))
                    wait(act, bwd_step, BWD * (2 * k + h - 1))
                f(decay[h][:, HT * th:HT * th + HT, j, :],
                  p_delta[i % 2][:, :].rearrange("p (t x) -> p t x", t=HT), ACT.Exp,
                  scale=a_col[:, TILES * h + j:TILES * h + j + 1]).then_inc(decay_ready, 1)

            def twice_inject(k, h):
                unit = 2 * k + h
                act.wait_ge(inject_ready, 8 * unit + 8)
                wait(act, bwd_step, BWD * (unit - 1) + BWD - len(POOL_SUMS))
                f(twice[:, :, :], inject[:, 0, :, :], ACT.Copy, scale=2.0).then_inc(twice_ready, 1)

            def copy_b(k, th):
                act.wait_ge(b_ready, 2 * k + th + 1)
                if th == 0:
                    wait(act, inject_ready, 16 * k)
                f(b_rep[:, HT * th:HT * th + HT, :], p_c[:, :].rearrange("p (t x) -> p t x", t=HT),
                  ACT.Copy).then_inc(b_copied, 1)

            def copy_c(k, th):
                act.wait_ge(c_ready, 2 * k + th + 1)
                if th == 0:
                    wait(act, c_step, 2 * SC * k)
                f(c_rep[:, HT * th:HT * th + HT, :], p_c[:, :].rearrange("p (t x) -> p t x", t=HT),
                  ACT.Copy).then_inc(c_copied, 1)

            def gelu_z(k):
                act.wait_ge(z_ready, k + 1)
                wait(act, gated, k)
                f(gz[:, :], p_c[:, :], ACT.Gelu).then_inc(gz_ready, 1)
                act.preload_act_table_set("natural_log_exp_and_others")

            def copy_yo(k):
                act.wait_ge(yo_ready, k + 1)
                wait(act, y_stored, DMA * k)
                wait(act, stat_done, 2 * k)
                f(yo[:, :, :], p_c[:, 0:2 * PB].rearrange("p (h x) -> p h x", h=2), ACT.Copy).then_inc(yo_copied, 1)

            def put_max(a, bank=p_s, buf=0):
                act.wait_ge(nmax_t, a + 1)
                f(qa[buf][96:99, :], bank[0:3, 0:PB // 2].bitcast(BF16), ACT.Copy).then_inc(nmax_in, 1)

            def probs(a, g):
                act.wait_ge(cols_ready, KG * a + g + 1)
                wait(act, pv_done, KG * a + max(g - 1, 0))
                f(prob[g % 2][:, :], p_s[:, :], ACT.Exp).then_inc(prob_ready, 1)

            def norm_o(a):
                act.wait_ge(den_step, 2 * a + 2)
                wait(act, o_turned, a)
                f(o_n[:, :], p_o[:, 0:CH], ACT.Copy, scale=rden[:, 1:2]).then_inc(o_norm, 1)

            def iteration(k, head, att, rows):
                has = att is not None
                if has:
                    probs(att, 0)
                abs_and_relu(k + 1)
                exp_abs(k + 1)
                if has:
                    probs(att, 1)
                log_part(k + 1)
                for j in range(8):
                    decays(k, 1, j)
                    if has and 1 <= j < KG - 1:
                        probs(att, j + 1)
                    if j == 1:
                        square(k + 1)
                        twice_inject(k, 0)
                    if j == 5:
                        top_part(k + 1)
                    if j == 6:
                        mid_part(k + 1)
                copy_c(k, 0)
                copy_c(k, 1)
                if has:
                    norm_o(att)
                if not head:
                    copy_yo(k - 1)
                copy_b(k + 1, 0)
                copy_b(k + 1, 1)
                twice_inject(k, 1)
                gelu_z(k)
                for j in range(8):
                    decays(k + 1, 0, j)
                if rows:
                    put_max(att + 1)

            def prep(b):
                act.wait_ge(gn_step, 12 * b + 8)
                f(gsd[:, :], gvar[:, :], ACT.Sqrt).then_inc(gn_act, 1)
                act.preload_act_table_set("natural_log_exp_and_others")
                act.wait_ge(gn_step, 12 * b + 12)

                def add_bias(c, par):
                    n_c = b * CHUNKS + c
                    wait(act, x1_stored[par], DMA // 2 * (n_c - par))
                    wait(act, v_ready, 2 * (n_c - 1))
                    for h in range(2):
                        act.wait_ge(xm_ready, 2 * n_c + h + 1)
                        f(x1c[par][:, h, :], xm[par][:, h, :], ACT.Identity, bias=gbias[:, h:h + 1]).then_inc(x1_ready, 1)

                add_bias(0, 0)
                for pair, more in chunk_pairs(act, b):
                    c0 = pair * 2
                    for par in range(2):
                        n_c = b * CHUNKS + c0 + par
                        act.wait_ge(kq_ready, 2 * n_c + 1)
                        wait(act, kq_res, 2 * n_c)
                        f(kf, p_delta[0][0:96, :], ACT.Identity, bias=bk_col[:, :]).then_inc(kq_copied, 1)
                        act.wait_ge(kq_ready, 2 * n_c + 2)
                        f(qf, p_delta[1][0:96, :], ACT.Identity, bias=bq_col[:, :]).then_inc(kq_copied, 1)
                        if more or par == 0:
                            add_bias(c0 + par + 1, 1 - par)
                        cols = bass.ds((c0 + par) * CHUNK, CHUNK)
                        act.wait_ge(kq_copied, 2 * n_c + 2)
                        wait(act, kq_parts, 6 * n_c)
                        wait(act, q_stored, 2 * DMA * n_c)
                        f(ka[0:96, cols], kf, ACT.Copy).then_inc(a_done, 1)
                        f(qac, qf, ACT.Copy).then_inc(a_done, 1)
                        act.wait_ge(kq_res, 2 * n_c + 1)
                        f(kb[:, cols], kres, ACT.Copy).then_inc(b_done, 1)
                        act.wait_ge(kq_res, 2 * n_c + 2)
                        f(qbc, qres, ACT.Copy).then_inc(b_done, 1)
                wait_alone(act, v_ready, 2 * CHUNKS * (b + 1))
                for par in range(2):
                    wait_alone(act, x1_stored[par], DMA * (CHUNKS // 2) * (b + 1))

            act.wait_ge(consts_in, CONSTS[0])
            act.preload_act_table_set("natural_log_exp_and_others")
            f(a_col[:, :], a_col[:, :], ACT.Exp).then_inc(setup_act, 1)
            act.wait_ge(setup_ready, 1)
            abs_and_relu(0)
            exp_abs(0)
            log_part(0)
            square(0)
            top_part(0)
            mid_part(0)
            copy_b(0, 0)
            copy_b(0, 1)
            for i in range(8):
                decays(0, 0, i)

            def phase(b, att):
                k0 = b * BLOCKS
                if att:
                    put_max(k0 - BLOCKS)
                for i in range(peeled(b)):
                    iteration(k0 + i, i == 0, k0 - BLOCKS + i if att else None, att)
                with act.Fori(peeled(b), BLOCKS - 1) as i:
                    iteration(k0 + i, False, k0 - BLOCKS + i if att else None, att)
                iteration(k0 + BLOCKS - 1, False, k0 - 1 if att else None, False)
                copy_yo(k0 + BLOCKS - 1)

            def alone(a, par, rows):
                for g in range(KG):
                    probs(a, g)
                if rows:
                    put_max(a + 1, p_y, 1 - par)
                norm_o(a)

            phase(0, False)
            prep(0)
            phase(1, True)
            with act.Fori(2, IMAGES) as b:
                prep(b - 1)
                phase(b, True)
            prep(IMAGES - 1)
            put_max(ALL - BLOCKS)
            with act.Fori(0, BLOCKS // 2 - 1) as pair:
                for par in range(2):
                    alone(pair * 2 + (ALL - BLOCKS + par), par, True)
            alone(ALL - 2, 0, True)
            alone(ALL - 1, 1, False)

        @block.vector
        def _(dve):
            tt = nc.vector.tensor_tensor
            SOFTPLUS_AFTER = (0, 1, 3, 4, 5, 6, 8, 13)
            MAX_AFTER = (0, 1, 2, 3, 5, 6, 8, 10)

            def softplus(k, n):
                if n == 0:
                    dve.wait_ge(e_ready, k + 1)
                    nc.vector.tensor_scalar(t_c[:, :], t_e[:, :], 1.0, -1.0, ALU.add, ALU.add).then_inc(sp_step, 1)
                if n == 1:
                    dve.wait_ge(sp_step, 5 * k + 1)
                    dve.wait_ge(ln_ready, k + 1)
                    tt(t_c[:, :], t_c[:, :], t_l[:, :], ALU.subtract).then_inc(sp_step, 1)
                if n == 2:
                    dve.wait_ge(sp_step, 5 * k + 2)
                    dve.wait_ge(square_ready, k + 1)
                    nc.vector.scalar_tensor_tensor(t_c[:, :], t_c[:, :], 0.0, t_l[:, :], ALU.max, ALU.min).then_inc(sp_step, 1)
                if n == 3:
                    dve.wait_ge(sp_step, 5 * k + 3)
                    tt(t_l[:, :], t_e[:, :], t_c[:, :], ALU.subtract).then_inc(sp_step, 1)
                if n == 4:
                    dve.wait_ge(sp_step, 5 * k + 4)
                    tt(t_d[:, 0, :], t_l[:, :], t_r[:, :], ALU.add).then_inc(sp_step, 1)
                if n == 5:
                    dve.wait_ge(sp_step, 5 * k + 5)
                    dve.wait_ge(u_ready, k + 1)
                    tt(t_d[:, 1, :], t_d[:, 0, :], p_c[:, :], ALU.mult).then_inc(du_ready, 1)
                if n == 6:
                    dve.wait_ge(top_ready, k + 1)
                    tt(t_rest[:, :, :], t_d[:, :, :], top[:, :, :], ALU.subtract).then_inc(res_ready, 1)
                if n == 7:
                    dve.wait_ge(mid_ready, k + 1)
                    tt(low[:, :, :], t_rest[:, :, :], mid[:, :, :], ALU.subtract).then_inc(low_ready, 1)

            def inject_item(k, h, i):
                n = 16 * k + 8 * h + i
                th, j = 1 - i // TILES, i % TILES
                if i == 0:
                    wait(dve, fwd_step, FWD * (2 * k + h))
                    wait(dve, bwd_step, BWD * (2 * k + h - 1) + 2 * (HT - 1))
                    dve.wait_ge(b_copied, 2 * k + 2)
                if i == TILES:
                    wait(dve, bwd_step, BWD * (2 * k + h - 1) + BWD - len(POOL_SUMS))
                dve.wait_ge(du_spread, n + 1)
                ts = slice(HT * th, HT * th + HT)
                tt(inject[:, ts, j, :], p_du[i % 2][:, :].rearrange("p (t x) -> p t x", t=HT),
                   b_rep[:, ts, :], ALU.mult).then_inc(inject_ready, 1)

            def forward(k, h, n):
                unit = 2 * k + h
                t = n // 2 + 1
                if n == FWD - 1:
                    dve.wait_ge(fwd_step, FWD * unit + FWD - 1)
                    nc.vector.scalar_tensor_tensor(fwd[h][:, t, :, :], inject[:, t, :, :], 2.0, fwd[h][:, t, :, :],
                                                   ALU.mult, ALU.add).then_inc(fwd_step, 1)
                elif n % 2:
                    dve.wait_ge(fwd_step, FWD * unit + n)
                    tt(fwd[h][:, t, :, :], fwd[h][:, t, :, :], inject[:, t, :, :], ALU.add).then_inc(fwd_step, 1)
                elif n:
                    dve.wait_ge(fwd_step, FWD * unit + n)
                    tt(fwd[h][:, t, :, :], decay[h][:, t, :, :], fwd[h][:, t - 1, :, :], ALU.mult).then_inc(fwd_step, 1)
                else:
                    dve.wait_ge(decay_ready, 8 * unit + 8)
                    dve.wait_ge(inject_ready, 8 * unit + 8)
                    wait(dve, y_summed, 2 * (unit - 1))
                    tt(fwd[h][:, 1, :, :], decay[h][:, 1, :, :], inject[:, 0, :, :], ALU.mult).then_inc(fwd_step, 1)

            def sum_and_c(k, h, n):
                unit = 2 * k + h
                what, t = C_STEPS[n]
                if what == "sum":
                    dve.wait_ge(bwd_step, BWD * unit + 2 * (TOK - 1 - t))
                    dve.wait_ge(fwd_step, FWD * unit + FWD)
                    tt(fwd[h][:, t, :, :], fwd[h][:, t, :, :], bwd[:, t, :, :], ALU.add).then_inc(c_step, 1)
                    return
                if ("sum", t) in C_STEPS:
                    dve.wait_ge(c_step, SC * unit + C_STEPS.index(("sum", t)) + 1)
                elif t == 0:
                    dve.wait_ge(bwd_step, BWD * unit + BWD - len(POOL_SUMS))
                elif t < TOK - 1:
                    dve.wait_ge(bwd_step, BWD * unit + BWD - POOL_SUMS.index(t))
                if t >= TOK - 2:
                    dve.wait_ge(c_copied, 2 * k + 2)
                tt(fwd[h][:, t, :, :], fwd[h][:, t, :, :],
                   c_rep[:, t, :].unsqueeze(1).to_broadcast([P, TILES, PB]), ALU.mult).then_inc(c_step, 1)

            def gate(k):
                dve.wait_ge(y_summed, 4 * k + 4)
                dve.wait_ge(gz_ready, k + 1)
                wait(dve, yo_ready, k)
                tt(yz[:, :], p_y[:, :], gz[:, :], ALU.mult).then_inc(gated, 1)

            def channel_stats(k, i):
                dve.wait_ge(yo_copied, k + 1)
                for h in range(2):
                    nc.vector.bn_stats(stats[:, h, i, :], yo[:, h, :]).then_inc(stat_done, 1)

            def max_item(a, g, banks=(p_o, p_s)):
                dve.wait_ge(rows_ready, KG * a + g + 1)
                nc.vector.tensor_reduce(mx8[:, g:g + 1], banks[g % 2][:, :], AX.X, ALU.max).then_inc(max_step, 1)

            def put_together(a):
                dve.wait_ge(max_step, KG * a + KG)
                nc.vector.tensor_reduce(nmax[:, :], mx8[:, :], AX.X, ALU.max, negate=True).then_inc(nmax_step, 1)
                dve.wait_ge(nmax_step, 5 * a + 1)
                nc.vector.tensor_copy(nparts[:, 0:1], nmax[:, :]).then_inc(nmax_step, 1)
                dve.wait_ge(nmax_step, 5 * a + 2)
                tt(nres[:, :], nmax[:, :], nparts[:, 0:1], ALU.subtract).then_inc(nmax_step, 1)
                dve.wait_ge(nmax_step, 5 * a + 3)
                nc.vector.tensor_copy(nparts[:, 1:2], nres[:, :]).then_inc(nmax_step, 1)
                dve.wait_ge(nmax_step, 5 * a + 4)
                tt(nparts[:, 2:3], nres[:, :], nparts[:, 1:2], ALU.subtract).then_inc(nmax_step, 1)

            def denominators(a):
                dve.wait_ge(pv_done, KG * a + KG)
                nc.vector.reciprocal(rden[:, 0:1], p_o[:, CH:CH + 1]).then_inc(den_step, 1)
                dve.wait_ge(den_step, 2 * a + 1)
                tt(rden[:, 1:2], rden[:, 0:1], gamma_col[:, :], ALU.mult).then_inc(den_step, 1)

            def add_residual(a, bank=p_s):
                dve.wait_ge(o_turned, a + 1)
                wait(dve, x1_in, DMA * (a + 1))
                wait(dve, out_stored, DMA * a)
                tt(o_c[:, :, :], bank[:, 0:2 * PB].rearrange("p (h x) -> p h x", h=2), x1b[:, :, :],
                   ALU.add).then_inc(o_added, 1)

            def iteration(k, i, head, att, rows):
                has = att is not None
                if not head:
                    sum_and_c(k - 1, 1, 0)
                for n in range(8):
                    inject_item(k, 0, n)
                for n in range(FWD):
                    forward(k, 0, n)
                    if not head and n + 1 < SC:
                        sum_and_c(k - 1, 1, n + 1)
                    if n in SOFTPLUS_AFTER:
                        softplus(k + 1, SOFTPLUS_AFTER.index(n))
                sum_and_c(k, 0, 0)
                for n in range(8):
                    inject_item(k, 1, n)
                    if n == 0 and has:
                        denominators(att)
                    if n == 1 and not head:
                        gate(k - 1)
                if has:
                    add_residual(att)
                for n in range(FWD):
                    forward(k, 1, n)
                    if n + 1 < SC:
                        sum_and_c(k, 0, n + 1)
                    if rows and n in MAX_AFTER:
                        max_item(att + 1, MAX_AFTER.index(n))
                    if n == 12 and not head:
                        channel_stats(k - 1, i - 1)
                if rows:
                    put_together(att + 1)

            def tail(k):
                for n in range(SC):
                    sum_and_c(k, 1, n)
                gate(k)
                channel_stats(k, BLOCKS - 1)

            def prep(b):
                g0 = 12 * b
                step = [0]

                def chain(ins):
                    ins.then_inc(gn_step, 1)
                    step[0] += 1
                    wait_alone(dve, gn_step, g0 + step[0])

                wait_alone(dve, stat_done, 2 * BLOCKS * (b + 1))
                for h in range(2):
                    chain(nc.vector.bn_aggr(mv[:, h, :], stats[:, h, :, :].rearrange("p n s -> p (n s)")))
                chain(tt(gst[:, :, 1], mv[:, :, 0], mv[:, :, 0], ALU.mult))
                nc.vector.tensor_copy(gst[:, :, 0], mv[:, :, 0])
                chain(tt(gst[:, :, 1], gst[:, :, 1], mv[:, :, 1], ALU.add))
                dve.wait_ge(gn_pe, b + 1)
                chain(nc.vector.tensor_copy(gsum[:, :, :], p_c[:, 0:4].rearrange("p (h s) -> p h s", h=2)))
                chain(tt(gvar[:, :], gsum[:, :, 0], gsum[:, :, 0], ALU.mult))
                chain(tt(gvar[:, :], gsum[:, :, 1], gvar[:, :], ALU.subtract))
                chain(nc.vector.tensor_scalar(gvar[:, :], gvar[:, :], GN_EPS, None, ALU.add))
                dve.wait_ge(gn_act, b + 1)
                chain(nc.vector.reciprocal(gsd[:, :], gsd[:, :]))
                chain(tt(gscale[:, :], gsd[:, :], gnw[:, :], ALU.mult))
                chain(tt(gbias[:, :], gsum[:, :, 0], gscale[:, :], ALU.mult))
                chain(tt(gbias[:, :], gnb[:, :], gbias[:, :], ALU.subtract))

                def scale_and_add(c, par):
                    n_c = b * CHUNKS + c
                    dve.wait_ge(chunk_in[par], DMA * (n_c - par) + 2 * DMA)
                    wait(dve, x1_ready, 2 * (n_c - 1))
                    for h in range(2):
                        nc.vector.scalar_tensor_tensor(xm[par][:, h, :], yc[par][:, h, :], gscale[:, h:h + 1],
                                                       xc[par][:, h, :], ALU.mult, ALU.add).then_inc(xm_ready, 1)

                scale_and_add(0, 0)
                for pair, more in chunk_pairs(dve, b):
                    c0 = pair * 2
                    for par in range(2):
                        n_c = b * CHUNKS + c0 + par
                        cols = bass.ds((c0 + par) * CHUNK, CHUNK)
                        if more or par == 0:
                            scale_and_add(c0 + par + 1, 1 - par)
                        dve.wait_ge(a_done, 2 * n_c + 1)
                        wait(dve, b_done, 2 * n_c)
                        tt(kres, kf, ka[0:96, cols], ALU.subtract).then_inc(kq_res, 1)
                        dve.wait_ge(a_done, 2 * n_c + 2)
                        tt(qres, qf, qac, ALU.subtract).then_inc(kq_res, 1)
                        dve.wait_ge(b_done, 2 * n_c + 1)
                        dve.wait_ge(kq_res, 2 * n_c + 2)
                        nc.vector.tensor_copy(kb[32:64, cols], ka[32:64, cols]).then_inc(kq_parts, 1)
                        nc.vector.tensor_copy(ka[64:96, cols], kb[64:96, cols]).then_inc(kq_parts, 1)
                        dve.wait_ge(kq_parts, 6 * n_c + 2)
                        tt(kb[64:96, cols], kres[64:96, :], kb[64:96, cols], ALU.subtract).then_inc(kq_parts, 1)
                        dve.wait_ge(b_done, 2 * n_c + 2)
                        nc.vector.tensor_copy(qbc[64:96, :], qac[64:96, :]).then_inc(kq_parts, 1)
                        nc.vector.tensor_copy(qac[32:64, :], qbc[32:64, :]).then_inc(kq_parts, 1)
                        dve.wait_ge(kq_parts, 6 * n_c + 5)
                        tt(qbc[32:64, :], qres[32:64, :], qbc[32:64, :], ALU.subtract).then_inc(kq_parts, 1)
                        for m in range(2):
                            dve.wait_ge(v_ready, 2 * n_c + m + 1)
                            tt(v_t[:, bass.ds((c0 + par) * 4 + 2 * m, 2), 0:CH],
                               p_du[m][:, :].rearrange("p (m c) -> p m c", m=2),
                               bv_rep[:, :].unsqueeze(1).to_broadcast([P, 2, CH]), ALU.add).then_inc(v_copied, 1)
                wait_alone(dve, b_done, 2 * CHUNKS * (b + 1))
                wait_alone(dve, q_stored, 2 * DMA * CHUNKS * (b + 1))

            cp = nc.vector.tensor_copy
            dve.wait_ge(consts_in, CONSTS[0])
            dve.wait_ge(setup_pe, 1)
            cp(s_mid[0:DIN, 128:128 + GCN], p_c[0:DIN, 0:GCN]).then_inc(setup_dve, 1)
            dve.wait_ge(setup_pe, 2)
            cp(s_mid[0:2, 64:128], p_y[0:2, 0:DIN]).then_inc(setup_dve, 1)
            for n in range(2):
                cp(s_mid[0:DIN, 384 + n * P:384 + (n + 1) * P].rearrange("p (d n) -> p d n", d=8),
                   s_small[0:DIN, 2 + n * NST:2 + (n + 1) * NST].unsqueeze(1).to_broadcast([DIN, 8, NST]))
            dve.wait_ge(setup_pe, 5)
            cp(s_mid[0:DIN, 256:256 + DIN], p_delta[0][0:DIN, 0:DIN]).then_inc(setup_dve, 1)
            cp(s_mid[0:DIN, 256 + DIN:256 + P], p_delta[0][0:DIN, 0:DIN]).then_inc(setup_dve, 1)
            dve.wait_ge(setup_pe, 6)
            cp(w_dbc[:, :, :], p_delta[1][0:GCN, 0:3 * P].rearrange("p (n c) -> p n c", n=3)).then_inc(setup_dve, 1)
            nc.vector.tensor_scalar(s_small[0:GCN, 128:192], s_small[0:GCN, 128:192], 2.0, None, ALU.mult).then_inc(setup_dve, 1)
            dve.wait_ge(setup_dve, 6)
            tt(w_skip[:, :], w_in[:, 0:DIN], s_small[0:GCN, 128:192], ALU.mult).then_inc(setup_dve, 1)
            nc.vector.tensor_scalar(b2_col[:, :], b2_col[:, :], 2.0, None, ALU.mult).then_inc(setup_dve, 1)
            dve.wait_ge(setup_act, 1)
            nc.vector.tensor_scalar(a_col[:, :], a_col[:, :], -1.0, None, ALU.mult).then_inc(setup_dve, 1)
            for bank, w in ((p_s, wq_t), (p_o, wk_t)):
                for r in range(3):
                    cp(w[:, :, 32 * r:32 * r + 32], bank[:, 0:64].rearrange("p (h d) -> p h d", h=2)).then_inc(setup_dve, 1)
            for h in range(2):
                cp(wv_t[:, h, :], p_du[h][:, 0:CH]).then_inc(setup_dve, 1)
            cp(identb[:, :], ident[:, :]).then_inc(setup_dve, 1)
            cp(spread[:, :, :], s_qk[0:96, 2 * CH:4 * CH].rearrange("p (j x) -> p j x", j=TILES)).then_inc(setup_dve, 1)
            for h in range(2):
                d = slice(DIN * h, DIN * h + DIN)
                other = slice(DIN * (1 - h), DIN * (1 - h) + DIN)
                cp(w_out[d, h, :], w_out_raw[d, :]).then_inc(setup_dve, 1)
                nc.vector.memset(w_out[other, h, :], 0.0).then_inc(setup_dve, 1)
            nc.vector.memset(ka[96:99, :], 1.0).then_inc(setup_dve, 1)
            nc.vector.memset(v_t[:, :, CH:CH + 1], 1.0).then_inc(setup_dve, 1)
            dve.wait_ge(setup_dve, 25)
            nc.vector.memset(nres[:, :], 0.0).then_inc(setup_ready, 1)
            for n in range(8):
                softplus(0, n)

            def find_max(a, banks=(p_o, p_s)):
                for g in range(KG):
                    max_item(a, g, banks)
                put_together(a)

            def phase(b, att):
                k0 = b * BLOCKS
                if att:
                    find_max(k0 - BLOCKS)
                for i in range(peeled(b)):
                    iteration(k0 + i, i, i == 0, k0 - BLOCKS + i if att else None, att)
                with dve.Fori(peeled(b), BLOCKS - 1) as i:
                    iteration(k0 + i, i, False, k0 - BLOCKS + i if att else None, att)
                iteration(k0 + BLOCKS - 1, BLOCKS - 1, False, k0 - 1 if att else None, False)
                tail(k0 + BLOCKS - 1)

            def alone(a, rows):
                if rows:
                    find_max(a + 1, p_delta)
                denominators(a)
                add_residual(a, p_du[0])

            phase(0, False)
            prep(0)
            phase(1, True)
            with dve.Fori(2, IMAGES) as b:
                prep(b - 1)
                phase(b, True)
            prep(IMAGES - 1)
            find_max(ALL - BLOCKS)
            with dve.Fori(0, BLOCKS // 2 - 1) as pair:
                for par in range(2):
                    alone(pair * 2 + (ALL - BLOCKS + par), True)
            alone(ALL - 2, True)
            alone(ALL - 1, False)

        @block.gpsimd
        def _(pool):
            tt = nc.gpsimd.tensor_tensor

            def backward(k, h):
                unit = 2 * k + h
                for t in reversed(range(TOK - 1)):
                    n = BWD * unit + 2 * (TOK - 2 - t)
                    if t == TOK - 2:
                        pool.wait_ge(decay_ready, 8 * unit + 4)
                        pool.wait_ge(inject_ready, 8 * unit + 4)
                    if t == HT - 1:
                        pool.wait_ge(decay_ready, 8 * unit + 8)
                        pool.wait_ge(inject_ready, 8 * unit + 8)
                    later = inject[:, TOK - 1, :, :] if t == TOK - 2 else bwd[:, t + 1, :, :]
                    if 0 < t and t not in POOL_SUMS:
                        wait(pool, c_step, SC * (unit - 1) + C_STEPS.index(("sum", t)) + 1)
                    wait(pool, bwd_step, n)
                    tt(bwd[:, t, :, :], decay[h][:, t, :, :], later, ALU.mult).then_inc(bwd_step, 1)
                    pool.wait_ge(bwd_step, n + 1)
                    if t:
                        tt(bwd[:, t, :, :], bwd[:, t, :, :], inject[:, t, :, :], ALU.add).then_inc(bwd_step, 1)
                    else:
                        wait(pool, y_summed, 2 * (unit - 1))
                        pool.wait_ge(twice_ready, unit + 1)
                        tt(fwd[h][:, 0, :, :], bwd[:, 0, :, :], twice[:, :, :], ALU.add).then_inc(bwd_step, 1)
                pool.wait_ge(fwd_step, FWD * unit + FWD)
                for t in sorted(POOL_SUMS, reverse=True):
                    tt(fwd[h][:, t, :, :], fwd[h][:, t, :, :], bwd[:, t, :, :], ALU.add).then_inc(bwd_step, 1)

            pool.wait_ge(setup_ready, 1)
            for h in range(2):
                backward(0, h)
            with pool.Fori(1, ALL) as k:
                for h in range(2):
                    backward(k, h)


def constants():
    spread = np.zeros((96, TILES, P), np.float32)
    for part in range(3):
        for j in range(TILES):
            for d in range(8):
                spread[32 * part + 8 * j + d, j, NST * d:NST * d + NST] = 1
    total = np.zeros((P, 2 * TILES, DIN), np.float32)
    for j in range(2 * TILES):
        for d in range(8):
            total[NST * d:NST * d + NST, j, 8 * j + d] = 1
    group = np.zeros((P, P), np.float32)
    for g in range(2):
        group[64 * g:64 * g + 64, 64 * g:64 * g + 64] = 1 / 64
    return {"ident": np.eye(P, dtype=np.float32), "spread": spread, "sum": total, "group": group}


_INS = ["x", "L0_conv_W_in", "L0_conv_W_x", "L0_conv_W_dt", "L0_conv_b_dt", "L0_conv_A_logs", "L0_conv_Ds",
        "L0_conv_W_out", "L0_conv_gn_w", "L0_conv_gn_b", "L1_conv_Wq", "L1_conv_bq", "L1_conv_Wk", "L1_conv_bk",
        "L1_conv_Wv", "L1_conv_bv", "L1_conv_gamma"]


def kernel(**inputs):
    import concourse.bacc as bacc
    from concourse.bass_utils import run_bass_kernel_spmd

    nc = bacc.Bacc("TRN2", target_bir_lowering=False, num_devices=1, dynamic_dma_scratch_size=1024)
    arrays, args = {}, []
    data = [(name, np.ascontiguousarray(np.atleast_1d(inputs[name]))) for name in _INS]
    for name, a in data + list(constants().items()):
        arrays[f"in_{name}"] = a
        args.append(nc.dram_tensor(f"in_{name}", a.shape, mybir.dt.from_np(a.dtype), kind="ExternalInput").ap())
    out = nc.dram_tensor("out", (IMAGES, CH, 64, 64), F32, kind="ExternalOutput").ap()
    build(nc, *args, out)
    r = run_bass_kernel_spmd(nc, [arrays], core_ids=[0])
    return r.results[0]["out"]
```
